# Optimizing a Trainium2 kernel written in Bass

```python
import numpy as np
import jax
import jax.numpy as jnp

def _softmax(x, axis=-1):
    return jax.nn.softmax(x, axis=axis)

def _gelu(x):
    return jax.nn.gelu(x, approximate=True)

def _silu(x):
    return jax.nn.silu(x)

def _sigmoid(x):
    return jax.nn.sigmoid(x)

def _layernorm(x, axis=-1, eps=1e-05):
    m = jnp.mean(x, axis=axis, keepdims=True)
    v = jnp.var(x, axis=axis, keepdims=True)
    return (x - m) / jnp.sqrt(v + eps)

def _scatter_add(tgt, idx, src, axis=0):
    return tgt.at[idx].add(src)

def _segment_sum(src, seg, n):
    return jax.ops.segment_sum(src, seg, n)
kernel_name = 'mk_seq_preln_d2_jaxref_r8_2b5cf1'

def setup_inputs(seed: int=0):
    np.random.seed(seed)
    _w = jnp.asarray

    def _L0_attn_setup():
        import jax, jax.numpy as jnp
        import numpy as np
        import math
        B, S, D = (2, 512, 128)
        H, HD = (16, 64)
        WIN = 128
        G = 32
        SCALE = 1.0 / math.sqrt(HD)

        def _forward(x, wq, wk, wv, wo, ws1, bs1, ws2, bs2):
            b, s, d = x.shape
            neg = jnp.finfo(x.dtype).min
            h = jax.nn.gelu(x @ ws1 + bs1, approximate=False)
            scores = (h @ ws2 + bs2).squeeze(-1)
            causal_bs = jnp.triu(jnp.ones((b, s), bool), 1)
            scores = jnp.where(causal_bs, neg, scores)
            _, idx = jax.lax.top_k(scores, min(G, s))
            g_tok = jnp.take_along_axis(x, idx[:, :, None], axis=1)
            q = (x @ wq).reshape(b, s, H, HD).transpose(0, 2, 1, 3)
            k = (x @ wk).reshape(b, s, H, HD).transpose(0, 2, 1, 3)
            v = (x @ wv).reshape(b, s, H, HD).transpose(0, 2, 1, 3)
            gk = (g_tok @ wk).reshape(b, -1, H, HD).transpose(0, 2, 1, 3)
            gv = (g_tok @ wv).reshape(b, -1, H, HD).transpose(0, 2, 1, 3)
            nw = s // WIN
            qw = q.reshape(b, H, nw, WIN, HD)
            kw = k.reshape(b, H, nw, WIN, HD)
            vw = v.reshape(b, H, nw, WIN, HD)
            att = jnp.einsum('bhwqd,bhwkd->bhwqk', qw, kw) * SCALE
            cm = jnp.triu(jnp.ones((WIN, WIN), bool), 1)
            att = jnp.where(cm, neg, att)
            p = jax.nn.softmax(att, axis=-1)
            local_out = jnp.einsum('bhwqk,bhwkd->bhwqd', p, vw).reshape(b, H, s, HD)
            gatt = jnp.einsum('bhsd,bhgd->bhsg', q, gk) * SCALE
            gp = jax.nn.softmax(gatt, axis=-1)
            global_out = jnp.einsum('bhsg,bhgd->bhsd', gp, gv)
            out = (local_out + global_out).transpose(0, 2, 1, 3).reshape(b, s, H * HD)
            return out @ wo
        key = jax.random.key(seed)
        ks = jax.random.split(key, 9)
        w = 0.02
        return {'x': jax.random.normal(ks[0], (B, S, D), jnp.float32), 'wq': jax.random.normal(ks[1], (D, H * HD), jnp.float32) * w, 'wk': jax.random.normal(ks[2], (D, H * HD), jnp.float32) * w, 'wv': jax.random.normal(ks[3], (D, H * HD), jnp.float32) * w, 'wo': jax.random.normal(ks[4], (H * HD, D), jnp.float32) * w, 'ws1': jax.random.normal(ks[5], (D, D // 4), jnp.float32) * w, 'bs1': jnp.zeros((D // 4,), jnp.float32), 'ws2': jax.random.normal(ks[6], (D // 4, 1), jnp.float32) * w, 'bs2': jnp.zeros((1,), jnp.float32)}
    _L0_attn_in = _L0_attn_setup()

    def _L0_ffn_setup():
        import math
        import jax, jax.numpy as jnp
        import numpy as np
        B, S, H, BOT, RD, N, K = (4, 256, 128, 128, 48, 512, 8)
        key = jax.random.key(seed)
        ks = jax.random.split(key, 12)
        hidden_states = jax.random.normal(ks[0], (B, S, H), jnp.float32)
        q_proj_w = jax.random.normal(ks[1], (BOT, H), jnp.float32) * (1.0 / math.sqrt(H))
        router_w = jax.random.normal(ks[2], (RD, BOT), jnp.float32) * (1.0 / math.sqrt(BOT))
        aux_keys = jax.random.normal(ks[3], (N, BOT), jnp.float32) * 0.01
        aux_values = jax.random.normal(ks[4], (N, H), jnp.float32) * 0.02
        reliability_mask = jax.random.uniform(ks[5], (N,), jnp.float32)
        unc_w1 = jax.random.normal(ks[6], (H // 4, H), jnp.float32) * (1.0 / math.sqrt(H))
        unc_b1 = jnp.zeros((H // 4,), jnp.float32)
        unc_w2 = jax.random.normal(ks[7], (1, H // 4), jnp.float32) * 0.02
        unc_b2 = jnp.zeros((1,), jnp.float32)
        gate_w1 = jnp.asarray(0.5, jnp.float32)
        gate_bias = jnp.asarray(-1.0, jnp.float32)
        return {'hidden_states': hidden_states, 'q_proj_w': q_proj_w, 'router_w': router_w, 'aux_keys': aux_keys, 'aux_values': aux_values, 'reliability_mask': reliability_mask, 'unc_w1': unc_w1, 'unc_b1': unc_b1, 'unc_w2': unc_w2, 'unc_b2': unc_b2, 'gate_w1': gate_w1, 'gate_bias': gate_bias}
    _L0_ffn_in = _L0_ffn_setup()

    def _L1_attn_setup():
        import jax, jax.numpy as jnp
        import numpy as np
        HIDDEN = 128
        N_HEADS = 16
        D_HEAD = HIDDEN // N_HEADS

        def _rope(q, k):
            B, H, N, d = q.shape
            inv_freq = 1.0 / 10000.0 ** (jnp.arange(0, d, 2, dtype=jnp.float32) / d)
            pos = jnp.arange(N, dtype=jnp.float32)
            thetas = pos[:, None] * inv_freq[None, :]
            cos, sin = (jnp.cos(thetas), jnp.sin(thetas))

            def rot(x):
                xp = x.reshape(B, H, N, d // 2, 2)
                xx, xy = (xp[..., 0], xp[..., 1])
                rx = xx * cos - xy * sin
                ry = xx * sin + xy * cos
                return jnp.stack([rx, ry], axis=-1).reshape(B, H, N, d)
            return (rot(q), rot(k))
        key = jax.random.key(seed)
        ks = jax.random.split(key, 9)
        B, N, Hd = (4, 256, HIDDEN)
        s = 1.0 / np.sqrt(Hd)
        return {'x': jax.random.normal(ks[0], (B, N, Hd), jnp.float32), 'Wq': jax.random.normal(ks[1], (Hd, Hd), jnp.float32) * s, 'bq': jax.random.normal(ks[2], (Hd,), jnp.float32) * 0.02, 'Wk': jax.random.normal(ks[3], (Hd, Hd), jnp.float32) * s, 'bk': jax.random.normal(ks[4], (Hd,), jnp.float32) * 0.02, 'Wv': jax.random.normal(ks[5], (Hd, Hd), jnp.float32) * s, 'bv': jax.random.normal(ks[6], (Hd,), jnp.float32) * 0.02, 'Wo': jax.random.normal(ks[7], (Hd, Hd), jnp.float32) * s, 'bo': jax.random.normal(ks[8], (Hd,), jnp.float32) * 0.02}
    _L1_attn_in = _L1_attn_setup()

    def _L1_ffn_setup():
        import jax, jax.numpy as jnp
        import numpy as np
        from jax import lax
        B, N, D, H, E, K = (16, 128, 128, 512, 8, 2)
        key = jax.random.key(seed)
        ks = jax.random.split(key, 12)
        s = 0.02
        return {'x': jax.random.normal(ks[0], (B, N, D), jnp.float32), 'alpha': jnp.asarray(0.9, jnp.float32), 'w_gate': jax.random.normal(ks[1], (D, E), jnp.float32) * s, 'b_gate': jnp.zeros((E,), jnp.float32), 'W1m': jax.random.normal(ks[2], (D, H), jnp.float32) * s, 'b1m': jnp.zeros((H,), jnp.float32), 'W2m': jax.random.normal(ks[3], (H, D), jnp.float32) * s, 'b2m': jnp.zeros((D,), jnp.float32), 'W1e': jax.random.normal(ks[4], (E, D, H), jnp.float32) * s, 'b1e': jnp.zeros((E, H), jnp.float32), 'W2e': jax.random.normal(ks[5], (E, H, D), jnp.float32) * s, 'b2e': jnp.zeros((E, D), jnp.float32)}
    _L1_ffn_in = _L1_ffn_setup()
    _d = {'L0_attn_x': _L0_attn_in['x'], 'L0_attn_wq': _L0_attn_in['wq'], 'L0_attn_wk': _L0_attn_in['wk'], 'L0_attn_wv': _L0_attn_in['wv'], 'L0_attn_wo': _L0_attn_in['wo'], 'L0_attn_ws1': _L0_attn_in['ws1'], 'L0_attn_bs1': _L0_attn_in['bs1'], 'L0_attn_ws2': _L0_attn_in['ws2'], 'L0_attn_bs2': _L0_attn_in['bs2'], 'L0_ffn_q_proj_w': _L0_ffn_in['q_proj_w'], 'L0_ffn_router_w': _L0_ffn_in['router_w'], 'L0_ffn_aux_keys': _L0_ffn_in['aux_keys'], 'L0_ffn_aux_values': _L0_ffn_in['aux_values'], 'L0_ffn_reliability_mask': _L0_ffn_in['reliability_mask'], 'L0_ffn_unc_w1': _L0_ffn_in['unc_w1'], 'L0_ffn_unc_b1': _L0_ffn_in['unc_b1'], 'L0_ffn_unc_w2': _L0_ffn_in['unc_w2'], 'L0_ffn_unc_b2': _L0_ffn_in['unc_b2'], 'L0_ffn_gate_w1': _L0_ffn_in['gate_w1'], 'L0_ffn_gate_bias': _L0_ffn_in['gate_bias'], 'L1_attn_Wq': _L1_attn_in['Wq'], 'L1_attn_bq': _L1_attn_in['bq'], 'L1_attn_Wk': _L1_attn_in['Wk'], 'L1_attn_bk': _L1_attn_in['bk'], 'L1_attn_Wv': _L1_attn_in['Wv'], 'L1_attn_bv': _L1_attn_in['bv'], 'L1_attn_Wo': _L1_attn_in['Wo'], 'L1_attn_bo': _L1_attn_in['bo'], 'L1_ffn_alpha': _L1_ffn_in['alpha'], 'L1_ffn_w_gate': _L1_ffn_in['w_gate'], 'L1_ffn_b_gate': _L1_ffn_in['b_gate'], 'L1_ffn_W1m': _L1_ffn_in['W1m'], 'L1_ffn_b1m': _L1_ffn_in['b1m'], 'L1_ffn_W2m': _L1_ffn_in['W2m'], 'L1_ffn_b2m': _L1_ffn_in['b2m'], 'L1_ffn_W1e': _L1_ffn_in['W1e'], 'L1_ffn_b1e': _L1_ffn_in['b1e'], 'L1_ffn_W2e': _L1_ffn_in['W2e'], 'L1_ffn_b2e': _L1_ffn_in['b2e']}
    _x0 = _d['L0_attn_x']
    _d['L0_attn_x'] = jax.random.normal(jax.random.fold_in(jax.random.key(seed), 1), (1, 2048, 128), dtype=_x0.dtype)
    del _x0
    return _d

def reference(L0_attn_x, L0_attn_wq, L0_attn_wk, L0_attn_wv, L0_attn_wo, L0_attn_ws1, L0_attn_bs1, L0_attn_ws2, L0_attn_bs2, L0_ffn_q_proj_w, L0_ffn_router_w, L0_ffn_aux_keys, L0_ffn_aux_values, L0_ffn_reliability_mask, L0_ffn_unc_w1, L0_ffn_unc_b1, L0_ffn_unc_w2, L0_ffn_unc_b2, L0_ffn_gate_w1, L0_ffn_gate_bias, L1_attn_Wq, L1_attn_bq, L1_attn_Wk, L1_attn_bk, L1_attn_Wv, L1_attn_bv, L1_attn_Wo, L1_attn_bo, L1_ffn_alpha, L1_ffn_w_gate, L1_ffn_b_gate, L1_ffn_W1m, L1_ffn_b1m, L1_ffn_W2m, L1_ffn_b2m, L1_ffn_W1e, L1_ffn_b1e, L1_ffn_W2e, L1_ffn_b2e):

    def _L0_attn_ref(x, wq, wk, wv, wo, ws1, bs1, ws2, bs2):
        import jax, jax.numpy as jnp
        import numpy as np
        import math
        B, S, D = (2, 512, 128)
        H, HD = (16, 64)
        WIN = 128
        G = 32
        SCALE = 1.0 / math.sqrt(HD)

        def _forward(x, wq, wk, wv, wo, ws1, bs1, ws2, bs2):
            b, s, d = x.shape
            neg = jnp.finfo(x.dtype).min
            h = jax.nn.gelu(x @ ws1 + bs1, approximate=False)
            scores = (h @ ws2 + bs2).squeeze(-1)
            causal_bs = jnp.triu(jnp.ones((b, s), bool), 1)
            scores = jnp.where(causal_bs, neg, scores)
            _, idx = jax.lax.top_k(scores, min(G, s))
            g_tok = jnp.take_along_axis(x, idx[:, :, None], axis=1)
            q = (x @ wq).reshape(b, s, H, HD).transpose(0, 2, 1, 3)
            k = (x @ wk).reshape(b, s, H, HD).transpose(0, 2, 1, 3)
            v = (x @ wv).reshape(b, s, H, HD).transpose(0, 2, 1, 3)
            gk = (g_tok @ wk).reshape(b, -1, H, HD).transpose(0, 2, 1, 3)
            gv = (g_tok @ wv).reshape(b, -1, H, HD).transpose(0, 2, 1, 3)
            nw = s // WIN
            qw = q.reshape(b, H, nw, WIN, HD)
            kw = k.reshape(b, H, nw, WIN, HD)
            vw = v.reshape(b, H, nw, WIN, HD)
            att = jnp.einsum('bhwqd,bhwkd->bhwqk', qw, kw) * SCALE
            cm = jnp.triu(jnp.ones((WIN, WIN), bool), 1)
            att = jnp.where(cm, neg, att)
            p = jax.nn.softmax(att, axis=-1)
            local_out = jnp.einsum('bhwqk,bhwkd->bhwqd', p, vw).reshape(b, H, s, HD)
            gatt = jnp.einsum('bhsd,bhgd->bhsg', q, gk) * SCALE
            gp = jax.nn.softmax(gatt, axis=-1)
            global_out = jnp.einsum('bhsg,bhgd->bhsd', gp, gv)
            out = (local_out + global_out).transpose(0, 2, 1, 3).reshape(b, s, H * HD)
            return out @ wo
        return _forward(x, wq, wk, wv, wo, ws1, bs1, ws2, bs2)

    def _L0_ffn_ref(hidden_states, q_proj_w, router_w, aux_keys, aux_values, reliability_mask, unc_w1, unc_b1, unc_w2, unc_b2, gate_w1, gate_bias):
        import math
        import jax, jax.numpy as jnp
        import numpy as np
        B, S, H, BOT, RD, N, K = (4, 256, 128, 128, 48, 512, 8)
        query = jnp.einsum('bsh,dh->bsd', hidden_states, q_proj_w)
        rq = jnp.einsum('bsd,rd->bsr', query, router_w)
        rk = jnp.einsum('nd,rd->nr', aux_keys, router_w)
        scores = jnp.einsum('bsr,nr->bsn', rq, rk) / math.sqrt(RD)
        scores = scores + reliability_mask[None, None, :]
        top_scores, top_idx = jax.lax.top_k(scores, K)
        mean = hidden_states.mean(axis=-1, keepdims=True)
        variance = ((hidden_states - mean) ** 2).mean(axis=-1)
        log_var = jnp.log1p(variance)
        normalized_var = log_var / (log_var.mean() + 1e-06)
        h1 = jax.nn.gelu(jnp.einsum('bsh,fh->bsf', hidden_states, unc_w1) + unc_b1, approximate=False)
        learned = (jnp.einsum('bsf,of->bso', h1, unc_w2) + unc_b2)[..., 0]
        uncertainty = jnp.clip(normalized_var * 0.5 + jax.nn.sigmoid(learned) * 2.5, 0.0, 5.0)
        gate = jax.nn.sigmoid(gate_w1 * uncertainty + gate_bias)
        w = jax.nn.softmax(top_scores, axis=-1)
        v = aux_values[top_idx]
        agg = jnp.einsum('bsk,bskh->bsh', w, v)
        out = hidden_states + gate[..., None] * agg
        return out

    def _L1_attn_ref(x, Wq, bq, Wk, bk, Wv, bv, Wo, bo):
        import jax, jax.numpy as jnp
        import numpy as np
        HIDDEN = 128
        N_HEADS = 16
        D_HEAD = HIDDEN // N_HEADS

        def _rope(q, k):
            B, H, N, d = q.shape
            inv_freq = 1.0 / 10000.0 ** (jnp.arange(0, d, 2, dtype=jnp.float32) / d)
            pos = jnp.arange(N, dtype=jnp.float32)
            thetas = pos[:, None] * inv_freq[None, :]
            cos, sin = (jnp.cos(thetas), jnp.sin(thetas))

            def rot(x):
                xp = x.reshape(B, H, N, d // 2, 2)
                xx, xy = (xp[..., 0], xp[..., 1])
                rx = xx * cos - xy * sin
                ry = xx * sin + xy * cos
                return jnp.stack([rx, ry], axis=-1).reshape(B, H, N, d)
            return (rot(q), rot(k))
        B, N, _ = x.shape
        H, d = (N_HEADS, D_HEAD)
        q = (x @ Wq.T + bq).reshape(B, N, H, d).transpose(0, 2, 1, 3)
        k = (x @ Wk.T + bk).reshape(B, N, H, d).transpose(0, 2, 1, 3)
        v = (x @ Wv.T + bv).reshape(B, N, H, d).transpose(0, 2, 1, 3)
        q, k = _rope(q, k)
        scores = jnp.einsum('bhnd,bhmd->bhnm', q, k) / jnp.sqrt(jnp.asarray(d, x.dtype))
        attn = jax.nn.softmax(scores, axis=-1)
        out = jnp.einsum('bhnm,bhmd->bhnd', attn, v)
        out = out.transpose(0, 2, 1, 3).reshape(B, N, H * d)
        return out @ Wo.T + bo

    def _L1_ffn_ref(x, alpha, w_gate, b_gate, W1m, b1m, W2m, b2m, W1e, b1e, W2e, b2e):
        import jax, jax.numpy as jnp
        import numpy as np
        from jax import lax
        B, N, D, H, E, K = (16, 128, 128, 512, 8, 2)
        main = jax.nn.gelu(x @ W1m + b1m) @ W2m + b2m
        logits = jnp.mean(x, axis=1) @ w_gate + b_gate
        probs = jax.nn.softmax(logits, axis=-1)
        top_vals, top_idx = lax.top_k(probs, K)
        gate_w = top_vals / jnp.sum(top_vals, axis=-1, keepdims=True)
        W1g = W1e[top_idx]
        b1g = b1e[top_idx]
        W2g = W2e[top_idx]
        b2g = b2e[top_idx]
        h = jax.nn.gelu(jnp.einsum('bnd,bkdh->bknh', x, W1g) + b1g[:, :, None, :])
        eo = jnp.einsum('bknh,bkhd->bknd', h, W2g) + b2g[:, :, None, :]
        expert_out = jnp.einsum('bk,bknd->bnd', gate_w, eo)
        a = jnp.clip(alpha, 0.1, 1.0)
        return a * main + (1.0 - a) * expert_out
    x = L0_attn_x
    x = x + _L0_attn_ref(_layernorm(x, axis=-1), L0_attn_wq, L0_attn_wk, L0_attn_wv, L0_attn_wo, L0_attn_ws1, L0_attn_bs1, L0_attn_ws2, L0_attn_bs2)
    x = x + _L0_ffn_ref(_layernorm(x, axis=-1), L0_ffn_q_proj_w, L0_ffn_router_w, L0_ffn_aux_keys, L0_ffn_aux_values, L0_ffn_reliability_mask, L0_ffn_unc_w1, L0_ffn_unc_b1, L0_ffn_unc_w2, L0_ffn_unc_b2, L0_ffn_gate_w1, L0_ffn_gate_bias)
    x = x + _L1_attn_ref(_layernorm(x, axis=-1), L1_attn_Wq, L1_attn_bq, L1_attn_Wk, L1_attn_bk, L1_attn_Wv, L1_attn_bv, L1_attn_Wo, L1_attn_bo)
    x = x + _L1_ffn_ref(_layernorm(x, axis=-1), L1_ffn_alpha, L1_ffn_w_gate, L1_ffn_b_gate, L1_ffn_W1m, L1_ffn_b1m, L1_ffn_W2m, L1_ffn_b2m, L1_ffn_W1e, L1_ffn_b1e, L1_ffn_W2e, L1_ffn_b2e)
    return x

_drawn_inputs = setup_inputs


def setup_inputs(seed=0):
    import zlib

    import numpy as np

    out = dict(_drawn_inputs(seed))
    spreads = {'L0_attn_bs1': (0.0, 0.1),
     'L0_ffn_unc_b1': (0.0, 2.0),
     'L1_ffn_b_gate': (0.0, 0.8),
     'L1_ffn_b1m': (0.0, 0.725),
     'L1_ffn_b2m': (0.0, 0.1),
     'L1_ffn_b1e': (0.0, 0.8),
     'L1_ffn_b2e': (0.0, 2.0)}
    factors = {'L0_attn_wq': 8.0,
     'L0_attn_wk': 8.0,
     'L0_ffn_q_proj_w': 8.0,
     'L0_ffn_router_w': 8.0,
     'L0_ffn_aux_keys': 8.0,
     'L0_ffn_aux_values': 8.0,
     'L0_ffn_unc_w1': 57.79,
     'L0_ffn_unc_w2': 53.19,
     'L1_attn_bq': 64.0,
     'L1_attn_bk': 64.0,
     'L1_attn_bv': 5.219,
     'L1_attn_bo': 5.394,
     'L1_ffn_w_gate': 25.991,
     'L1_ffn_W1e': 8.0,
     'L1_ffn_W2e': 8.0}
    for name, (base, spread) in spreads.items():
        noise = np.random.default_rng([zlib.crc32(name.encode()), seed]).standard_normal(out[name].shape)
        drawn = base * np.exp(spread * noise) if base else spread * noise
        out[name] = jnp.asarray(drawn.astype(out[name].dtype))
    for name, factor in factors.items():
        out[name] = (out[name] * factor).astype(out[name].dtype)
    return out
```

```python
from contextlib import ExitStack

import numpy as np
import concourse.bass as bass
from concourse import mybir

F32 = mybir.dt.float32
BF16 = mybir.dt.bfloat16
U32 = mybir.dt.uint32
ACT = mybir.ActivationFunctionType
ALU = mybir.AluOpType
AX_X = mybir.AxisListType.X

P = 128
N = 2048
D = 128
NT = N // P
BANK = 512
NC = N // BANK
TPB = BANK // P
EPS = 1e-5

H0, HD0, G0 = 16, 64, 32
PAIRS = H0 // 2
WL = P + G0
F32_LOW = -3.4028234663852886e38
MASKED = -1e30

RD, NKEY, UH = 48, 512, 32

H1, HD1 = 16, 8
PARTS = 3
QROWS = PARTS * PARTS * HD1
MROW = QROWS
KROWS = QROWS + PARTS
VCOLS = 32

HID, NE = 512, 8
HT = HID // P
NETS = 3


class Memory:
    pass


def ln_block(nc, m, tag, loads=()):
    with ExitStack() as ctx:
        stats_ready = ctx.enter_context(nc.semaphore(f"{tag}_stats_ready"))
        moments_ready = ctx.enter_context(nc.semaphore(f"{tag}_moments_ready"))
        var_eps_ready = ctx.enter_context(nc.semaphore(f"{tag}_var_eps_ready"))
        std_ready = ctx.enter_context(nc.semaphore(f"{tag}_std_ready"))
        rstd_ready = ctx.enter_context(nc.semaphore(f"{tag}_rstd_ready"))
        xn_ready = ctx.enter_context(nc.semaphore(f"{tag}_xn_ready"))
        turned = ctx.enter_context(nc.semaphore(f"{tag}_turned"))
        turned_saved = ctx.enter_context(nc.semaphore(f"{tag}_turned_saved"))
        loaded = ctx.enter_context(nc.semaphore(f"{tag}_loaded"))
        block = ctx.enter_context(nc.Block())

        @block.sync
        def _(sp):
            for dst, src in loads:
                sp.dma_start(dst, src, allow_slow_non_contiguous=True).then_inc(loaded, 16)
            if loads:
                sp.wait_ge(loaded, 16 * len(loads))

        @block.vector
        def _(dve):
            for t in range(NT):
                nc.vector.bn_stats(m.stats[:, t * 6:t * 6 + 6], m.x[:, t * D:(t + 1) * D]).then_inc(stats_ready, 1)
            dve.wait_ge(stats_ready, NT)
            for t in range(NT):
                nc.vector.bn_aggr(m.moments[:, t * 2:t * 2 + 2], m.stats[:, t * 6:t * 6 + 6]).then_inc(moments_ready, 1)
            dve.wait_ge(moments_ready, NT)
            mv = m.moments[:, :].rearrange("p (t c) -> p t c", c=2)
            nc.vector.tensor_scalar(m.rstd[:, :], mv[:, :, 1], EPS, None, ALU.add).then_inc(var_eps_ready, 1)
            dve.wait_ge(std_ready, 1)
            nc.vector.reciprocal(m.rstd[:, :], m.std[:, :]).then_inc(rstd_ready, 1)
            dve.wait_ge(rstd_ready, 1)
            for t in range(NT):
                nc.vector.tensor_scalar(m.xn[:, t * D:(t + 1) * D], m.x[:, t * D:(t + 1) * D],
                                        mv[:, t, 0:1], m.rstd[:, t:t + 1], ALU.subtract, ALU.mult).then_inc(xn_ready, 1)

        @block.scalar
        def _(act):
            act.wait_ge(var_eps_ready, 1)
            nc.scalar.activation(m.std[:, :], m.rstd[:, :], ACT.Sqrt).then_inc(std_ready, 1)
            for c in range(NC):
                act.wait_ge(turned, c + 1)
                nc.scalar.activation(m.xnT[:, c * BANK:(c + 1) * BANK], m.psum[:, c, :], ACT.Copy).then_inc(turned_saved, 1)

        @block.tensor
        def _(pe):
            for c in range(NC):
                pe.wait_ge(xn_ready, TPB * (c + 1))
                for i in range(TPB):
                    t = TPB * c + i
                    mm = nc.tensor.transpose(m.psum[:, c, i * P:(i + 1) * P], m.xn[:, t * D:(t + 1) * D], m.ident[:, :])
                mm.then_inc(turned, 1)


def setup_block(nc, m, a):
    with ExitStack() as ctx:
        zeroed = ctx.enter_context(nc.semaphore("zeroed"))
        patterned = ctx.enter_context(nc.semaphore("patterned"))
        loaded = ctx.enter_context(nc.semaphore("loaded"))
        block = ctx.enter_context(nc.Block())

        @block.sync
        def _(sp):
            sp.dma_start(m.x[:, :].rearrange("p (t d) -> p t d", d=D),
                         a["L0_attn_x"][0].rearrange("(t p) d -> p t d", p=P)).then_inc(loaded, 16)
            sp.dma_start(m.ws1[:, :], a["L0_attn_ws1"]).then_inc(loaded, 16)
            sp.dma_start(m.bs1[:, :], a["L0_attn_bs1"].rearrange("(p o) -> p o", o=1)).then_inc(loaded, 16)
            sp.dma_start(m.ws2[:, :], a["L0_attn_ws2"]).then_inc(loaded, 16)
            sp.dma_start(m.bs2[:, :], a["L0_attn_bs2"].rearrange("(o c) -> o c", o=1).broadcast_to([P, 1])).then_inc(loaded, 16)
            sp.wait_ge(loaded, 5 * 16)

        @block.gpsimd
        def _(pool):
            nc.gpsimd.memset(m.ident[:, :], 0.0).then_inc(zeroed, 1)
            nc.gpsimd.memset(m.identb[:, :], 0.0).then_inc(zeroed, 1)
            nc.gpsimd.memset(m.mask[:, :], 0.0).then_inc(zeroed, 1)
            nc.gpsimd.memset(m.ones[:, :], 1.0).then_inc(zeroed, 1)
            pool.wait_ge(zeroed, 4)
            nc.gpsimd.affine_select(out=m.ident[:, :], in_=m.ident[:, :], compare_op=ALU.not_equal, fill=1.0,
                                    base=0, pattern=[[-1, P]], channel_multiplier=1).then_inc(patterned, 1)
            nc.gpsimd.affine_select(out=m.identb[:, :], in_=m.identb[:, :], compare_op=ALU.not_equal, fill=1.0,
                                    base=0, pattern=[[-1, P]], channel_multiplier=1).then_inc(patterned, 1)
            for j in range(2):
                w = m.mask[:, j * WL:j * WL + P]
                nc.gpsimd.affine_select(out=w, in_=w, compare_op=ALU.is_ge, fill=MASKED,
                                        base=0, pattern=[[-1, P]], channel_multiplier=1).then_inc(patterned, 1)


def attn0_block(nc, m, a):
    SCALE = HD0 ** -0.5
    with ExitStack() as ctx:
        def sb(name, shape, dt=F32):
            return ctx.enter_context(nc.sbuf_tensor(name, shape, dt))

        def sem(name):
            return ctx.enter_context(nc.semaphore(name))

        w_cur = sb("w_cur", [P, 3, P])
        wo_cur = sb("wo_cur", [P, D])
        qz = sb("qz", [P, 2, N])
        kx = sb("kx", [P, NT, WL])
        v = sb("v0", [P, NT, P])
        gv = sb("gv", [2 * G0, P])
        gtok = sb("gtok", [P, 2 * G0])
        sm = sb("sm", [P, 4, 2 * WL])
        pr = sb("pr", [P, 4, 2 * WL])
        nmax = sb("nmax", [P, 4, 4])
        total = sb("total", [P, 4, 4])
        rtotal = sb("rtotal", [P, 4, 4])
        pt = sb("pt", [P, 2, 3 * P])
        oT = sb("oT", [P, 3, P])
        ws2r = sb("ws2r", [UH, P])
        gate_h = sb("gate_h", [UH, 1])
        gate_s = sb("gate_s", [P, 1])
        gate_m = sb("gate_m", [P, 1], U32)

        w_loaded = sem("w_loaded")
        wo_loaded = sem("wo_loaded")
        zeroed = sem("zeroed0")
        ws2_spread = sem("ws2_spread")
        token_copied = sem("token_copied")
        score_hidden = sem("score_hidden")
        score_gelu = sem("score_gelu")
        score_ready = sem("score_ready")
        score_saved = sem("score_saved")
        low_ready = sem("low_ready")
        gtok_ready = sem("gtok_ready")
        q_ready, q_saved = sem("q_ready"), sem("q_saved")
        k_ready, k_saved = sem("k_ready"), sem("k_saved")
        v_ready, v_saved = sem("v_ready"), sem("v_saved")
        g_ready, g_saved = sem("g_ready"), sem("g_saved")
        scores_ready, masked = sem("scores_ready"), sem("masked")
        max_ready, exp_ready = sem("max_ready"), sem("exp_ready")
        rtotal_ready, probs_ready = sem("rtotal_ready"), sem("probs_ready")
        pt_ready, pt_saved = sem("pt_ready"), sem("pt_saved")
        o_ready, o_saved = sem("o_ready"), sem("o_saved")
        wo_done, y_added = sem("wo_done"), sem("y_added")
        block = ctx.enter_context(nc.Block())

        def start_at_one(eng, *sems):
            for s in sems:
                eng.sem_inc(s, 1)

        S_B, T_B, O_B, Y_B, G_B = 0, 2, 4, 6, 7

        @block.sync
        def _(sp):
            with sp.Fori(0, PAIRS) as p:
                sp.wait_ge(v_ready, 1 + p * NC)
                for i, w in enumerate((a["L0_attn_wq"], a["L0_attn_wk"], a["L0_attn_wv"])):
                    sp.dma_start(w_cur[:, i, :], w[:, bass.ds(p * P, P)]).then_inc(w_loaded, 16)
                sp.wait_ge(wo_done, 1 + p * NT)
                sp.dma_start(wo_cur[:, :], a["L0_attn_wo"][bass.ds(p * P, P), :]).then_inc(wo_loaded, 16)

        @block.tensor
        def _(pe):
            start_at_one(pe, q_ready, k_ready, v_ready, g_ready, scores_ready, pt_ready, o_ready, wo_done)
            nc.tensor.matmul(m.psum[0:UH, G_B, 0:1], m.ws1[:, :], m.xnT[:, 0:1], start=True, stop=True).then_inc(score_hidden, 1)
            pe.wait_ge(score_gelu, 1)
            pe.wait_ge(ws2_spread, 1)
            nc.tensor.matmul(m.psum[:, Y_B, 0:1], ws2r[:, :], gate_h[:, :], start=True, stop=True).then_inc(score_ready, 1)
            pe.wait_ge(gtok_ready, 1)
            with pe.Fori(0, PAIRS) as p:
                pe.wait_ge(w_loaded, p * 48 + 48)
                pe.wait_ge(masked, 1 + p * NT)
                pe.wait_ge(pt_saved, 1 + p * NT)
                pe.wait_ge(o_saved, 1 + p * NT)
                pe.wait_ge(y_added, 1 + p * NC)
                nc.tensor.matmul(m.psum[:, G_B, 0:G0], w_cur[:, 1, :], gtok[:, 0:G0], start=True, stop=True)
                nc.tensor.matmul(m.psum[0:2 * G0, G_B, P:2 * P], gtok[:, :], w_cur[:, 2, :],
                                 start=True, stop=True).then_inc(g_ready, 1)
                for c in range(NC):
                    if c >= 2:
                        pe.wait_ge(q_saved, 1 + p * NC + c - 1)
                    nc.tensor.matmul(m.psum[:, S_B + c % 2, :], w_cur[:, 0, :], m.xnT[:, c * BANK:(c + 1) * BANK],
                                     start=True, stop=True).then_inc(q_ready, 1)
                    if c >= 2:
                        pe.wait_ge(k_saved, 1 + p * NC + c - 1)
                    nc.tensor.matmul(m.psum[:, T_B + c % 2, :], w_cur[:, 1, :], m.xnT[:, c * BANK:(c + 1) * BANK],
                                     start=True, stop=True).then_inc(k_ready, 1)
                    if c >= 2:
                        pe.wait_ge(v_saved, 1 + p * NC + c - 1)
                    for i in range(TPB):
                        t = TPB * c + i
                        mm = nc.tensor.matmul(m.psum[:, O_B + c % 2, i * P:(i + 1) * P], m.xnT[:, t * P:(t + 1) * P],
                                              w_cur[:, 2, :], start=True, stop=True)
                    mm.then_inc(v_ready, 1)
                pe.wait_ge(q_saved, 1 + p * NC + NC)
                pe.wait_ge(k_saved, 1 + p * NC + NC)
                pe.wait_ge(g_saved, 1 + p + 1)
                for s in range(NT + 4):
                    if s < NT:
                        if s >= 2:
                            pe.wait_ge(masked, 1 + p * NT + s - 1)
                        for j in range(2):
                            mm = nc.tensor.matmul(m.psum[:, S_B + s % 2, j * WL:(j + 1) * WL],
                                                  qz[:, j, s * P:(s + 1) * P], kx[:, s, :], start=True, stop=True)
                        mm.then_inc(scores_ready, 1)
                    w = s - 2
                    if 0 <= w < NT:
                        pe.wait_ge(probs_ready, 1 + p * NT + w + 1)
                        if w >= 2:
                            pe.wait_ge(pt_saved, 1 + p * NT + w - 1)
                        for j in range(2):
                            nc.tensor.transpose(m.psum[:, T_B + w % 2, j * P:(j + 1) * P], pr[:, w % 4, j * P:(j + 1) * P],
                                                m.ident[:, :])
                        nc.tensor.transpose(m.psum[0:2 * G0, T_B + w % 2, 2 * P:3 * P], pr[:, w % 4, 2 * P:2 * WL],
                                            m.ident[:, :]).then_inc(pt_ready, 1)
                    w = s - 3
                    if 0 <= w < NT:
                        if w == 0:
                            pe.wait_ge(v_saved, 1 + p * NC + NC)
                        pe.wait_ge(pt_saved, 1 + p * NT + w + 1)
                        if w >= 2:
                            pe.wait_ge(o_saved, 1 + p * NT + w - 1)
                        ob = m.psum[:, O_B + w % 2, 0:P]
                        nc.tensor.matmul(ob, gv[:, :], pt[0:2 * G0, w % 2, 2 * P:3 * P], start=True, stop=False)
                        for j in range(2):
                            mm = nc.tensor.matmul(ob[j * HD0:(j + 1) * HD0, :], v[:, w, j * HD0:(j + 1) * HD0],
                                                  pt[:, w % 2, j * P:(j + 1) * P], start=False, stop=True)
                        mm.then_inc(o_ready, 1)
                    w = s - 4
                    if 0 <= w < NT:
                        if w == 0:
                            pe.wait_ge(wo_loaded, p * 16 + 16)
                        pe.wait_ge(o_saved, 1 + p * NT + w + 1)
                        if w % TPB == 0 and w >= 2 * TPB:
                            pe.wait_ge(y_added, 1 + p * NC + w // TPB - 1)
                        nc.tensor.matmul(m.psum[:, Y_B + (w // TPB) % 2, (w % TPB) * P:(w % TPB + 1) * P],
                                         oT[:, w % 3, :], wo_cur[:, :], start=True, stop=True).then_inc(wo_done, 1)

        @block.vector
        def _(dve):
            start_at_one(dve, k_saved, v_saved, g_saved, masked, max_ready, rtotal_ready, pt_saved, o_saved, y_added)
            nc.vector.tensor_scalar(ws2r[:, :], m.ones[0:UH, :], m.ws2[:, 0:1], None, ALU.mult).then_inc(ws2_spread, 1)
            nc.vector.tensor_copy(gtok[:, 0:G0], m.xnT[:, 0:G0]).then_inc(token_copied, 1)
            nc.vector.tensor_copy(gtok[:, G0:2 * G0], m.xnT[:, 0:G0]).then_inc(token_copied, 1)
            dve.wait_ge(score_ready, 1)
            nc.vector.tensor_scalar(gate_s[:, :], m.psum[:, Y_B, 0:1], m.bs2[:, 0:1], None, ALU.add).then_inc(score_saved, 1)
            dve.wait_ge(score_saved, 1)
            nc.vector.tensor_scalar(gate_m[:, :], gate_s[:, :], F32_LOW, None, ALU.is_lt).then_inc(low_ready, 1)
            dve.wait_ge(low_ready, 1)
            dve.wait_ge(token_copied, 2)
            for j in range(2):
                nc.vector.copy_predicated(gtok[:, j * G0:j * G0 + 1], gate_m[:, :], m.xnT[:, G0:G0 + 1])\
                    .then_inc(*((gtok_ready, 1) if j else (token_copied, 1)))
            with dve.Fori(0, PAIRS) as p:
                dve.wait_ge(g_ready, 1 + p + 1)
                nc.vector.tensor_copy(kx[:, :, P:WL], m.psum[:, G_B, 0:G0].rearrange("p (o g) -> p o g", o=1)
                                      .broadcast_to([P, NT, G0]))
                dve.wait_ge(zeroed, 3)
                for j in range(2):
                    mm = nc.vector.tensor_copy(gv[j * G0:(j + 1) * G0, j * HD0:(j + 1) * HD0],
                                               m.psum[j * G0:(j + 1) * G0, G_B, P + j * HD0:P + (j + 1) * HD0])
                mm.then_inc(g_saved, 1)
                for c in range(NC):
                    dve.wait_ge(k_ready, 1 + p * NC + c + 1)
                    nc.vector.tensor_copy(kx[:, TPB * c:TPB * (c + 1), 0:P],
                                          m.psum[:, T_B + c % 2, :].rearrange("p (t k) -> p t k", t=TPB)).then_inc(k_saved, 1)
                    dve.wait_ge(v_ready, 1 + p * NC + c + 1)
                    nc.vector.tensor_copy(v[:, TPB * c:TPB * (c + 1), :],
                                          m.psum[:, O_B + c % 2, :].rearrange("p (t k) -> p t k", t=TPB)).then_inc(v_saved, 1)
                for s in range(NT + 5):
                    if s < NT:
                        dve.wait_ge(scores_ready, 1 + p * NT + s + 1)
                        dve.wait_ge(exp_ready, 1 + p * NT + max(s - 3, 0))
                        nc.vector.tensor_tensor(sm[:, s % 4, :], m.psum[:, S_B + s % 2, 0:2 * WL], m.mask[:, :],
                                                ALU.add).then_inc(masked, 1)
                        dve.wait_ge(masked, 1 + p * NT + s + 1)
                        smw = sm[:, s % 4, :].rearrange("p (j c) -> p j c", j=2)
                        nc.vector.tensor_reduce(nmax[:, s % 4, 0:2], smw[:, :, 0:P], AX_X, ALU.max, negate=True)
                        nc.vector.tensor_reduce(nmax[:, s % 4, 2:4], smw[:, :, P:WL], AX_X, ALU.max,
                                                negate=True).then_inc(max_ready, 1)
                    w = s - 1
                    if 0 <= w < NT:
                        dve.wait_ge(exp_ready, 1 + p * NT + w + 1)
                        dve.wait_ge(probs_ready, 1 + p * NT + max(w - 3, 0))
                        nc.vector.reciprocal(rtotal[:, w % 4, :], total[:, w % 4, :]).then_inc(rtotal_ready, 1)
                    w = s - 2
                    if 0 <= w < NT:
                        dve.wait_ge(pt_ready, 1 + p * NT + w + 1)
                        dve.wait_ge(o_ready, 1 + p * NT + max(w - 1, 0))
                        nc.vector.tensor_copy(pt[:, w % 2, 0:2 * P], m.psum[:, T_B + w % 2, 0:2 * P])
                        nc.vector.tensor_copy(pt[0:2 * G0, w % 2, 2 * P:3 * P],
                                              m.psum[0:2 * G0, T_B + w % 2, 2 * P:3 * P]).then_inc(pt_saved, 1)
                    w = s - 3
                    if 0 <= w < NT:
                        dve.wait_ge(o_ready, 1 + p * NT + w + 1)
                        dve.wait_ge(wo_done, 1 + p * NT + max(w - 2, 0))
                        nc.vector.tensor_copy(oT[:, w % 3, :], m.psum[:, O_B + w % 2, 0:P]).then_inc(o_saved, 1)
                    g = s // TPB - 2
                    if s % TPB == 0 and g >= 0:
                        dve.wait_ge(wo_done, 1 + p * NT + TPB * (g + 1))
                        dve.wait_ge(y_added, 1 + p * NC + g)
                        xg = m.x[:, g * BANK:(g + 1) * BANK]
                        nc.vector.tensor_tensor(xg, xg, m.psum[:, Y_B + g % 2, :], ALU.add).then_inc(y_added, 1)

        @block.scalar
        def _(act):
            start_at_one(act, q_saved, exp_ready)
            act.wait_ge(score_hidden, 1)
            nc.scalar.activation(gate_h[:, :], m.psum[0:UH, G_B, 0:1], ACT.Gelu, bias=m.bs1[:, 0:1]).then_inc(score_gelu, 1)
            act.wait_ge(zeroed, 3)
            with act.Fori(0, PAIRS) as p:
                for c in range(NC):
                    act.wait_ge(q_ready, 1 + p * NC + c + 1)
                    for j in range(2):
                        r = slice(j * HD0, (j + 1) * HD0)
                        mm = nc.scalar.activation(qz[r, j, c * BANK:(c + 1) * BANK], m.psum[r, S_B + c % 2, :],
                                                  ACT.Copy, scale=SCALE)
                    mm.then_inc(q_saved, 1)
                for w in range(NT):
                    act.wait_ge(max_ready, 1 + p * NT + w + 1)
                    act.wait_ge(pt_ready, 1 + p * NT + max(w - 3, 0))
                    act.wait_ge(rtotal_ready, 1 + p * NT + max(w - 3, 0))
                    for j in range(2):
                        nc.scalar.activation(pr[:, w % 4, j * P:(j + 1) * P], sm[:, w % 4, j * WL:j * WL + P], ACT.Exp,
                                             bias=nmax[:, w % 4, j:j + 1], accum_out=total[:, w % 4, j:j + 1])
                        mm = nc.scalar.activation(pr[:, w % 4, 2 * P + j * G0:2 * P + (j + 1) * G0],
                                                  sm[:, w % 4, j * WL + P:(j + 1) * WL], ACT.Exp,
                                                  bias=nmax[:, w % 4, 2 + j:3 + j], accum_out=total[:, w % 4, 2 + j:3 + j])
                    mm.then_inc(exp_ready, 1)

        @block.gpsimd
        def _(pool):
            start_at_one(pool, probs_ready)
            nc.gpsimd.memset(qz[HD0:P, 0, :], 0.0).then_inc(zeroed, 1)
            nc.gpsimd.memset(qz[0:HD0, 1, :], 0.0).then_inc(zeroed, 1)
            nc.gpsimd.memset(gv[:, :], 0.0).then_inc(zeroed, 1)
            with pool.Fori(0, PAIRS) as p:
                for w in range(NT):
                    pool.wait_ge(rtotal_ready, 1 + p * NT + w + 1)
                    for cols, r in ((slice(0, 2 * P), slice(0, 2)), (slice(2 * P, 2 * WL), slice(2, 4))):
                        prw = pr[:, w % 4, cols].rearrange("p (j c) -> p j c", j=2)
                        rb = rtotal[:, w % 4, r].rearrange("p (j o) -> p j o", o=1).broadcast_to(list(prw.shape))
                        mm = nc.gpsimd.tensor_tensor(prw, prw, rb, ALU.mult)
                    mm.then_inc(probs_ready, 1)


def memory_block(nc, m, a):
    REPLACED = -3e38
    with ExitStack() as ctx:
        def sb(name, shape, dt=F32):
            return ctx.enter_context(nc.sbuf_tensor(name, shape, dt))

        def sem(name):
            return ctx.enter_context(nc.semaphore(name))

        qyT = sb("qyT", [P, N])
        rqT = sb("rqT", [P, N])
        rkT = sb("rkT", [P, NKEY])
        h1T = sb("h1T", [UH, N])
        logvar = sb("logvar", [P, NT])
        logvar_sum = sb("logvar_sum", [P, 1])
        learned = sb("learned", [P, NT])
        gate = sb("gate", [P, NT])
        norm = sb("norm", [P, 1])
        sc = sb("sc", [P, 3, NKEY])
        sr = sb("sr", [P, NKEY])
        ex = sb("ex", [P, 2, NKEY])
        wt = sb("wt", [P, 2, NKEY])
        wT = sb("wT", [P, 2, NKEY])
        best = sb("best", [P, NT, 8])
        nbest = sb("nbest", [P, NT])
        wsum = sb("wsum", [P, NT])
        coef = sb("coef", [P, NT])

        zeroed = sem("zeroed1")
        qy_ready, qy_saved = sem("qy_ready"), sem("qy_saved")
        rq_ready, rq_saved = sem("rq_ready"), sem("rq_saved")
        h1_ready, h1_saved = sem("h1_ready"), sem("h1_saved")
        learned_ready, logvar_ready, total_ready = sem("learned_ready"), sem("logvar_ready"), sem("total_ready")
        sigmoid_ready, gate_step, gate_ready = sem("sigmoid_ready"), sem("gate_step"), sem("gate_ready")
        stats_ready, var_ready, x_added = sem("m_stats_ready"), sem("m_var_ready"), sem("x_added")
        sc_ready, sc_saved = sem("sc_ready"), sem("sc_saved")
        best_ready, nbest_ready, ex_ready, replaced = sem("best_ready"), sem("nbest_ready"), sem("ex_ready"), sem("replaced")
        wt_ready, wT_ready, wT_saved = sem("wt_ready"), sem("wT_ready"), sem("wT_saved")
        agg_ready, wsum_ready, coef_ready, y_added = sem("agg_ready"), sem("wsum_ready"), sem("coef_ready"), sem("m_y_added")
        block = ctx.enter_context(nc.Block())
        mv = m.moments[:, :].rearrange("p (t c) -> p t c", c=2)

        @block.tensor
        def _(pe):
            for c in range(NC):
                nc.tensor.matmul(m.psum[:, c, :], m.qpT[:, :], m.xnT[:, c * BANK:(c + 1) * BANK],
                                 start=True, stop=True).then_inc(qy_ready, 1)
            for c in range(NC):
                nc.tensor.matmul(m.psum[0:UH, 4 + c, :], m.uw1T[:, :], m.xnT[:, c * BANK:(c + 1) * BANK],
                                 start=True, stop=True).then_inc(h1_ready, 1)
            for c in range(NC):
                pe.wait_ge(qy_saved, c + 1)
                nc.tensor.matmul(m.psum[0:RD, c, :], m.rwT[:, :], qyT[:, c * BANK:(c + 1) * BANK],
                                 start=True, stop=True).then_inc(rq_ready, 1)
            pe.wait_ge(h1_saved, NC)
            nc.tensor.matmul(m.psum[0:RD, 4, :], m.rwT[:, :], m.akT[:, :],
                             start=True, stop=True).then_inc(rq_ready, 1)
            for t in range(NT):
                mm = nc.tensor.matmul(m.psum[:, 5, t:t + 1], h1T[:, t * P:(t + 1) * P], m.uw2T[:, :], start=True, stop=True)
            mm.then_inc(learned_ready, 1)
            pe.wait_ge(logvar_ready, 1)
            nc.tensor.matmul(m.psum[:, 6, 0:1], m.ones[:, :], logvar_sum[:, :], start=True, stop=True).then_inc(total_ready, 1)
            pe.wait_ge(rq_saved, NC + 1)
            for s in range(NT + 3):
                if s < NT:
                    if s >= 2:
                        pe.wait_ge(sc_saved, s - 1)
                    nc.tensor.matmul(m.psum[:, s % 2, :], rqT[:, s * P:(s + 1) * P], rkT[:, :],
                                     start=True, stop=True).then_inc(sc_ready, 1)
                t = s - 2
                if 0 <= t < NT:
                    pe.wait_ge(wt_ready, t + 1)
                    if t >= 2:
                        pe.wait_ge(wT_saved, t - 1)
                    for i in range(NKEY // P):
                        mm = nc.tensor.transpose(m.psum[:, 2 + t % 2, i * P:(i + 1) * P], wt[:, t % 2, i * P:(i + 1) * P],
                                                 m.ident[:, :])
                    mm.then_inc(wT_ready, 1)
                t = s - 3
                if 0 <= t < NT:
                    pe.wait_ge(wT_saved, t + 1)
                    if t == 0:
                        pe.wait_ge(gate_step, 1)
                    if t >= 2:
                        pe.wait_ge(y_added, t - 1)
                    for i in range(NKEY // P):
                        mm = nc.tensor.matmul(m.psum[:, 6 + t % 2, 0:D], wT[:, t % 2, i * P:(i + 1) * P],
                                              m.av[:, i * D:(i + 1) * D], start=(i == 0), stop=(i == NKEY // P - 1))
                    mm.then_inc(agg_ready, 1)

        @block.gpsimd
        def _(pool):
            nc.gpsimd.memset(rqT[:, :], 0.0).then_inc(zeroed, 1)
            nc.gpsimd.memset(rkT[:, :], 0.0).then_inc(zeroed, 1)
            nc.gpsimd.tensor_tensor(m.x[:, :], m.x[:, :], m.xn[:, :], ALU.add).then_inc(x_added, 1)

        @block.vector
        def _(dve):
            for t in range(NT):
                nc.vector.bn_stats(m.stats[:, t * 6:t * 6 + 6], m.xn[:, t * D:(t + 1) * D]).then_inc(stats_ready, 1)
            dve.wait_ge(stats_ready, NT)
            for t in range(NT):
                nc.vector.bn_aggr(m.moments[:, t * 2:t * 2 + 2], m.stats[:, t * 6:t * 6 + 6]).then_inc(var_ready, 1)
            dve.wait_ge(zeroed, 2)
            for c in range(NC + 1):
                dve.wait_ge(rq_ready, c + 1)
                dst = rqT[0:RD, c * BANK:(c + 1) * BANK] if c < NC else rkT[0:RD, :]
                nc.vector.tensor_copy(dst, m.psum[0:RD, c, :]).then_inc(rq_saved, 1)

            def gates():
                dve.wait_ge(total_ready, 1)
                nc.vector.tensor_scalar(norm[:, :], m.psum[:, 6, 0:1], 1.0 / N, 1e-6, ALU.mult, ALU.add).then_inc(gate_step, 1)
                dve.wait_ge(gate_step, 1)
                nc.vector.reciprocal(norm[:, :], norm[:, :]).then_inc(gate_step, 1)
                dve.wait_ge(gate_step, 2)
                nc.vector.tensor_scalar(logvar[:, :], logvar[:, :], norm[:, 0:1], 0.5, ALU.mult, ALU.mult).then_inc(gate_step, 1)
                dve.wait_ge(sigmoid_ready, 1)
                dve.wait_ge(gate_step, 3)
                nc.vector.scalar_tensor_tensor(gate[:, :], learned[:, :], 2.5, logvar[:, :], ALU.mult, ALU.add).then_inc(gate_step, 1)
                dve.wait_ge(gate_step, 4)
                nc.vector.tensor_scalar(gate[:, :], gate[:, :], 0.0, 5.0, ALU.max, ALU.min).then_inc(gate_step, 1)

            for s in range(NT + 4):
                if s < NT:
                    dve.wait_ge(sc_ready, s + 1)
                    if s >= 3:
                        dve.wait_ge(ex_ready, s - 2)
                    nc.vector.scalar_tensor_tensor(sc[:, s % 3, :], m.psum[:, s % 2, :], RD ** -0.5, m.rel[:, :],
                                                   ALU.mult, ALU.add).then_inc(sc_saved, 1)
                    dve.wait_ge(sc_saved, s + 1)
                    nc.vector.max(best[:, s, :], sc[:, s % 3, :]).then_inc(best_ready, 1)
                    dve.wait_ge(best_ready, s + 1)
                    nc.vector.tensor_scalar(nbest[:, s:s + 1], best[:, s, 0:1], -1.0, None, ALU.mult).then_inc(nbest_ready, 1)
                    if s >= 1:
                        dve.wait_ge(wt_ready, s)
                    nc.vector.match_replace(sr[:, :], best[:, s, :], sc[:, s % 3, :], REPLACED).then_inc(replaced, 1)
                    dve.wait_ge(replaced, s + 1)
                    dve.wait_ge(ex_ready, s + 1)
                    if s >= 2:
                        dve.wait_ge(wT_ready, s - 1)
                    nc.vector.scalar_tensor_tensor(wt[:, s % 2, :], sr[:, :], REPLACED, ex[:, s % 2, :], ALU.is_equal, ALU.mult,
                                                   accum_out=wsum[:, s:s + 1]).then_inc(wt_ready, 1)
                if s == 0:
                    gates()
                t = s - 4
                if 0 <= t < NT:
                    if t == 0:
                        dve.wait_ge(gate_ready, 1)
                    dve.wait_ge(wt_ready, t + 1)
                    nc.vector.reciprocal(coef[:, t:t + 1], wsum[:, t:t + 1]).then_inc(wsum_ready, 1)
                    dve.wait_ge(wsum_ready, t + 1)
                    nc.vector.tensor_scalar(coef[:, t:t + 1], coef[:, t:t + 1], gate[:, t:t + 1], None, ALU.mult).then_inc(coef_ready, 1)
                    dve.wait_ge(coef_ready, t + 1)
                    dve.wait_ge(agg_ready, t + 1)
                    dve.wait_ge(x_added, 1)
                    xt = m.x[:, t * D:(t + 1) * D]
                    nc.vector.scalar_tensor_tensor(xt, m.psum[:, 6 + t % 2, 0:D], coef[:, t:t + 1], xt,
                                                   ALU.mult, ALU.add).then_inc(y_added, 1)

        @block.scalar
        def _(act):
            for c in range(NC):
                act.wait_ge(qy_ready, c + 1)
                nc.scalar.activation(qyT[:, c * BANK:(c + 1) * BANK], m.psum[:, c, :], ACT.Copy).then_inc(qy_saved, 1)
            for c in range(NC):
                act.wait_ge(h1_ready, c + 1)
                nc.scalar.activation(h1T[:, c * BANK:(c + 1) * BANK], m.psum[0:UH, 4 + c, :], ACT.Gelu,
                                     bias=m.ub1[:, 0:1]).then_inc(h1_saved, 1)
            act.wait_ge(var_ready, NT)
            nc.scalar.activation(logvar[:, :], mv[:, :, 1], ACT.Ln, bias=m.ones[:, 0:1], accum_out=logvar_sum[:, :])\
                .then_inc(logvar_ready, 1)
            act.wait_ge(learned_ready, 1)
            nc.scalar.activation(learned[:, :], m.psum[:, 5, 0:NT], ACT.Sigmoid, bias=m.ub2[:, 0:1]).then_inc(sigmoid_ready, 1)
            for s in range(NT + 1):
                if s < NT:
                    act.wait_ge(nbest_ready, s + 1)
                    if s >= 2:
                        act.wait_ge(wt_ready, s - 1)
                    nc.scalar.activation(ex[:, s % 2, :], sc[:, s % 3, :], ACT.Exp, bias=nbest[:, s:s + 1]).then_inc(ex_ready, 1)
                if s == 0:
                    act.wait_ge(gate_step, 5)
                    nc.scalar.activation(gate[:, :], gate[:, :], ACT.Sigmoid, scale=m.gw[:, 0:1], bias=m.gb[:, 0:1])\
                        .then_inc(gate_ready, 1)
                t = s - 1
                if 0 <= t < NT:
                    act.wait_ge(wT_ready, t + 1)
                    if t >= 2:
                        act.wait_ge(agg_ready, t - 1)
                    nc.scalar.activation(wT[:, t % 2, :], m.psum[:, 2 + t % 2, :], ACT.Copy).then_inc(wT_saved, 1)


def project1_block(nc, m, a):
    with ExitStack() as ctx:
        def sb(name, shape, dt=F32):
            return ctx.enter_context(nc.sbuf_tensor(name, shape, dt))

        def sem(name):
            return ctx.enter_context(nc.semaphore(name))

        wsw = sb("wsw", [P, 2, P])
        direct = sb("direct", [P, 2, BANK])
        partner = sb("partner", [P, 2, BANK])
        rot = sb("rot", [P, 2, BANK])
        rest = sb("rest", [P, 2, BANK])
        parts = sb("parts", [P, 2, PARTS, N], BF16)

        swapped = sem("swapped")
        qk_ready, direct_ready, partner_ready = sem("qk_ready"), sem("direct_ready"), sem("partner_ready")
        rot_ready, part1, rest_ready, part2, part3 = sem("rot_ready"), sem("part1"), sem("rest_ready"), sem("part2"), sem("part3")
        v_ready, v_saved = sem("v1_ready"), sem("v1_saved")
        stored = sem("parts_stored")
        block = ctx.enter_context(nc.Block())
        weights, biases, biases_sw = (m.wqT, m.wkT), (m.bq, m.bk), (m.bqs, m.bks)

        JOBS = 2 * NC

        @block.tensor
        def _(pe):
            pe.wait_ge(swapped, 4)
            for u in range(JOBS):
                i, c = u // NC, u % NC
                if u >= 3:
                    pe.wait_ge(partner_ready, u - 2)
                rhs = m.xnT[:, c * BANK:(c + 1) * BANK]
                nc.tensor.matmul(m.psum[:, 2 * (u % 3), :], weights[i][:, :], rhs, start=True, stop=True)
                nc.tensor.matmul(m.psum[:, 2 * (u % 3) + 1, :], wsw[:, i, :], rhs, start=True, stop=True).then_inc(qk_ready, 1)
            for c in range(NC):
                if c >= 2:
                    pe.wait_ge(v_saved, c - 1)
                for i in range(TPB):
                    t = c * TPB + i
                    mm = nc.tensor.matmul(m.psum[:, 6 + c % 2, i * P:(i + 1) * P], m.xnT[:, t * P:(t + 1) * P], m.wvT[:, :],
                                          start=True, stop=True)
                mm.then_inc(v_ready, 1)

        @block.vector
        def _(dve):
            for i in range(2):
                src = weights[i][:, :].rearrange("p (f two) -> p f two", two=2)
                dst = wsw[:, i, :].rearrange("p (f two) -> p f two", two=2)
                for k in range(2):
                    nc.vector.tensor_copy(dst[:, :, k], src[:, :, 1 - k]).then_inc(swapped, 1)
            for s in range(JOBS + 1):
                if s < JOBS:
                    u, i, c = s, s // NC, s % NC
                    dve.wait_ge(qk_ready, u + 1)
                    if u >= 2:
                        dve.wait_ge(rot_ready, u - 1)
                    cols = slice(c * BANK, (c + 1) * BANK)
                    nc.vector.scalar_tensor_tensor(direct[:, u % 2, :], m.psum[:, 2 * (u % 3), :], biases[i][:, 0:1],
                                                   m.cos[:, cols], ALU.add, ALU.mult).then_inc(direct_ready, 1)
                    nc.vector.scalar_tensor_tensor(partner[:, u % 2, :], m.psum[:, 2 * (u % 3) + 1, :], biases_sw[i][:, 0:1],
                                                   m.sin[:, cols], ALU.add, ALU.mult).then_inc(partner_ready, 1)
                u = s - 1
                if u >= 0:
                    i, c = u // NC, u % NC
                    dve.wait_ge(rot_ready, u + 1)
                    dve.wait_ge(part1, u + 1)
                    if u >= 2:
                        dve.wait_ge(part3, u - 1)
                    nc.vector.tensor_tensor(rest[:, u % 2, :], rot[:, u % 2, :], parts[:, i, 0, c * BANK:(c + 1) * BANK],
                                            ALU.subtract).then_inc(rest_ready, 1)
            bv = m.bv[:, :].rearrange("p (o d) -> p o d", o=1).broadcast_to([P, TPB, D])
            for c in range(NC):
                dve.wait_ge(v_ready, c + 1)
                nc.vector.tensor_tensor(m.v1[:, c * TPB:(c + 1) * TPB, :],
                                        m.psum[:, 6 + c % 2, :].rearrange("p (t d) -> p t d", d=D), bv, ALU.add).then_inc(v_saved, 1)

        @block.gpsimd
        def _(pool):
            for s in range(JOBS + 1):
                if s < JOBS:
                    pool.wait_ge(partner_ready, s + 1)
                    if s >= 2:
                        pool.wait_ge(rest_ready, s - 1)
                    nc.gpsimd.tensor_tensor(rot[:, s % 2, :], direct[:, s % 2, :], partner[:, s % 2, :], ALU.add).then_inc(rot_ready, 1)
                u = s - 1
                if u >= 0:
                    i, c = u // NC, u % NC
                    pool.wait_ge(part2, u + 1)
                    cols = slice(c * BANK, (c + 1) * BANK)
                    nc.gpsimd.tensor_tensor(parts[:, i, 2, cols], rest[:, u % 2, :], parts[:, i, 1, cols], ALU.subtract).then_inc(part3, 1)

        @block.scalar
        def _(act):
            for s in range(JOBS + 1):
                if s < JOBS:
                    i, c = s // NC, s % NC
                    act.wait_ge(rot_ready, s + 1)
                    nc.scalar.activation(parts[:, i, 0, c * BANK:(c + 1) * BANK], rot[:, s % 2, :], ACT.Copy).then_inc(part1, 1)
                u = s - 1
                if u >= 0:
                    i, c = u // NC, u % NC
                    act.wait_ge(rest_ready, u + 1)
                    nc.scalar.activation(parts[:, i, 1, c * BANK:(c + 1) * BANK], rest[:, u % 2, :], ACT.Copy).then_inc(part2, 1)

        @block.sync
        def _(sp):
            for i, scratch in enumerate((m.q_parts, m.k_parts)):
                sp.wait_ge(part3, NC * (i + 1))
                sp.dma_start(scratch.rearrange("s r n -> r s n"), parts[:, i, :, :]).then_inc(stored, 16)
            sp.wait_ge(stored, 32)


def attn1_block(nc, m, a):
    SCALE = HD1 ** -0.5
    HALF = 2 * BANK
    NB = 3
    with ExitStack() as ctx:
        def sb(name, shape, dt=F32):
            return ctx.enter_context(nc.sbuf_tensor(name, shape, dt))

        def sem(name):
            return ctx.enter_context(nc.semaphore(name))

        qf = sb("qf", [KROWS, NB, N], BF16)
        kf = sb("kf", [KROWS, NB, N], BF16)
        vx = sb("vx", [P, NB, NT, VCOLS])
        pb = sb("pb", [P, 2, NC, BANK])
        rowmax = sb("rowmax", [P, NT, 2])
        nmax = sb("nmax1", [P, NT])
        nrest = sb("nrest", [P, NT])
        nparts = sb("nparts", [P, P // NT, NT], BF16)
        nT = sb("nT", [PARTS * NT, P], BF16)
        acc = sb("acc", [P, BANK])
        rsum = sb("rsum", [P, NT])

        loaded = [sem(f"qk_loaded{b}") for b in range(NB)]
        ones_loaded = sem("ones_loaded")
        nparts_zeroed = sem("nparts_zeroed")
        vx_zeroed, vx_ready = sem("vx_zeroed"), sem("vx_ready")
        rows_ready, rows_reduced = sem("rows_ready"), sem("rows_reduced")
        nmax_ready, npart1, nrest1, npart2, npart3 = sem("nmax_ready"), sem("npart1"), sem("nrest1"), sem("npart2"), sem("npart3")
        nT_ready, nT_saved, max_rows_loaded = sem("nT_ready"), sem("nT_saved"), sem("max_rows_loaded")
        st_ready, exp_ready, av_done = sem("st_ready"), sem("exp1_ready"), sem("av_done")
        acc_saved, accT_ready, rsum_ready, att_ready = sem("acc_saved"), sem("accT_ready"), sem("rsum_ready"), sem("att_ready")
        block = ctx.enter_context(nc.Block())

        START = 2

        def start_counts(eng, *sems):
            for s in sems:
                eng.sem_inc(s, START)

        M_B, E_B, A_B, T_B = 0, 4, 6, 7
        UNITS = NT * NC
        HALVES = 2 * NT
        ROUNDS = H1 // NB - 1
        LEAD = 12
        LOAD = 16 * 2 * PARTS * PARTS

        @block.sync
        def _(sp):
            for b in range(NB):
                sp.dma_start(kf[QROWS:KROWS, b, :], m.ones_rows).then_inc(ones_loaded, 16)

            def load(h, b):
                for j in range(PARTS):
                    r = slice(j * PARTS * HD1, (j + 1) * PARTS * HD1)
                    for i in range(PARTS):
                        r = slice((j * PARTS + i) * HD1, (j * PARTS + i + 1) * HD1)
                        sp.dma_start(qf[r, b, :], m.q_parts[i, bass.ds(h * HD1, HD1), :]).then_inc(loaded[b], 16)
                        sp.dma_start(kf[r, b, :], m.k_parts[j, bass.ds(h * HD1, HD1), :]).then_inc(loaded[b], 16)

            def max_rows(g, b):
                sp.wait_ge(nT_saved, START + g + 1)
                for i in range(PARTS):
                    sp.dma_start(qf[QROWS + i:QROWS + i + 1, b, :], nT[i * NT:(i + 1) * NT, :]).then_inc(max_rows_loaded, 16)

            for b in range(NB):
                load(b, b)
            max_rows(0, 0)
            with sp.Fori(0, ROUNDS) as r:
                for b in range(NB):
                    max_rows(r * NB + b + 1, (b + 1) % NB)
                    sp.wait_ge(av_done, START + (r * NB + b + 1) * NT)
                    load(r * NB + b + NB, b)
            for h in range(H1 - 1 - NB, H1 - 1):
                max_rows(h + 1, (h + 1) % NB)
                if h == H1 - 1 - NB:
                    sp.wait_ge(av_done, START + (h + 1) * NT)
                    load(h + NB, h % NB)

        @block.tensor
        def _(pe):
            start_counts(pe, rows_ready, nT_ready, st_ready, av_done, accT_ready)

            def rows(g, b, n):
                t, c, u = n // NC, n % NC, n // 2
                if n % 2 == 0:
                    pe.wait_ge(rows_reduced, START + g * HALVES + u - 1)
                mm = nc.tensor.matmul(m.psum[:, M_B + (u % 2) * 2 + n % 2, :], qf[0:QROWS, b, t * P:(t + 1) * P],
                                      kf[0:QROWS, b, c * BANK:(c + 1) * BANK], start=True, stop=True)
                if n % 2:
                    mm.then_inc(rows_ready, 1)

            def turn_max(g):
                pe.wait_ge(npart3, START + g + 1)
                pe.wait_ge(att_ready, START + g - 1)
                nc.tensor.transpose(m.psum[:, T_B, 0:P // 2].bitcast(BF16),
                                    nparts[:, :, :].rearrange("p a t -> p (a t)"), m.identb[:, :]).then_inc(nT_ready, 1)

            def turn_sums(h, last):
                pe.wait_ge(acc_saved, START + h + 1)
                pe.wait_ge(nT_saved, START + h + (1 if last else 2))
                for i in range(NC):
                    mm = nc.tensor.transpose(m.psum[:, T_B, i * P:(i + 1) * P], acc[:, i * P:(i + 1) * P], m.ident[:, :])
                mm.then_inc(accT_ready, 1)

            def weigh(h, b, t):
                pe.wait_ge(exp_ready, START + h * UNITS + (t + 1) * NC)
                if t == 0:
                    pe.wait_ge(acc_saved, START + h)
                    pe.wait_ge(vx_ready, START + h + 1)
                for c in range(NC):
                    mm = nc.tensor.matmul(m.psum[c * VCOLS:(c + 1) * VCOLS, A_B, :], vx[:, b, t, :], pb[:, t % 2, c, :],
                                          start=(t == 0), stop=(t == NT - 1))
                mm.then_inc(av_done, 1)

            def head(r, b):
                h = r * NB + b
                left = H1 - 1 - h if isinstance(h, int) else NB
                pe.wait_ge(max_rows_loaded, h * 16 * PARTS + 16 * PARTS)
                n = LEAD
                for t in range(NT + 1):
                    if n == UNITS and left >= 2:
                        b2 = b + 2
                        pe.wait_ge(loaded[b2 % NB], r * LOAD + (1 + b2 // NB) * LOAD)
                    for c, beside in enumerate((1, 2, 1, 0)):
                        if t == NT:
                            break
                        k = t * NC + c
                        pe.wait_ge(exp_ready, START + h * UNITS + k - 1)
                        nc.tensor.matmul(m.psum[:, E_B + k % 2, :], kf[:, b, t * P:(t + 1) * P],
                                         qf[:, b, c * BANK:(c + 1) * BANK], start=True, stop=True).then_inc(st_ready, 1)
                        for _ in range(beside):
                            if n < UNITS and left >= 1:
                                rows(h + 1, (b + 1) % NB, n)
                            elif n >= UNITS and left >= 2:
                                rows(h + 2, (b + 2) % NB, n - UNITS)
                            n += 1
                    if t >= 1:
                        weigh(h, b, t - 1)
                    if t == NT - 2 and left >= 1:
                        turn_max(h + 1)
                turn_sums(h, left == 0)

            pe.wait_ge(ones_loaded, 16 * NB)
            pe.wait_ge(loaded[0], LOAD)
            for n in range(UNITS):
                rows(0, 0, n)
            pe.wait_ge(loaded[1], LOAD)
            for n in range(LEAD):
                if n == 4:
                    turn_max(0)
                rows(1, 1, n)
            with pe.Fori(0, ROUNDS) as r:
                for b in range(NB):
                    head(r, b)
            for h in range(ROUNDS * NB, H1):
                head(h // NB, h % NB)

        @block.vector
        def _(dve):
            start_counts(dve, rows_reduced, nmax_ready, npart1, nrest1, npart2, npart3, nT_saved, acc_saved, rsum_ready, att_ready)

            def reduce_rows(g, first, end):
                for u in range(first, end):
                    dve.wait_ge(rows_ready, START + g * HALVES + u + 1)
                    nc.vector.tensor_reduce(rowmax[:, u // 2, u % 2:u % 2 + 1],
                                            m.psum[:, M_B + (u % 2) * 2:M_B + (u % 2) * 2 + 2, :].rearrange("p b c -> p (b c)"),
                                            AX_X, ALU.max).then_inc(rows_reduced, 1)

            def split_maxima(g):
                dve.wait_ge(rows_reduced, START + (g + 1) * HALVES)
                nc.vector.tensor_reduce(nmax[:, :], rowmax[:, :, :], AX_X, ALU.max, negate=True).then_inc(nmax_ready, 1)
                dve.wait_ge(nmax_ready, START + g + 1)
                nc.vector.tensor_copy(nparts[:, 0, :], nmax[:, :]).then_inc(npart1, 1)
                dve.wait_ge(npart1, START + g + 1)
                nc.vector.tensor_tensor(nrest[:, :], nmax[:, :], nparts[:, 0, :], ALU.subtract).then_inc(nrest1, 1)
                dve.wait_ge(nrest1, START + g + 1)
                nc.vector.tensor_copy(nparts[:, 1, :], nrest[:, :]).then_inc(npart2, 1)
                dve.wait_ge(npart2, START + g + 1)
                nc.vector.tensor_tensor(nparts[:, 2, :], nrest[:, :], nparts[:, 1, :], ALU.subtract).then_inc(npart3, 1)

            def save_turned(g):
                if not (isinstance(g, int) and g == 0):
                    dve.wait_ge(max_rows_loaded, g * 16 * PARTS)
                dve.wait_ge(nT_ready, START + g + 1)
                nc.vector.tensor_copy(nT[:, :], m.psum[0:PARTS * NT, T_B, 0:P // 2].bitcast(BF16)).then_inc(nT_saved, 1)

            def sums(h):
                dve.wait_ge(av_done, START + (h + 1) * NT)
                dve.wait_ge(accT_ready, START + h)
                nc.vector.tensor_copy(acc[:, :], m.psum[:, A_B, :]).then_inc(acc_saved, 1)
                dve.wait_ge(accT_ready, START + h + 1)
                turned = m.psum[:, T_B, :].rearrange("p (i j c) -> p i j c", i=TPB, j=NC)
                nc.vector.reciprocal(rsum[:, :].rearrange("p (i j) -> p i j", i=TPB), turned[:, :, :, HD1]).then_inc(rsum_ready, 1)
                dve.wait_ge(rsum_ready, START + h + 1)
                rb = rsum[:, :].rearrange("p (i j o) -> p i j o", i=TPB, o=1).broadcast_to([P, TPB, NC, HD1])
                dst = m.att[:, :, bass.ds(h * HD1, HD1)].rearrange("p (j i) d -> p i j d", i=TPB)
                nc.vector.tensor_tensor(dst, turned[:, :, :, 0:HD1], rb, ALU.mult).then_inc(att_ready, 1)

            nc.vector.memset(nparts[:, :, :], 0.0).then_inc(nparts_zeroed, 1)
            dve.wait_ge(nparts_zeroed, 1)

            def maxima(g, more):
                split_maxima(g)
                if more:
                    reduce_rows(g + 1, 0, 2)
                save_turned(g)
                if more:
                    reduce_rows(g + 1, 2, LEAD // 2)

            reduce_rows(0, 0, HALVES)
            maxima(0, True)
            with dve.Fori(0, ROUNDS) as r:
                for b in range(NB):
                    h = r * NB + b
                    reduce_rows(h + 1, LEAD // 2, HALVES)
                    maxima(h + 1, True)
                    sums(h)
            for h in range(ROUNDS * NB, H1):
                if h + 1 < H1:
                    reduce_rows(h + 1, LEAD // 2, HALVES)
                    maxima(h + 1, h + 2 < H1)
                sums(h)

        @block.scalar
        def _(act):
            start_counts(act, exp_ready)

            def head(h):
                for k in range(UNITS):
                    t, c = k // NC, k % NC
                    if c == 0:
                        act.wait_ge(av_done, START + h * NT + t - 1)
                    act.wait_ge(st_ready, START + h * UNITS + k + 1)
                    nc.scalar.activation(pb[:, t % 2, c, :], m.psum[:, E_B + k % 2, :], ACT.Exp, scale=SCALE).then_inc(exp_ready, 1)

            with act.Fori(0, ROUNDS) as r:
                for b in range(NB):
                    head(r * NB + b)
            for h in range(ROUNDS * NB, H1):
                head(h)

        @block.gpsimd
        def _(pool):
            start_counts(pool, vx_ready)
            nc.gpsimd.memset(vx[:, :, :, :], 0.0).then_inc(vx_zeroed, 1)
            pool.wait_ge(vx_zeroed, 1)
            nc.gpsimd.memset(vx[:, :, :, HD1:HD1 + 1], 1.0).then_inc(vx_zeroed, 1)
            pool.wait_ge(vx_zeroed, 2)

            def values(h, b):
                nc.gpsimd.tensor_copy(vx[:, b, :, 0:HD1], m.v1[:, :, bass.ds(h * HD1, HD1)]).then_inc(vx_ready, 1)

            for b in range(NB):
                values(b, b)
            with pool.Fori(0, ROUNDS) as r:
                for b in range(NB):
                    pool.wait_ge(av_done, START + (r * NB + b + 1) * NT)
                    values(r * NB + b + NB, b)
            pool.wait_ge(av_done, START + (H1 - NB) * NT)
            values(H1 - 1, 0)


def output1_block(nc, m, a):
    with ExitStack() as ctx:
        def sem(name):
            return ctx.enter_context(nc.semaphore(name))

        attT = ctx.enter_context(nc.sbuf_tensor("attT", [P, N], F32))
        attT_ready, attT_saved, biased = sem("attT_ready"), sem("attT_saved"), sem("biased")
        o_ready, x_added = sem("o1_ready"), sem("o1_added")
        block = ctx.enter_context(nc.Block())

        @block.gpsimd
        def _(pool):
            bo = m.bo[:, :].rearrange("p (o d) -> p o d", o=1).broadcast_to([P, NT, D])
            x = m.x[:, :].rearrange("p (t d) -> p t d", d=D)
            nc.gpsimd.tensor_tensor(x, x, bo, ALU.add).then_inc(biased, 1)

        @block.tensor
        def _(pe):
            for c in range(NC):
                for i in range(TPB):
                    mm = nc.tensor.transpose(m.psum[:, c, i * P:(i + 1) * P], m.att[:, c * TPB + i, :], m.ident[:, :])
                mm.then_inc(attT_ready, 1)
            for c in range(NC):
                pe.wait_ge(attT_saved, c + 1)
                for i in range(TPB):
                    t = c * TPB + i
                    mm = nc.tensor.matmul(m.psum[:, 4 + c, i * P:(i + 1) * P], attT[:, t * P:(t + 1) * P], m.woT[:, :],
                                          start=True, stop=True)
                mm.then_inc(o_ready, 1)

        @block.scalar
        def _(act):
            for c in range(NC):
                act.wait_ge(attT_ready, c + 1)
                nc.scalar.activation(attT[:, c * BANK:(c + 1) * BANK], m.psum[:, c, :], ACT.Copy).then_inc(attT_saved, 1)

        @block.vector
        def _(dve):
            dve.wait_ge(biased, 1)
            for c in range(NC):
                dve.wait_ge(o_ready, c + 1)
                xc = m.x[:, c * BANK:(c + 1) * BANK]
                nc.vector.tensor_tensor(xc, xc, m.psum[:, 4 + c, :], ALU.add).then_inc(x_added, 1)


def experts_block(nc, m, a):
    K = NETS * HT
    with ExitStack() as ctx:
        def sb(name, shape, dt=F32):
            return ctx.enter_context(nc.sbuf_tensor(name, shape, dt))

        def sem(name):
            return ctx.enter_context(nc.semaphore(name))

        w1 = sb("w1", [P, NETS, HID])
        w2 = sb("w2", [P, NETS, HT, D])
        w2s = sb("w2s", [P, NETS, HT, D])
        b1 = sb("b1", [P, NETS, HT])
        b2 = sb("b2", [P, NETS, D])
        b2s = sb("b2s", [P, D])
        hT = sb("hT", [P, K, BANK])
        mean = sb("mean", [P, 1])
        lg = sb("lg", [1, NE])
        pw = sb("pw", [1, NE])
        psum_1 = sb("psum_1", [1, 1])
        nlg = sb("nlg", [1, 1])
        top = sb("top", [1, 8])
        chosen = sb("chosen", [1, 8], U32)
        cf = sb("cf", [1, NETS])
        cfb = sb("cfb", [P, NETS])
        al = sb("al", [1, 2])

        main_loaded, expert_loaded = sem("main_loaded"), sem("expert_loaded")
        step, logits_ready, exp_done, cf_ready, coef_ready, cfb_saved = (sem("step"), sem("logits_ready"), sem("exp2_ready"),
                                                                         sem("cf_ready"), sem("coefs_ready"), sem("cfb_saved"))
        chosen_ready, w2s_ready, b2_added = sem("chosen_ready"), sem("w2s_ready"), sem("b2_added")
        b2_step = sem("b2_step")
        h_ready, h_saved, y_ready, y_added = sem("h_ready"), sem("h_saved"), sem("y_ready"), sem("y2_added")
        block = ctx.enter_context(nc.Block())
        START = 2

        @block.sync
        def _(sp):
            def net(i, w1_src, w2_src, b1_src, b2_src, s):
                sp.dma_start(w1[:, i, :], w1_src).then_inc(s, 16)
                sp.dma_start(w2[:, i, :, :], w2_src.rearrange("(k p) d -> p k d", p=P)).then_inc(s, 16)
                sp.dma_start(b1[:, i, :], b1_src.rearrange("(k p) -> p k", p=P), allow_slow_non_contiguous=True).then_inc(s, 16)
                sp.dma_start(b2[:, i, :], b2_src.broadcast_to([P, D])).then_inc(s, 16)

            net(0, a["L1_ffn_W1m"], a["L1_ffn_W2m"], a["L1_ffn_b1m"], a["L1_ffn_b2m"].rearrange("(o d) -> o d", o=1), main_loaded)
            sp.wait_ge(chosen_ready, 1)
            for i in range(2):
                e = sp.value_load(chosen[0:1, i:i + 1], min_val=0, max_val=NE - 1)
                net(1 + i, a["L1_ffn_W1e"][bass.ds(e, 1)].rearrange("o d h -> (o d) h"),
                    a["L1_ffn_W2e"][bass.ds(e, 1)].rearrange("o h d -> (o h) d"),
                    a["L1_ffn_b1e"][bass.ds(e, 1)].rearrange("o h -> (o h)"), a["L1_ffn_b2e"][bass.ds(e, 1), :], expert_loaded)

        @block.vector
        def _(dve):
            n = [0]

            def chain(ins):
                n[0] += 1
                ins.then_inc(step, 1)
                dve.wait_ge(step, n[0])

            dve.sem_inc(y_added, START)
            chain(nc.vector.tensor_reduce(mean[:, :], m.xnT[:, :], AX_X, ALU.add))
            nc.vector.tensor_scalar(mean[:, :], mean[:, :], 1.0 / N, None, ALU.mult).then_inc(cf_ready, 1)
            dve.wait_ge(logits_ready, 1)
            chain(nc.vector.tensor_tensor(lg[:, :], m.psum[0:1, 6, 0:NE], m.bg[:, :], ALU.add))
            chain(nc.vector.tensor_reduce(nlg[:, :], lg[:, :], AX_X, ALU.max, negate=True))
            nc.vector.tensor_scalar(al[:, 0:1], m.alpha[:, :], 0.1, 1.0, ALU.max, ALU.min).then_inc(cf_ready, 1)
            dve.wait_ge(exp_done, 1)
            chain(nc.vector.reciprocal(psum_1[:, :], psum_1[:, :]))
            chain(nc.vector.tensor_scalar(pw[:, :], pw[:, :], psum_1[:, 0:1], None, ALU.mult))
            chain(nc.vector.max(top[:, :], pw[:, :]))
            nc.vector.max_index(chosen[:, :], top[:, :], pw[:, :]).then_inc(chosen_ready, 1)
            chain(nc.vector.tensor_tensor(nlg[:, :], top[:, 0:1], top[:, 1:2], ALU.add))
            chain(nc.vector.reciprocal(nlg[:, :], nlg[:, :]))
            chain(nc.vector.tensor_scalar(al[:, 1:2], al[:, 0:1], -1.0, 1.0, ALU.mult, ALU.add))
            chain(nc.vector.tensor_copy(cf[:, 0:1], al[:, 0:1]))
            nc.vector.tensor_scalar(cf[:, 1:3], top[:, 0:2], nlg[:, 0:1], al[:, 1:2], ALU.mult, ALU.mult).then_inc(cf_ready, 1)
            dve.wait_ge(coef_ready, 1)
            nc.vector.tensor_copy(cfb[:, :], m.psum[:, 7, 0:NETS]).then_inc(cfb_saved, 1)
            dve.wait_ge(cfb_saved, 1)
            for i in range(NETS):
                dve.wait_ge(*((expert_loaded, 128) if i else (main_loaded, 64)))
                nc.vector.tensor_scalar(w2s[:, i, :, :], w2[:, i, :, :], cfb[:, i:i + 1], None, ALU.mult).then_inc(w2s_ready, 1)
            nc.vector.tensor_scalar(b2s[:, :], b2[:, 0, :], cfb[:, 0:1], None, ALU.mult).then_inc(b2_step, 1)
            for i in range(1, NETS):
                dve.wait_ge(b2_step, i)
                nc.vector.scalar_tensor_tensor(b2s[:, :], b2[:, i, :], cfb[:, i:i + 1], b2s[:, :], ALU.mult, ALU.add).then_inc(b2_step, 1)
            dve.wait_ge(b2_added, 1)
            with dve.Fori(0, NC) as c:
                dve.wait_ge(y_ready, START + c + 1)
                xc = m.x[:, bass.ds(c * BANK, BANK)]
                nc.vector.tensor_tensor(xc, xc, m.psum[:, 4, :], ALU.add).then_inc(y_added, 1)

        @block.gpsimd
        def _(pool):
            pool.wait_ge(b2_step, NETS)
            x = m.x[:, :].rearrange("p (t d) -> p t d", d=D)
            nc.gpsimd.tensor_tensor(x, x, b2s[:, :].rearrange("p (o d) -> p o d", o=1).broadcast_to([P, NT, D]),
                                    ALU.add).then_inc(b2_added, 1)

        @block.scalar
        def _(act):
            act.sem_inc(h_saved, START)
            act.wait_ge(step, 3)
            nc.scalar.activation(pw[:, :], lg[:, :], ACT.Exp, bias=nlg[:, 0:1], accum_out=psum_1[:, :]).then_inc(exp_done, 1)
            act.wait_ge(main_loaded, 64)
            act.wait_ge(expert_loaded, 128)
            b1f = b1[:, :, :].rearrange("p i k -> p (i k)")
            with act.Fori(0, NC) as c:
                for k in range(K):
                    act.wait_ge(h_ready, START + c * K + k + 1)
                    nc.scalar.activation(hT[:, k, :], m.psum[:, k % 4, :], ACT.Gelu_apprx_tanh, bias=b1f[:, k:k + 1]).then_inc(h_saved, 1)

        @block.tensor
        def _(pe):
            pe.sem_inc(h_ready, START)
            pe.sem_inc(y_ready, START)
            pe.wait_ge(cf_ready, 1)
            nc.tensor.matmul(m.psum[0:1, 6, 0:NE], mean[:, :], m.wg[:, :], start=True, stop=True).then_inc(logits_ready, 1)
            pe.wait_ge(cf_ready, 3)
            nc.tensor.matmul(m.psum[:, 7, 0:NETS], m.ones[0:1, :], cf[:, :], start=True, stop=True).then_inc(coef_ready, 1)
            pe.wait_ge(main_loaded, 64)
            pe.wait_ge(expert_loaded, 128)
            pe.wait_ge(w2s_ready, NETS)
            with pe.Fori(0, NC) as c:
                for k in range(K):
                    i, q = k // HT, k % HT
                    pe.wait_ge(h_saved, START + c * K + max(k - 3, 0))
                    nc.tensor.matmul(m.psum[:, k % 4, :], w1[:, i, q * P:(q + 1) * P], m.xnT[:, bass.ds(c * BANK, BANK)],
                                     start=True, stop=True).then_inc(h_ready, 1)
                pe.wait_ge(y_added, START + c)
                for j in range(TPB):
                    for k in range(K):
                        if j == 0:
                            pe.wait_ge(h_saved, START + c * K + k + 1)
                        mm = nc.tensor.matmul(m.psum[:, 4, j * P:(j + 1) * P], hT[:, k, j * P:(j + 1) * P],
                                              w2s[:, k // HT, k % HT, :], start=(k == 0), stop=(k == K - 1))
                mm.then_inc(y_ready, 1)


def store_block(nc, m, out):
    with ExitStack() as ctx:
        stored = ctx.enter_context(nc.semaphore("stored"))
        block = ctx.enter_context(nc.Block())

        @block.sync
        def _(sp):
            sp.dma_start(out[0].rearrange("(t p) d -> p t d", p=P),
                         m.x[:, :].rearrange("p (t d) -> p t d", d=D)).then_inc(stored, 16)
            sp.wait_ge(stored, 16)


def build(nc, a, out):
    with ExitStack() as ctx:
        def sb(name, shape, dt=F32):
            return ctx.enter_context(nc.sbuf_tensor(name, shape, dt))

        m = Memory()
        m.x = sb("x", [P, NT * D])
        m.xn = sb("xn", [P, NT * D])
        m.xnT = sb("xnT", [P, N])
        m.stats = sb("stats", [P, NT * 6])
        m.moments = sb("moments", [P, NT * 2])
        m.std = sb("std", [P, NT])
        m.rstd = sb("rstd", [P, NT])
        m.ident = sb("ident", [P, P])
        m.identb = sb("identb", [P, P], BF16)
        m.ones = sb("ones", [P, P])
        m.mask = sb("mask", [P, 2 * WL])
        m.ws1 = sb("ws1", [P, UH])
        m.bs1 = sb("bs1", [UH, 1])
        m.ws2 = sb("ws2", [UH, 1])
        m.bs2 = sb("bs2", [P, 1])
        m.psum = ctx.enter_context(nc.psum_tensor("psum", [P, 8, BANK], F32))
        setup_block(nc, m, a)
        ln_block(nc, m, "ln0")
        attn0_block(nc, m, a)

        def row(ap):
            return ap.rearrange("(o d) -> o d", o=1)

        def column(ap):
            return ap.rearrange("(p o) -> p o", o=1)

        with ExitStack() as layer:
            def lb(name, shape, dt=F32):
                return layer.enter_context(nc.sbuf_tensor(name, shape, dt))

            m.qpT, m.rwT, m.akT = lb("qpT", [P, P]), lb("rwT", [P, RD]), lb("akT", [P, NKEY])
            m.av, m.rel = lb("av", [P, NKEY // P * D]), lb("rel", [P, NKEY])
            m.uw1T, m.ub1, m.uw2T, m.ub2 = lb("uw1T", [P, UH]), lb("ub1", [UH, 1]), lb("uw2T", [UH, 1]), lb("ub2", [P, 1])
            m.gw, m.gb = lb("gw", [P, 1]), lb("gb", [P, 1])
            ln_block(nc, m, "ln1", [
                (m.qpT[:, :], a["L0_ffn_q_proj_w"]), (m.rwT[:, :], a["L0_ffn_router_w"]), (m.akT[:, :], a["L0_ffn_aux_keys"]),
                (m.av[:, :].rearrange("p (k d) -> p k d", d=D), a["L0_ffn_aux_values"].rearrange("(k p) d -> p k d", p=P)),
                (m.rel[:, :], row(a["L0_ffn_reliability_mask"]).broadcast_to([P, NKEY])),
                (m.uw1T[:, :], a["L0_ffn_unc_w1"]), (m.ub1[:, :], column(a["L0_ffn_unc_b1"])), (m.uw2T[:, :], a["L0_ffn_unc_w2"]),
                (m.ub2[:, :], row(a["L0_ffn_unc_b2"]).broadcast_to([P, 1])), (m.gw[:, :], row(a["L0_ffn_gate_w1"]).broadcast_to([P, 1])),
                (m.gb[:, :], row(a["L0_ffn_gate_bias"]).broadcast_to([P, 1]))])
            memory_block(nc, m, a)
        with ExitStack() as layer:
            def lb(name, shape, dt=F32):
                return layer.enter_context(nc.sbuf_tensor(name, shape, dt))

            m.v1, m.att = lb("v1", [P, NT, D]), lb("att", [P, NT, D])
            m.woT, m.bo = lb("woT", [P, P]), lb("bo", [P, D])
            m.q_parts = nc.dram_tensor("q_parts", [PARTS, P, N], BF16, kind="Internal").ap()
            m.k_parts = nc.dram_tensor("k_parts", [PARTS, P, N], BF16, kind="Internal").ap()
            m.ones_rows = nc.inline_tensor(np.ones((PARTS, N), mybir.dt.np(BF16)), "ones_rows").ap()
            freq = (1.0 / np.float32(10000.0) ** (np.arange(0, HD1, 2, dtype=np.float32) / HD1)).astype(np.float32)
            angle = np.arange(N, dtype=np.float32)[None, :] * np.repeat(freq, 2)[:, None]
            sign = np.where(np.arange(HD1) % 2, 1.0, -1.0).astype(np.float32)[:, None]
            cos_t = nc.inline_tensor(np.tile(np.cos(angle), (H1, 1)).astype(np.float32), "cos_table").ap()
            sin_t = nc.inline_tensor(np.tile(np.sin(angle) * sign, (H1, 1)).astype(np.float32), "sin_table").ap()
            with ExitStack() as early:
                def eb(name, shape, dt=F32):
                    return early.enter_context(nc.sbuf_tensor(name, shape, dt))

                m.wqT, m.wkT, m.wvT = eb("wqT", [P, P]), eb("wkT", [P, P]), eb("wvT", [P, P])
                m.bq, m.bk, m.bqs, m.bks, m.bv = eb("bq", [P, 1]), eb("bk", [P, 1]), eb("bqs", [P, 1]), eb("bks", [P, 1]), eb("bv", [P, D])
                m.cos, m.sin = eb("cos", [P, N]), eb("sin", [P, N])
                loads = [(m.wqT[:, :], a["L1_attn_Wq"]), (m.wkT[:, :], a["L1_attn_Wk"]), (m.wvT[:, :], a["L1_attn_Wv"]),
                         (m.woT[:, :], a["L1_attn_Wo"]), (m.bq[:, :], column(a["L1_attn_bq"])), (m.bk[:, :], column(a["L1_attn_bk"])),
                         (m.bv[:, :], row(a["L1_attn_bv"]).broadcast_to([P, D])), (m.bo[:, :], row(a["L1_attn_bo"]).broadcast_to([P, D]))]
                for dst, src in ((m.bqs, a["L1_attn_bq"]), (m.bks, a["L1_attn_bk"])):
                    for k in range(2):
                        loads.append((dst[k:P:2, :], src.rearrange("(f two) -> two f", two=2)[1 - k].rearrange("(p o) -> p o", o=1)))
                loads += [(m.cos[:, :], cos_t), (m.sin[:, :], sin_t)]
                ln_block(nc, m, "ln2", loads)
                project1_block(nc, m, a)
            attn1_block(nc, m, a)
            output1_block(nc, m, a)
        with ExitStack() as layer:
            def lb(name, shape, dt=F32):
                return layer.enter_context(nc.sbuf_tensor(name, shape, dt))

            m.wg, m.bg, m.alpha = lb("wg", [P, NE]), lb("bg", [1, NE]), lb("alpha", [1, 1])
            ln_block(nc, m, "ln3", [(m.wg[:, :], a["L1_ffn_w_gate"]), (m.bg[:, :], row(a["L1_ffn_b_gate"])),
                                    (m.alpha[:, :], row(a["L1_ffn_alpha"]))])
            experts_block(nc, m, a)
        store_block(nc, m, out)


_INS = ['L0_attn_x', 'L0_attn_wq', 'L0_attn_wk', 'L0_attn_wv', 'L0_attn_wo', 'L0_attn_ws1', 'L0_attn_bs1', 'L0_attn_ws2', 'L0_attn_bs2',
        'L0_ffn_q_proj_w', 'L0_ffn_router_w', 'L0_ffn_aux_keys', 'L0_ffn_aux_values', 'L0_ffn_reliability_mask', 'L0_ffn_unc_w1',
        'L0_ffn_unc_b1', 'L0_ffn_unc_w2', 'L0_ffn_unc_b2', 'L0_ffn_gate_w1', 'L0_ffn_gate_bias', 'L1_attn_Wq', 'L1_attn_bq', 'L1_attn_Wk',
        'L1_attn_bk', 'L1_attn_Wv', 'L1_attn_bv', 'L1_attn_Wo', 'L1_attn_bo', 'L1_ffn_alpha', 'L1_ffn_w_gate', 'L1_ffn_b_gate', 'L1_ffn_W1m',
        'L1_ffn_b1m', 'L1_ffn_W2m', 'L1_ffn_b2m', 'L1_ffn_W1e', 'L1_ffn_b1e', 'L1_ffn_W2e', 'L1_ffn_b2e']
_TURNED = ['L0_ffn_q_proj_w', 'L0_ffn_router_w', 'L0_ffn_aux_keys', 'L0_ffn_unc_w1', 'L0_ffn_unc_w2',
           'L1_attn_Wq', 'L1_attn_Wk', 'L1_attn_Wv', 'L1_attn_Wo']


def kernel(**inputs):
    import numpy as _np
    import concourse.bacc as _bacc
    from concourse import mybir as _mybir
    from concourse.bass_utils import run_bass_kernel_spmd as _run

    nc = _bacc.Bacc("TRN2", target_bir_lowering=False, num_devices=1)
    arrays, args = {}, {}
    for name in _INS:
        x = inputs[name]
        if name in _TURNED:
            x = _np.asarray(x).T
        x = _np.ascontiguousarray(x)
        if x.ndim == 0:
            x = x.reshape(1)
        arrays[f"in_{name}"] = x
        args[name] = nc.dram_tensor(f"in_{name}", x.shape, _mybir.dt.from_np(x.dtype), kind="ExternalInput").ap()
    out = nc.dram_tensor("out_0", (1, N, D), F32, kind="ExternalOutput").ap()
    build(nc, args, out)
    r = _run(nc, [arrays], core_ids=[0])
    return r.results[0]["out_0"]
```

```python
from contextlib import ExitStack

import numpy as np
import concourse.bass as bass
from concourse import mybir

F32 = mybir.dt.float32
BF16 = mybir.dt.bfloat16
U32 = mybir.dt.uint32
ACT = mybir.ActivationFunctionType
ALU = mybir.AluOpType
AX_X = mybir.AxisListType.X

P = 128
N = 2048
D = 128
NT = N // P
BANK = 512
NC = N // BANK
TPB = BANK // P
EPS = 1e-5

H0, HD0, G0 = 16, 64, 32
PAIRS = H0 // 2
WL = P + G0
F32_LOW = -3.4028234663852886e38
MASKED = -1e30

RD, NKEY, UH = 48, 512, 32

H1, HD1 = 16, 8
PARTS = 3
QROWS = PARTS * PARTS * HD1
MROW = QROWS
KROWS = QROWS + PARTS
VCOLS = 32

HID, NE = 512, 8
HT = HID // P
NETS = 3


class Memory:
    pass


def ln_block(nc, m, tag, loads=()):
    with ExitStack() as ctx:
        stats_ready = ctx.enter_context(nc.semaphore(f"{tag}_stats_ready"))
        moments_ready = ctx.enter_context(nc.semaphore(f"{tag}_moments_ready"))
        var_eps_ready = ctx.enter_context(nc.semaphore(f"{tag}_var_eps_ready"))
        std_ready = ctx.enter_context(nc.semaphore(f"{tag}_std_ready"))
        rstd_ready = ctx.enter_context(nc.semaphore(f"{tag}_rstd_ready"))
        xn_ready = ctx.enter_context(nc.semaphore(f"{tag}_xn_ready"))
        turned = ctx.enter_context(nc.semaphore(f"{tag}_turned"))
        loaded = ctx.enter_context(nc.semaphore(f"{tag}_loaded"))
        block = ctx.enter_context(nc.Block())

        @block.sync
        def _(sp):
            for dst, src in loads:
                sp.dma_start(dst, src, allow_slow_non_contiguous=True).then_inc(loaded, 16)
            if loads:
                sp.wait_ge(loaded, 16 * len(loads))

        @block.vector
        def _(dve):
            for t in range(NT):
                nc.vector.bn_stats(m.stats[:, t * 6:t * 6 + 6], m.x[:, t * D:(t + 1) * D]).then_inc(stats_ready, 1)
            dve.wait_ge(stats_ready, NT)
            for t in range(NT):
                nc.vector.bn_aggr(m.moments[:, t * 2:t * 2 + 2], m.stats[:, t * 6:t * 6 + 6]).then_inc(moments_ready, 1)
            dve.wait_ge(moments_ready, NT)
            mv = m.moments[:, :].rearrange("p (t c) -> p t c", c=2)
            nc.vector.tensor_scalar(m.rstd[:, :], mv[:, :, 1], EPS, None, ALU.add).then_inc(var_eps_ready, 1)
            dve.wait_ge(std_ready, 1)
            nc.vector.reciprocal(m.rstd[:, :], m.std[:, :]).then_inc(rstd_ready, 1)
            dve.wait_ge(rstd_ready, 1)
            for t in range(NT):
                nc.vector.tensor_scalar(m.xn[:, t * D:(t + 1) * D], m.x[:, t * D:(t + 1) * D],
                                        mv[:, t, 0:1], m.rstd[:, t:t + 1], ALU.subtract, ALU.mult).then_inc(xn_ready, 1)

        @block.scalar
        def _(act):
            act.wait_ge(var_eps_ready, 1)
            nc.scalar.activation(m.std[:, :], m.rstd[:, :], ACT.Sqrt).then_inc(std_ready, 1)
            for c in range(NC):
                act.wait_ge(turned, c + 1)
                nc.scalar.activation(m.xnT[:, c * BANK:(c + 1) * BANK], m.psum[:, c, :], ACT.Copy)

        @block.tensor
        def _(pe):
            for c in range(NC):
                pe.wait_ge(xn_ready, TPB * (c + 1))
                for i in range(TPB):
                    t = TPB * c + i
                    mm = nc.tensor.transpose(m.psum[:, c, i * P:(i + 1) * P], m.xn[:, t * D:(t + 1) * D], m.ident[:, :])
                mm.then_inc(turned, 1)


def setup_block(nc, m, a):
    with ExitStack() as ctx:
        zeroed = ctx.enter_context(nc.semaphore("zeroed"))
        patterned = ctx.enter_context(nc.semaphore("patterned"))
        loaded = ctx.enter_context(nc.semaphore("loaded"))
        block = ctx.enter_context(nc.Block())

        @block.sync
        def _(sp):
            sp.dma_start(m.x[:, :].rearrange("p (t d) -> p t d", d=D),
                         a["L0_attn_x"][0].rearrange("(t p) d -> p t d", p=P)).then_inc(loaded, 16)
            sp.dma_start(m.ws1[:, :], a["L0_attn_ws1"]).then_inc(loaded, 16)
            sp.dma_start(m.bs1[:, :], a["L0_attn_bs1"].rearrange("(p o) -> p o", o=1)).then_inc(loaded, 16)
            sp.dma_start(m.ws2[:, :], a["L0_attn_ws2"]).then_inc(loaded, 16)
            sp.dma_start(m.bs2[:, :], a["L0_attn_bs2"].rearrange("(o c) -> o c", o=1).broadcast_to([P, 1])).then_inc(loaded, 16)
            sp.wait_ge(loaded, 5 * 16)

        @block.gpsimd
        def _(pool):
            nc.gpsimd.memset(m.ident[:, :], 0.0).then_inc(zeroed, 1)
            nc.gpsimd.memset(m.identb[:, :], 0.0).then_inc(zeroed, 1)
            nc.gpsimd.memset(m.mask[:, :], 0.0).then_inc(zeroed, 1)
            nc.gpsimd.memset(m.ones[:, :], 1.0).then_inc(zeroed, 1)
            pool.wait_ge(zeroed, 4)
            nc.gpsimd.affine_select(out=m.ident[:, :], in_=m.ident[:, :], compare_op=ALU.not_equal, fill=1.0,
                                    base=0, pattern=[[-1, P]], channel_multiplier=1).then_inc(patterned, 1)
            nc.gpsimd.affine_select(out=m.identb[:, :], in_=m.identb[:, :], compare_op=ALU.not_equal, fill=1.0,
                                    base=0, pattern=[[-1, P]], channel_multiplier=1).then_inc(patterned, 1)
            for j in range(2):
                w = m.mask[:, j * WL:j * WL + P]
                nc.gpsimd.affine_select(out=w, in_=w, compare_op=ALU.is_ge, fill=MASKED,
                                        base=0, pattern=[[-1, P]], channel_multiplier=1).then_inc(patterned, 1)


def attn0_block(nc, m, a):
    SCALE = HD0 ** -0.5
    with ExitStack() as ctx:
        def sb(name, shape, dt=F32):
            return ctx.enter_context(nc.sbuf_tensor(name, shape, dt))

        def sem(name):
            return ctx.enter_context(nc.semaphore(name))

        w_cur = sb("w_cur", [P, 2, 3, P])
        wo_cur = sb("wo_cur", [P, 2, D])
        qz = sb("qz", [P, 2, 2, N])
        kx = sb("kx", [P, 2, NT, WL])
        v = sb("v0", [P, 2, NT, P])
        gv = sb("gv", [2 * G0, 2, P])
        gtok = sb("gtok", [P, 2 * G0])
        sm = sb("sm", [P, 4, 2 * WL])
        pr = sb("pr", [P, 4, 2 * WL])
        nmax = sb("nmax", [P, 4, 4])
        total = sb("total", [P, 4, 4])
        rtotal = sb("rtotal", [P, 4, 4])
        pt = sb("pt", [P, 2, 3 * P])
        oT = sb("oT", [P, 4, P])
        ws2r = sb("ws2r", [UH, P])
        gate_h = sb("gate_h", [UH, 1])
        gate_s = sb("gate_s", [P, 1])
        gate_m = sb("gate_m", [P, 1], U32)

        w_loaded = (sem("w_even_loaded"), sem("w_odd_loaded"))
        wo_loaded = (sem("wo_even_loaded"), sem("wo_odd_loaded"))
        zeroed = sem("zeroed0")
        ws2_spread = sem("ws2_spread")
        token_copied = sem("token_copied")
        score_hidden = sem("score_hidden")
        score_gelu = sem("score_gelu")
        score_ready = sem("score_ready")
        score_saved = sem("score_saved")
        low_ready = sem("low_ready")
        gtok_ready = sem("gtok_ready")
        q_ready, q_saved = sem("q_ready"), sem("q_saved")
        k_ready, k_saved = sem("k_ready"), sem("k_saved")
        v_ready, v_saved = sem("v_ready"), sem("v_saved")
        g_ready, g_saved = sem("g_ready"), sem("g_saved")
        scores_ready, masked = sem("scores_ready"), sem("masked")
        max_ready, exp_ready = sem("max_ready"), sem("exp_ready")
        rtotal_ready, probs_ready = sem("rtotal_ready"), sem("probs_ready")
        pt_ready, pt_saved = sem("pt_ready"), sem("pt_saved")
        o_ready, o_saved = sem("o_ready"), sem("o_saved")
        wo_done, y_added = sem("wo_done"), sem("y_added")
        block = ctx.enter_context(nc.Block())

        ROUND = 2 * NT
        LAG = 4
        LAST = PAIRS // 2 - 1

        S_B, T_B, O_B, Y_B, J_B = 0, 2, 4, 6, 7
        gk_ps = m.psum[:, J_B, 0:G0]
        gv_ps = m.psum[0:2 * G0, J_B, P:2 * P]

        def job(i, more):
            k = i % NT - LAG
            if i < 0 or k < 0 or i >= ROUND or (i >= NT and not more):
                return None
            return i // NT + 1, k // 3, "qkv"[k % 3]

        @block.sync
        def _(sp):
            def load_w(pair, b):
                for i, w in enumerate((a["L0_attn_wq"], a["L0_attn_wk"], a["L0_attn_wv"])):
                    sp.dma_start(w_cur[:, b, i, :], w[:, bass.ds(pair * P, P)]).then_inc(w_loaded[b], 16)

            def load_wo(pair, b):
                sp.dma_start(wo_cur[:, b, :], a["L0_attn_wo"][bass.ds(pair * P, P), :]).then_inc(wo_loaded[b], 16)

            for b in range(2):
                load_w(b, b)
                load_wo(b, b)
            with sp.Fori(0, LAST) as r:
                for b in range(2):
                    sp.wait_ge(v_ready, r * 2 * NC + (b + 1) * NC)
                    load_w(r * 2 + (2 + b), b)
                for b in range(2):
                    sp.wait_ge(wo_done, r * ROUND + (b + 1) * NT)
                    load_wo(r * 2 + (2 + b), b)

        @block.tensor
        def _(pe):
            nc.tensor.matmul(m.psum[0:UH, J_B, 0:1], m.ws1[:, :], m.xnT[:, 0:1], start=True, stop=True).then_inc(score_hidden, 1)
            pe.wait_ge(score_gelu, 1)
            pe.wait_ge(ws2_spread, 1)
            nc.tensor.matmul(m.psum[:, Y_B, 0:1], ws2r[:, :], gate_h[:, :], start=True, stop=True).then_inc(score_ready, 1)
            pe.wait_ge(gtok_ready, 1)

            def project_globals(b):
                nc.tensor.matmul(gk_ps, w_cur[:, b, 1, :], gtok[:, 0:G0], start=True, stop=True)
                nc.tensor.matmul(gv_ps, gtok[:, :], w_cur[:, b, 2, :], start=True, stop=True).then_inc(g_ready, 1)

            def project(b, c, what, bank):
                if what == "v":
                    for i in range(TPB):
                        t = TPB * c + i
                        mm = nc.tensor.matmul(m.psum[:, bank, i * P:(i + 1) * P], m.xnT[:, t * P:(t + 1) * P],
                                              w_cur[:, b, 2, :], start=True, stop=True)
                    mm.then_inc(v_ready, 1)
                elif what == "q":
                    nc.tensor.matmul(m.psum[:, bank, :], w_cur[:, b, 0, :], m.xnT[:, c * BANK:(c + 1) * BANK],
                                     start=True, stop=True).then_inc(q_ready, 1)
                else:
                    nc.tensor.matmul(m.psum[:, bank, :], w_cur[:, b, 1, :], m.xnT[:, c * BANK:(c + 1) * BANK],
                                     start=True, stop=True).then_inc(k_ready, 1)

            def step(r, i, more=True):
                if i < ROUND or more:
                    b, s = i // NT % 2, i % NT
                    if s == 0:
                        pe.wait_ge(q_saved, r * 2 * NC + (i // NT + 1) * NC)
                        pe.wait_ge(k_saved, r * 2 * NC + (i // NT + 1) * NC)
                        pe.wait_ge(g_saved, r * 2 + i // NT + 1)
                    if i >= 2:
                        pe.wait_ge(masked, r * ROUND + i - 1)
                    for j in range(2):
                        mm = nc.tensor.matmul(m.psum[:, S_B + i % 2, j * WL:(j + 1) * WL],
                                              qz[:, b, j, s * P:(s + 1) * P], kx[:, b, s, :], start=True, stop=True)
                    mm.then_inc(scores_ready, 1)
                if job(i, more) and job(i, more)[1:] == (0, "q"):
                    q = job(i, more)[0]
                    pe.wait_ge(w_loaded[q % 2], (r + q // 2) * 48 + 48)
                    pe.wait_ge(v_saved, r * 2 * NC + q * NC)
                    project_globals(q % 2)
                w = i - 2
                if 0 <= w < ROUND or (w >= ROUND and more):
                    pe.wait_ge(probs_ready, r * ROUND + w + 1)
                    if w >= 2:
                        pe.wait_ge(pt_saved, r * ROUND + w - 1)
                    for j in range(2):
                        nc.tensor.transpose(m.psum[:, T_B + w % 2, j * P:(j + 1) * P], pr[:, w % 4, j * P:(j + 1) * P],
                                            m.ident[:, :])
                    nc.tensor.transpose(m.psum[0:2 * G0, T_B + w % 2, 2 * P:3 * P], pr[:, w % 4, 2 * P:2 * WL],
                                        m.ident[:, :]).then_inc(pt_ready, 1)
                w = i - 3
                if 0 <= w < ROUND or (w >= ROUND and more):
                    b, s = w // NT % 2, w % NT
                    if s == 0:
                        pe.wait_ge(v_saved, r * 2 * NC + (w // NT + 1) * NC)
                    pe.wait_ge(pt_saved, r * ROUND + w + 1)
                    if w >= 2:
                        pe.wait_ge(o_saved, r * ROUND + w - 1)
                    ob = m.psum[:, O_B + w % 2, 0:P]
                    nc.tensor.matmul(ob, gv[:, b, :], pt[0:2 * G0, w % 2, 2 * P:3 * P], start=True, stop=False)
                    for j in range(2):
                        mm = nc.tensor.matmul(ob[j * HD0:(j + 1) * HD0, :], v[:, b, s, j * HD0:(j + 1) * HD0],
                                              pt[:, w % 2, j * P:(j + 1) * P], start=False, stop=True)
                    mm.then_inc(o_ready, 1)
                w = i - LAG
                if 0 <= w < ROUND:
                    b = w // NT
                    if w % NT == 0:
                        pe.wait_ge(wo_loaded[b], r * 16 + 16)
                    pe.wait_ge(o_saved, r * ROUND + w + 1)
                    if w % TPB == 0:
                        pe.wait_ge(y_added, r * 2 * NC + w // TPB + 1)
                    nc.tensor.matmul(m.psum[:, Y_B, (w % TPB) * P:(w % TPB + 1) * P],
                                     oT[:, w % 4, :], wo_cur[:, b, :], start=True, stop=True).then_inc(wo_done, 1)
                if job(i, more):
                    q, c, what = job(i, more)
                    if what == "q" and c == 0:
                        pe.wait_ge(g_saved, r * 2 + q + 1)
                    elif what == "q":
                        pe.wait_ge(v_saved, r * 2 * NC + q * NC + c)
                    elif what == "k":
                        pe.wait_ge(q_saved, r * 2 * NC + q * NC + c + 1)
                    else:
                        pe.wait_ge(k_saved, r * 2 * NC + q * NC + c + 1)
                    project(q % 2, c, what, J_B)

            pe.wait_ge(w_loaded[0], 48)
            project_globals(0)
            for c in range(NC):
                if c == 0:
                    pe.wait_ge(g_saved, 1)
                else:
                    pe.wait_ge(q_saved, c)
                project(0, c, "q", J_B)
                if c >= 1:
                    pe.wait_ge(k_saved, c)
                project(0, c, "k", Y_B)
                if c >= 1:
                    pe.wait_ge(v_saved, c)
                project(0, c, "v", O_B + 1)
            for i in range(LAG):
                step(0, i)
            with pe.Fori(0, LAST) as r:
                for i in range(LAG, ROUND + LAG):
                    step(r, i)
            for i in range(LAG, ROUND + LAG):
                step(LAST, i, more=False)

        @block.vector
        def _(dve):
            dve.sem_inc(y_added, 1)
            nc.vector.tensor_scalar(ws2r[:, :], m.ones[0:UH, :], m.ws2[:, 0:1], None, ALU.mult).then_inc(ws2_spread, 1)
            nc.vector.tensor_copy(gtok[:, 0:G0], m.xnT[:, 0:G0]).then_inc(token_copied, 1)
            nc.vector.tensor_copy(gtok[:, G0:2 * G0], m.xnT[:, 0:G0]).then_inc(token_copied, 1)
            dve.wait_ge(score_ready, 1)
            nc.vector.tensor_scalar(gate_s[:, :], m.psum[:, Y_B, 0:1], m.bs2[:, 0:1], None, ALU.add).then_inc(score_saved, 1)
            dve.wait_ge(score_saved, 1)
            nc.vector.tensor_scalar(gate_m[:, :], gate_s[:, :], F32_LOW, None, ALU.is_lt).then_inc(low_ready, 1)
            dve.wait_ge(low_ready, 1)
            dve.wait_ge(token_copied, 2)
            for j in range(2):
                nc.vector.copy_predicated(gtok[:, j * G0:j * G0 + 1], gate_m[:, :], m.xnT[:, G0:G0 + 1])\
                    .then_inc(*((gtok_ready, 1) if j else (token_copied, 1)))

            def save_globals(r, q):
                b = q % 2
                dve.wait_ge(g_ready, r * 2 + q + 1)
                nc.vector.tensor_copy(kx[:, b, :, P:WL], gk_ps.rearrange("p (o g) -> p o g", o=1).broadcast_to([P, NT, G0]))
                for j in range(2):
                    mm = nc.vector.tensor_copy(gv[j * G0:(j + 1) * G0, b, j * HD0:(j + 1) * HD0],
                                               gv_ps[j * G0:(j + 1) * G0, j * HD0:(j + 1) * HD0])
                mm.then_inc(g_saved, 1)

            def save_keys(r, q, c, bank):
                dve.wait_ge(k_ready, r * 2 * NC + q * NC + c + 1)
                nc.vector.tensor_copy(kx[:, q % 2, TPB * c:TPB * (c + 1), 0:P],
                                      m.psum[:, bank, :].rearrange("p (t k) -> p t k", t=TPB)).then_inc(k_saved, 1)

            def save_values(r, q, c, bank):
                dve.wait_ge(v_ready, r * 2 * NC + q * NC + c + 1)
                nc.vector.tensor_copy(v[:, q % 2, TPB * c:TPB * (c + 1), :],
                                      m.psum[:, bank, :].rearrange("p (t k) -> p t k", t=TPB)).then_inc(v_saved, 1)

            def step(r, i, more=True):
                if job(i - 1, more):
                    q, c, what = job(i - 1, more)
                    if what == "k":
                        save_keys(r, q, c, J_B)
                    elif what == "v":
                        save_values(r, q, c, J_B)
                if i < ROUND or more:
                    dve.wait_ge(scores_ready, r * ROUND + i + 1)
                    nc.vector.tensor_tensor(sm[:, i % 4, :], m.psum[:, S_B + i % 2, 0:2 * WL], m.mask[:, :],
                                            ALU.add).then_inc(masked, 1)
                    dve.wait_ge(masked, r * ROUND + i + 1)
                    smw = sm[:, i % 4, :].rearrange("p (j c) -> p j c", j=2)
                    nc.vector.tensor_reduce(nmax[:, i % 4, 0:2], smw[:, :, 0:P], AX_X, ALU.max, negate=True)
                    nc.vector.tensor_reduce(nmax[:, i % 4, 2:4], smw[:, :, P:WL], AX_X, ALU.max,
                                            negate=True).then_inc(max_ready, 1)
                if job(i, more) and job(i, more)[1:] == (0, "q"):
                    save_globals(r, job(i, more)[0])
                w = i - 1
                if 0 <= w < ROUND or (w >= ROUND and more):
                    dve.wait_ge(exp_ready, r * ROUND + w + 1)
                    nc.vector.reciprocal(rtotal[:, w % 4, :], total[:, w % 4, :]).then_inc(rtotal_ready, 1)
                w = i - 2
                if 0 <= w < ROUND or (w >= ROUND and more):
                    dve.wait_ge(pt_ready, r * ROUND + w + 1)
                    if w >= 2:
                        dve.wait_ge(o_ready, r * ROUND + w - 1)
                    nc.vector.tensor_copy(pt[:, w % 2, 0:2 * P], m.psum[:, T_B + w % 2, 0:2 * P])
                    nc.vector.tensor_copy(pt[0:2 * G0, w % 2, 2 * P:3 * P],
                                          m.psum[0:2 * G0, T_B + w % 2, 2 * P:3 * P]).then_inc(pt_saved, 1)
                if i % TPB == TPB - 1 and i > LAG:
                    g = i // TPB - 1
                    dve.wait_ge(wo_done, r * ROUND + TPB * (g + 1))
                    dve.wait_ge(y_added, r * 2 * NC + g + 1)
                    xg = m.x[:, g % NC * BANK:(g % NC + 1) * BANK]
                    nc.vector.tensor_tensor(xg, xg, m.psum[:, Y_B, :], ALU.add).then_inc(y_added, 1)

            dve.wait_ge(zeroed, 5)
            save_globals(0, 0)
            for c in range(NC):
                save_keys(0, 0, c, Y_B)
                save_values(0, 0, c, O_B + 1)
            for i in range(LAG):
                step(0, i)
            with dve.Fori(0, LAST) as r:
                for i in range(LAG, ROUND + LAG):
                    step(r, i)
            for i in range(LAG, ROUND + LAG):
                step(LAST, i, more=False)

        @block.scalar
        def _(act):
            act.wait_ge(score_hidden, 1)
            nc.scalar.activation(gate_h[:, :], m.psum[0:UH, J_B, 0:1], ACT.Gelu, bias=m.bs1[:, 0:1]).then_inc(score_gelu, 1)

            def save_queries(r, q, c):
                act.wait_ge(q_ready, r * 2 * NC + q * NC + c + 1)
                for j in range(2):
                    h = slice(j * HD0, (j + 1) * HD0)
                    mm = nc.scalar.activation(qz[h, q % 2, j, c * BANK:(c + 1) * BANK], m.psum[h, J_B, :],
                                              ACT.Copy, scale=SCALE)
                mm.then_inc(q_saved, 1)

            def step(r, i, more=True):
                if job(i - 1, more) and job(i - 1, more)[2] == "q":
                    save_queries(r, job(i - 1, more)[0], job(i - 1, more)[1])
                if i < ROUND or more:
                    act.wait_ge(max_ready, r * ROUND + i + 1)
                    if i >= 4:
                        act.wait_ge(pt_ready, r * ROUND + i - 3)
                    for j in range(2):
                        nc.scalar.activation(pr[:, i % 4, j * P:(j + 1) * P], sm[:, i % 4, j * WL:j * WL + P], ACT.Exp,
                                             bias=nmax[:, i % 4, j:j + 1], accum_out=total[:, i % 4, j:j + 1])
                        mm = nc.scalar.activation(pr[:, i % 4, 2 * P + j * G0:2 * P + (j + 1) * G0],
                                                  sm[:, i % 4, j * WL + P:(j + 1) * WL], ACT.Exp,
                                                  bias=nmax[:, i % 4, 2 + j:3 + j], accum_out=total[:, i % 4, 2 + j:3 + j])
                    mm.then_inc(exp_ready, 1)
                w = i - 3
                if 0 <= w < ROUND or (w >= ROUND and more):
                    act.wait_ge(o_ready, r * ROUND + w + 1)
                    nc.scalar.activation(oT[:, w % 4, :], m.psum[:, O_B + w % 2, 0:P], ACT.Copy).then_inc(o_saved, 1)

            act.wait_ge(zeroed, 5)
            for c in range(NC):
                save_queries(0, 0, c)
            for i in range(LAG):
                step(0, i)
            with act.Fori(0, LAST) as r:
                for i in range(LAG, ROUND + LAG):
                    step(r, i)
            for i in range(LAG, ROUND + LAG):
                step(LAST, i, more=False)

        @block.gpsimd
        def _(pool):
            for b in range(2):
                nc.gpsimd.memset(qz[HD0:P, b, 0, :], 0.0).then_inc(zeroed, 1)
                nc.gpsimd.memset(qz[0:HD0, b, 1, :], 0.0).then_inc(zeroed, 1)
            nc.gpsimd.memset(gv[:, :, :], 0.0).then_inc(zeroed, 1)
            with pool.Fori(0, PAIRS) as p:
                for w in range(NT):
                    pool.wait_ge(rtotal_ready, p * NT + w + 1)
                    for cols, r in ((slice(0, 2 * P), slice(0, 2)), (slice(2 * P, 2 * WL), slice(2, 4))):
                        prw = pr[:, w % 4, cols].rearrange("p (j c) -> p j c", j=2)
                        rb = rtotal[:, w % 4, r].rearrange("p (j o) -> p j o", o=1).broadcast_to(list(prw.shape))
                        mm = nc.gpsimd.tensor_tensor(prw, prw, rb, ALU.mult)
                    mm.then_inc(probs_ready, 1)


def memory_block(nc, m, a):
    REPLACED = -3e38
    with ExitStack() as ctx:
        def sb(name, shape, dt=F32):
            return ctx.enter_context(nc.sbuf_tensor(name, shape, dt))

        def sem(name):
            return ctx.enter_context(nc.semaphore(name))

        qyT = sb("qyT", [P, N])
        rqT = sb("rqT", [P, N])
        rkT = sb("rkT", [P, NKEY])
        h1T = sb("h1T", [UH, N])
        logvar = sb("logvar", [P, NT])
        logvar_sum = sb("logvar_sum", [P, 1])
        learned = sb("learned", [P, NT])
        gate = sb("gate", [P, NT])
        norm = sb("norm", [P, 1])
        sc = sb("sc", [P, 3, NKEY])
        sr = sb("sr", [P, NKEY])
        ex = sb("ex", [P, 2, NKEY])
        wt = sb("wt", [P, 2, NKEY])
        wT = sb("wT", [P, 2, NKEY])
        best = sb("best", [P, NT, 8])
        nbest = sb("nbest", [P, NT])
        wsum = sb("wsum", [P, NT])
        coef = sb("coef", [P, NT])

        zeroed = sem("zeroed1")
        qy_ready, qy_saved = sem("qy_ready"), sem("qy_saved")
        rq_ready, rq_saved = sem("rq_ready"), sem("rq_saved")
        h1_ready, h1_saved = sem("h1_ready"), sem("h1_saved")
        learned_ready, logvar_ready, total_ready = sem("learned_ready"), sem("logvar_ready"), sem("total_ready")
        sigmoid_ready, gate_step, gate_ready = sem("sigmoid_ready"), sem("gate_step"), sem("gate_ready")
        stats_ready, var_ready, x_added = sem("m_stats_ready"), sem("m_var_ready"), sem("x_added")
        sc_ready, sc_saved = sem("sc_ready"), sem("sc_saved")
        best_ready, nbest_ready, ex_ready, replaced = sem("best_ready"), sem("nbest_ready"), sem("ex_ready"), sem("replaced")
        wt_ready, wT_ready, wT_saved = sem("wt_ready"), sem("wT_ready"), sem("wT_saved")
        agg_ready, wsum_ready, coef_ready, y_added = sem("agg_ready"), sem("wsum_ready"), sem("coef_ready"), sem("m_y_added")
        block = ctx.enter_context(nc.Block())
        mv = m.moments[:, :].rearrange("p (t c) -> p t c", c=2)

        @block.tensor
        def _(pe):
            for c in range(NC):
                nc.tensor.matmul(m.psum[:, c, :], m.qpT[:, :], m.xnT[:, c * BANK:(c + 1) * BANK],
                                 start=True, stop=True).then_inc(qy_ready, 1)
            for c in range(NC):
                nc.tensor.matmul(m.psum[0:UH, 4 + c, :], m.uw1T[:, :], m.xnT[:, c * BANK:(c + 1) * BANK],
                                 start=True, stop=True).then_inc(h1_ready, 1)
            for c in range(NC):
                pe.wait_ge(qy_saved, c + 1)
                nc.tensor.matmul(m.psum[0:RD, c, :], m.rwT[:, :], qyT[:, c * BANK:(c + 1) * BANK],
                                 start=True, stop=True).then_inc(rq_ready, 1)
            pe.wait_ge(h1_saved, NC)
            nc.tensor.matmul(m.psum[0:RD, 4, :], m.rwT[:, :], m.akT[:, :],
                             start=True, stop=True).then_inc(rq_ready, 1)
            for t in range(NT):
                mm = nc.tensor.matmul(m.psum[:, 5, t:t + 1], h1T[:, t * P:(t + 1) * P], m.uw2T[:, :], start=True, stop=True)
            mm.then_inc(learned_ready, 1)
            pe.wait_ge(logvar_ready, 1)
            nc.tensor.matmul(m.psum[:, 6, 0:1], m.ones[:, :], logvar_sum[:, :], start=True, stop=True).then_inc(total_ready, 1)
            pe.wait_ge(rq_saved, NC + 1)
            for s in range(NT + 3):
                if s < NT:
                    if s >= 2:
                        pe.wait_ge(sc_saved, s - 1)
                    nc.tensor.matmul(m.psum[:, s % 2, :], rqT[:, s * P:(s + 1) * P], rkT[:, :],
                                     start=True, stop=True).then_inc(sc_ready, 1)
                t = s - 2
                if 0 <= t < NT:
                    pe.wait_ge(wt_ready, t + 1)
                    if t >= 2:
                        pe.wait_ge(wT_saved, t - 1)
                    for i in range(NKEY // P):
                        mm = nc.tensor.transpose(m.psum[:, 2 + t % 2, i * P:(i + 1) * P], wt[:, t % 2, i * P:(i + 1) * P],
                                                 m.ident[:, :])
                    mm.then_inc(wT_ready, 1)
                t = s - 3
                if 0 <= t < NT:
                    pe.wait_ge(wT_saved, t + 1)
                    if t == 0:
                        pe.wait_ge(gate_step, 1)
                    if t >= 2:
                        pe.wait_ge(y_added, t - 1)
                    for i in range(NKEY // P):
                        mm = nc.tensor.matmul(m.psum[:, 6 + t % 2, 0:D], wT[:, t % 2, i * P:(i + 1) * P],
                                              m.av[:, i * D:(i + 1) * D], start=(i == 0), stop=(i == NKEY // P - 1))
                    mm.then_inc(agg_ready, 1)

        @block.gpsimd
        def _(pool):
            nc.gpsimd.memset(rqT[:, :], 0.0).then_inc(zeroed, 1)
            nc.gpsimd.memset(rkT[:, :], 0.0).then_inc(zeroed, 1)
            nc.gpsimd.tensor_tensor(m.x[:, :], m.x[:, :], m.xn[:, :], ALU.add).then_inc(x_added, 1)

        @block.vector
        def _(dve):
            for t in range(NT):
                nc.vector.bn_stats(m.stats[:, t * 6:t * 6 + 6], m.xn[:, t * D:(t + 1) * D]).then_inc(stats_ready, 1)
            dve.wait_ge(stats_ready, NT)
            for t in range(NT):
                nc.vector.bn_aggr(m.moments[:, t * 2:t * 2 + 2], m.stats[:, t * 6:t * 6 + 6]).then_inc(var_ready, 1)
            dve.wait_ge(zeroed, 2)
            for c in range(NC + 1):
                dve.wait_ge(rq_ready, c + 1)
                dst = rqT[0:RD, c * BANK:(c + 1) * BANK] if c < NC else rkT[0:RD, :]
                nc.vector.tensor_copy(dst, m.psum[0:RD, c, :]).then_inc(rq_saved, 1)

            def gates():
                dve.wait_ge(total_ready, 1)
                nc.vector.tensor_scalar(norm[:, :], m.psum[:, 6, 0:1], 1.0 / N, 1e-6, ALU.mult, ALU.add).then_inc(gate_step, 1)
                dve.wait_ge(gate_step, 1)
                nc.vector.reciprocal(norm[:, :], norm[:, :]).then_inc(gate_step, 1)
                dve.wait_ge(gate_step, 2)
                nc.vector.tensor_scalar(logvar[:, :], logvar[:, :], norm[:, 0:1], 0.5, ALU.mult, ALU.mult).then_inc(gate_step, 1)
                dve.wait_ge(sigmoid_ready, 1)
                dve.wait_ge(gate_step, 3)
                nc.vector.scalar_tensor_tensor(gate[:, :], learned[:, :], 2.5, logvar[:, :], ALU.mult, ALU.add).then_inc(gate_step, 1)
                dve.wait_ge(gate_step, 4)
                nc.vector.tensor_scalar(gate[:, :], gate[:, :], 0.0, 5.0, ALU.max, ALU.min).then_inc(gate_step, 1)

            for s in range(NT + 4):
                if s < NT:
                    dve.wait_ge(sc_ready, s + 1)
                    if s >= 3:
                        dve.wait_ge(ex_ready, s - 2)
                    nc.vector.scalar_tensor_tensor(sc[:, s % 3, :], m.psum[:, s % 2, :], RD ** -0.5, m.rel[:, :],
                                                   ALU.mult, ALU.add).then_inc(sc_saved, 1)
                    dve.wait_ge(sc_saved, s + 1)
                    nc.vector.max(best[:, s, :], sc[:, s % 3, :]).then_inc(best_ready, 1)
                    dve.wait_ge(best_ready, s + 1)
                    nc.vector.tensor_scalar(nbest[:, s:s + 1], best[:, s, 0:1], -1.0, None, ALU.mult).then_inc(nbest_ready, 1)
                    if s >= 1:
                        dve.wait_ge(wt_ready, s)
                    nc.vector.match_replace(sr[:, :], best[:, s, :], sc[:, s % 3, :], REPLACED).then_inc(replaced, 1)
                    dve.wait_ge(replaced, s + 1)
                    dve.wait_ge(ex_ready, s + 1)
                    if s >= 2:
                        dve.wait_ge(wT_ready, s - 1)
                    nc.vector.scalar_tensor_tensor(wt[:, s % 2, :], sr[:, :], REPLACED, ex[:, s % 2, :], ALU.is_equal, ALU.mult,
                                                   accum_out=wsum[:, s:s + 1]).then_inc(wt_ready, 1)
                if s == 0:
                    gates()
                t = s - 4
                if 0 <= t < NT:
                    if t == 0:
                        dve.wait_ge(gate_ready, 1)
                    dve.wait_ge(wt_ready, t + 1)
                    nc.vector.reciprocal(coef[:, t:t + 1], wsum[:, t:t + 1]).then_inc(wsum_ready, 1)
                    dve.wait_ge(wsum_ready, t + 1)
                    nc.vector.tensor_scalar(coef[:, t:t + 1], coef[:, t:t + 1], gate[:, t:t + 1], None, ALU.mult).then_inc(coef_ready, 1)
                    dve.wait_ge(coef_ready, t + 1)
                    dve.wait_ge(agg_ready, t + 1)
                    dve.wait_ge(x_added, 1)
                    xt = m.x[:, t * D:(t + 1) * D]
                    nc.vector.scalar_tensor_tensor(xt, m.psum[:, 6 + t % 2, 0:D], coef[:, t:t + 1], xt,
                                                   ALU.mult, ALU.add).then_inc(y_added, 1)

        @block.scalar
        def _(act):
            for c in range(NC):
                act.wait_ge(qy_ready, c + 1)
                nc.scalar.activation(qyT[:, c * BANK:(c + 1) * BANK], m.psum[:, c, :], ACT.Copy).then_inc(qy_saved, 1)
            for c in range(NC):
                act.wait_ge(h1_ready, c + 1)
                nc.scalar.activation(h1T[:, c * BANK:(c + 1) * BANK], m.psum[0:UH, 4 + c, :], ACT.Gelu,
                                     bias=m.ub1[:, 0:1]).then_inc(h1_saved, 1)
            act.wait_ge(var_ready, NT)
            nc.scalar.activation(logvar[:, :], mv[:, :, 1], ACT.Ln, bias=m.ones[:, 0:1], accum_out=logvar_sum[:, :])\
                .then_inc(logvar_ready, 1)
            act.wait_ge(learned_ready, 1)
            nc.scalar.activation(learned[:, :], m.psum[:, 5, 0:NT], ACT.Sigmoid, bias=m.ub2[:, 0:1]).then_inc(sigmoid_ready, 1)
            for s in range(NT + 1):
                if s < NT:
                    act.wait_ge(nbest_ready, s + 1)
                    if s >= 2:
                        act.wait_ge(wt_ready, s - 1)
                    nc.scalar.activation(ex[:, s % 2, :], sc[:, s % 3, :], ACT.Exp, bias=nbest[:, s:s + 1]).then_inc(ex_ready, 1)
                if s == 0:
                    act.wait_ge(gate_step, 5)
                    nc.scalar.activation(gate[:, :], gate[:, :], ACT.Sigmoid, scale=m.gw[:, 0:1], bias=m.gb[:, 0:1])\
                        .then_inc(gate_ready, 1)
                t = s - 1
                if 0 <= t < NT:
                    act.wait_ge(wT_ready, t + 1)
                    if t >= 2:
                        act.wait_ge(agg_ready, t - 1)
                    nc.scalar.activation(wT[:, t % 2, :], m.psum[:, 2 + t % 2, :], ACT.Copy).then_inc(wT_saved, 1)


def project1_block(nc, m, a):
    with ExitStack() as ctx:
        def sb(name, shape, dt=F32):
            return ctx.enter_context(nc.sbuf_tensor(name, shape, dt))

        def sem(name):
            return ctx.enter_context(nc.semaphore(name))

        wsw = sb("wsw", [P, 2, P])
        direct = sb("direct", [P, 2, BANK])
        partner = sb("partner", [P, 2, BANK])
        rot = sb("rot", [P, 2, BANK])
        rest = sb("rest", [P, 2, BANK])
        parts = sb("parts", [P, 2, PARTS, N], BF16)

        swapped = sem("swapped")
        qk_ready, partner_ready = sem("qk_ready"), sem("partner_ready")
        rot_ready, part1, rest_ready, part2, part3 = sem("rot_ready"), sem("part1"), sem("rest_ready"), sem("part2"), sem("part3")
        v_ready, v_saved = sem("v1_ready"), sem("v1_saved")
        stored = sem("parts_stored")
        block = ctx.enter_context(nc.Block())
        weights, biases, biases_sw = (m.wqT, m.wkT), (m.bq, m.bk), (m.bqs, m.bks)

        JOBS = 2 * NC

        @block.tensor
        def _(pe):
            pe.wait_ge(swapped, 4)
            for u in range(JOBS):
                i, c = u // NC, u % NC
                if u >= 3:
                    pe.wait_ge(partner_ready, u - 2)
                rhs = m.xnT[:, c * BANK:(c + 1) * BANK]
                nc.tensor.matmul(m.psum[:, 2 * (u % 3), :], weights[i][:, :], rhs, start=True, stop=True)
                nc.tensor.matmul(m.psum[:, 2 * (u % 3) + 1, :], wsw[:, i, :], rhs, start=True, stop=True).then_inc(qk_ready, 1)
            for c in range(NC):
                if c >= 2:
                    pe.wait_ge(v_saved, c - 1)
                for i in range(TPB):
                    t = c * TPB + i
                    mm = nc.tensor.matmul(m.psum[:, 6 + c % 2, i * P:(i + 1) * P], m.xnT[:, t * P:(t + 1) * P], m.wvT[:, :],
                                          start=True, stop=True)
                mm.then_inc(v_ready, 1)

        @block.vector
        def _(dve):
            for i in range(2):
                src = weights[i][:, :].rearrange("p (f two) -> p f two", two=2)
                dst = wsw[:, i, :].rearrange("p (f two) -> p f two", two=2)
                for k in range(2):
                    nc.vector.tensor_copy(dst[:, :, k], src[:, :, 1 - k]).then_inc(swapped, 1)
            for s in range(JOBS + 1):
                if s < JOBS:
                    u, i, c = s, s // NC, s % NC
                    dve.wait_ge(qk_ready, u + 1)
                    if u >= 2:
                        dve.wait_ge(rot_ready, u - 1)
                    cols = slice(c * BANK, (c + 1) * BANK)
                    nc.vector.scalar_tensor_tensor(direct[:, u % 2, :], m.psum[:, 2 * (u % 3), :], biases[i][:, 0:1],
                                                   m.cos[:, cols], ALU.add, ALU.mult)
                    nc.vector.scalar_tensor_tensor(partner[:, u % 2, :], m.psum[:, 2 * (u % 3) + 1, :], biases_sw[i][:, 0:1],
                                                   m.sin[:, cols], ALU.add, ALU.mult).then_inc(partner_ready, 1)
                u = s - 1
                if u >= 0:
                    i, c = u // NC, u % NC
                    dve.wait_ge(rot_ready, u + 1)
                    dve.wait_ge(part1, u + 1)
                    if u >= 2:
                        dve.wait_ge(part3, u - 1)
                    nc.vector.tensor_tensor(rest[:, u % 2, :], rot[:, u % 2, :], parts[:, i, 0, c * BANK:(c + 1) * BANK],
                                            ALU.subtract).then_inc(rest_ready, 1)
            bv = m.bv[:, :].rearrange("p (o d) -> p o d", o=1).broadcast_to([P, TPB, D])
            for c in range(NC):
                dve.wait_ge(v_ready, c + 1)
                nc.vector.tensor_tensor(m.v1[:, c * TPB:(c + 1) * TPB, :],
                                        m.psum[:, 6 + c % 2, :].rearrange("p (t d) -> p t d", d=D), bv, ALU.add).then_inc(v_saved, 1)

        @block.gpsimd
        def _(pool):
            for s in range(JOBS + 1):
                if s < JOBS:
                    pool.wait_ge(partner_ready, s + 1)
                    if s >= 2:
                        pool.wait_ge(rest_ready, s - 1)
                    nc.gpsimd.tensor_tensor(rot[:, s % 2, :], direct[:, s % 2, :], partner[:, s % 2, :], ALU.add).then_inc(rot_ready, 1)
                u = s - 1
                if u >= 0:
                    i, c = u // NC, u % NC
                    pool.wait_ge(part2, u + 1)
                    cols = slice(c * BANK, (c + 1) * BANK)
                    nc.gpsimd.tensor_tensor(parts[:, i, 2, cols], rest[:, u % 2, :], parts[:, i, 1, cols], ALU.subtract).then_inc(part3, 1)

        @block.scalar
        def _(act):
            for s in range(JOBS + 1):
                if s < JOBS:
                    i, c = s // NC, s % NC
                    act.wait_ge(rot_ready, s + 1)
                    nc.scalar.activation(parts[:, i, 0, c * BANK:(c + 1) * BANK], rot[:, s % 2, :], ACT.Copy).then_inc(part1, 1)
                u = s - 1
                if u >= 0:
                    i, c = u // NC, u % NC
                    act.wait_ge(rest_ready, u + 1)
                    nc.scalar.activation(parts[:, i, 1, c * BANK:(c + 1) * BANK], rest[:, u % 2, :], ACT.Copy).then_inc(part2, 1)

        @block.sync
        def _(sp):
            for i, scratch in enumerate((m.q_parts, m.k_parts)):
                sp.wait_ge(part3, NC * (i + 1))
                sp.dma_start(scratch.rearrange("s r n -> r s n"), parts[:, i, :, :]).then_inc(stored, 16)
            sp.wait_ge(stored, 32)


def attn1_block(nc, m, a):
    SCALE = HD1 ** -0.5
    HALF = 2 * BANK
    NB = 3
    with ExitStack() as ctx:
        def sb(name, shape, dt=F32):
            return ctx.enter_context(nc.sbuf_tensor(name, shape, dt))

        def sem(name):
            return ctx.enter_context(nc.semaphore(name))

        qf = sb("qf", [KROWS, NB, N], BF16)
        kf = sb("kf", [KROWS, NB, N], BF16)
        vx = sb("vx", [P, NB, NT, VCOLS])
        pb = sb("pb", [P, 2, NC, BANK])
        rowmax = sb("rowmax", [P, NT, 2])
        nmax = sb("nmax1", [P, NT])
        nrest = sb("nrest", [P, NT])
        nparts = sb("nparts", [P, P // NT, NT], BF16)
        nT = sb("nT", [PARTS * NT, P], BF16)
        acc = sb("acc", [P, BANK])
        rsum = sb("rsum", [P, NT])

        loaded = [sem(f"qk_loaded{b}") for b in range(NB)]
        ones_loaded = sem("ones_loaded")
        nparts_zeroed = sem("nparts_zeroed")
        vx_zeroed, vx_ready = sem("vx_zeroed"), sem("vx_ready")
        rows_ready, rows_reduced = sem("rows_ready"), sem("rows_reduced")
        nmax_ready, npart1, nrest1, npart2, npart3 = sem("nmax_ready"), sem("npart1"), sem("nrest1"), sem("npart2"), sem("npart3")
        nT_ready, nT_saved, max_rows_loaded = sem("nT_ready"), sem("nT_saved"), sem("max_rows_loaded")
        st_ready, exp_ready, av_done = sem("st_ready"), sem("exp1_ready"), sem("av_done")
        acc_saved, accT_ready, rsum_ready, att_ready = sem("acc_saved"), sem("accT_ready"), sem("rsum_ready"), sem("att_ready")
        block = ctx.enter_context(nc.Block())

        START = 2

        def start_counts(eng, *sems):
            for s in sems:
                eng.sem_inc(s, START)

        M_B, E_B, A_B, T_B = 0, 4, 6, 7
        UNITS = NT * NC
        HALVES = 2 * NT
        ROUNDS = H1 // NB - 1
        LEAD = 12
        LOAD = 16 * 2 * PARTS * PARTS

        @block.sync
        def _(sp):
            for b in range(NB):
                sp.dma_start(kf[QROWS:KROWS, b, :], m.ones_rows).then_inc(ones_loaded, 16)

            def load(h, b):
                for j in range(PARTS):
                    r = slice(j * PARTS * HD1, (j + 1) * PARTS * HD1)
                    for i in range(PARTS):
                        r = slice((j * PARTS + i) * HD1, (j * PARTS + i + 1) * HD1)
                        sp.dma_start(qf[r, b, :], m.q_parts[i, bass.ds(h * HD1, HD1), :]).then_inc(loaded[b], 16)
                        sp.dma_start(kf[r, b, :], m.k_parts[j, bass.ds(h * HD1, HD1), :]).then_inc(loaded[b], 16)

            def max_rows(g, b):
                sp.wait_ge(nT_saved, START + g + 1)
                for i in range(PARTS):
                    sp.dma_start(qf[QROWS + i:QROWS + i + 1, b, :], nT[i * NT:(i + 1) * NT, :]).then_inc(max_rows_loaded, 16)

            for b in range(NB):
                load(b, b)
            max_rows(0, 0)
            with sp.Fori(0, ROUNDS) as r:
                for b in range(NB):
                    max_rows(r * NB + b + 1, (b + 1) % NB)
                    sp.wait_ge(av_done, START + (r * NB + b + 1) * NT)
                    load(r * NB + b + NB, b)
            for h in range(H1 - 1 - NB, H1 - 1):
                max_rows(h + 1, (h + 1) % NB)
                if h == H1 - 1 - NB:
                    sp.wait_ge(av_done, START + (h + 1) * NT)
                    load(h + NB, h % NB)

        @block.tensor
        def _(pe):
            start_counts(pe, rows_ready, nT_ready, st_ready, av_done, accT_ready)

            def rows(g, b, n):
                t, c, u = n // NC, n % NC, n // 2
                if n % 2 == 0:
                    pe.wait_ge(rows_reduced, START + g * HALVES + u - 1)
                mm = nc.tensor.matmul(m.psum[:, M_B + (u % 2) * 2 + n % 2, :], qf[0:QROWS, b, t * P:(t + 1) * P],
                                      kf[0:QROWS, b, c * BANK:(c + 1) * BANK], start=True, stop=True)
                if n % 2:
                    mm.then_inc(rows_ready, 1)

            def turn_max(g):
                pe.wait_ge(npart3, START + g + 1)
                pe.wait_ge(att_ready, START + g - 1)
                nc.tensor.transpose(m.psum[:, T_B, 0:P // 2].bitcast(BF16),
                                    nparts[:, :, :].rearrange("p a t -> p (a t)"), m.identb[:, :]).then_inc(nT_ready, 1)

            def turn_sums(h, last):
                pe.wait_ge(acc_saved, START + h + 1)
                pe.wait_ge(nT_saved, START + h + (1 if last else 2))
                for i in range(NC):
                    mm = nc.tensor.transpose(m.psum[:, T_B, i * P:(i + 1) * P], acc[:, i * P:(i + 1) * P], m.ident[:, :])
                mm.then_inc(accT_ready, 1)

            def weigh(h, b, t):
                pe.wait_ge(exp_ready, START + h * UNITS + (t + 1) * NC)
                if t == 0:
                    pe.wait_ge(acc_saved, START + h)
                    pe.wait_ge(vx_ready, START + h + 1)
                for c in range(NC):
                    mm = nc.tensor.matmul(m.psum[c * VCOLS:(c + 1) * VCOLS, A_B, :], vx[:, b, t, :], pb[:, t % 2, c, :],
                                          start=(t == 0), stop=(t == NT - 1))
                mm.then_inc(av_done, 1)

            def head(r, b):
                h = r * NB + b
                left = H1 - 1 - h if isinstance(h, int) else NB
                pe.wait_ge(max_rows_loaded, h * 16 * PARTS + 16 * PARTS)
                n = LEAD
                for t in range(NT + 1):
                    if n == UNITS and left >= 2:
                        b2 = b + 2
                        pe.wait_ge(loaded[b2 % NB], r * LOAD + (1 + b2 // NB) * LOAD)
                    for c, beside in enumerate((1, 2, 1, 0)):
                        if t == NT:
                            break
                        k = t * NC + c
                        pe.wait_ge(exp_ready, START + h * UNITS + k - 1)
                        nc.tensor.matmul(m.psum[:, E_B + k % 2, :], kf[:, b, t * P:(t + 1) * P],
                                         qf[:, b, c * BANK:(c + 1) * BANK], start=True, stop=True).then_inc(st_ready, 1)
                        for _ in range(beside):
                            if n < UNITS and left >= 1:
                                rows(h + 1, (b + 1) % NB, n)
                            elif n >= UNITS and left >= 2:
                                rows(h + 2, (b + 2) % NB, n - UNITS)
                            n += 1
                    if t >= 1:
                        weigh(h, b, t - 1)
                    if t == NT - 2 and left >= 1:
                        turn_max(h + 1)
                turn_sums(h, left == 0)

            pe.wait_ge(ones_loaded, 16 * NB)
            pe.wait_ge(loaded[0], LOAD)
            for n in range(UNITS):
                rows(0, 0, n)
            pe.wait_ge(loaded[1], LOAD)
            for n in range(LEAD):
                if n == 4:
                    turn_max(0)
                rows(1, 1, n)
            with pe.Fori(0, ROUNDS) as r:
                for b in range(NB):
                    head(r, b)
            for h in range(ROUNDS * NB, H1):
                head(h // NB, h % NB)

        @block.vector
        def _(dve):
            start_counts(dve, rows_reduced, nmax_ready, npart1, nrest1, npart2, npart3, nT_saved, acc_saved, rsum_ready, att_ready)

            def reduce_rows(g, first, end):
                for u in range(first, end):
                    dve.wait_ge(rows_ready, START + g * HALVES + u + 1)
                    nc.vector.tensor_reduce(rowmax[:, u // 2, u % 2:u % 2 + 1],
                                            m.psum[:, M_B + (u % 2) * 2:M_B + (u % 2) * 2 + 2, :].rearrange("p b c -> p (b c)"),
                                            AX_X, ALU.max).then_inc(rows_reduced, 1)

            def split_maxima(g):
                dve.wait_ge(rows_reduced, START + (g + 1) * HALVES)
                nc.vector.tensor_reduce(nmax[:, :], rowmax[:, :, :], AX_X, ALU.max, negate=True).then_inc(nmax_ready, 1)
                dve.wait_ge(nmax_ready, START + g + 1)
                nc.vector.tensor_copy(nparts[:, 0, :], nmax[:, :]).then_inc(npart1, 1)
                dve.wait_ge(npart1, START + g + 1)
                nc.vector.tensor_tensor(nrest[:, :], nmax[:, :], nparts[:, 0, :], ALU.subtract).then_inc(nrest1, 1)
                dve.wait_ge(nrest1, START + g + 1)
                nc.vector.tensor_copy(nparts[:, 1, :], nrest[:, :]).then_inc(npart2, 1)
                dve.wait_ge(npart2, START + g + 1)
                nc.vector.tensor_tensor(nparts[:, 2, :], nrest[:, :], nparts[:, 1, :], ALU.subtract).then_inc(npart3, 1)

            def save_turned(g):
                if not (isinstance(g, int) and g == 0):
                    dve.wait_ge(max_rows_loaded, g * 16 * PARTS)
                dve.wait_ge(nT_ready, START + g + 1)
                nc.vector.tensor_copy(nT[:, :], m.psum[0:PARTS * NT, T_B, 0:P // 2].bitcast(BF16)).then_inc(nT_saved, 1)

            def sums(h):
                dve.wait_ge(av_done, START + (h + 1) * NT)
                dve.wait_ge(accT_ready, START + h)
                nc.vector.tensor_copy(acc[:, :], m.psum[:, A_B, :]).then_inc(acc_saved, 1)
                dve.wait_ge(accT_ready, START + h + 1)
                turned = m.psum[:, T_B, :].rearrange("p (i j c) -> p i j c", i=TPB, j=NC)
                nc.vector.reciprocal(rsum[:, :].rearrange("p (i j) -> p i j", i=TPB), turned[:, :, :, HD1]).then_inc(rsum_ready, 1)
                dve.wait_ge(rsum_ready, START + h + 1)
                rb = rsum[:, :].rearrange("p (i j o) -> p i j o", i=TPB, o=1).broadcast_to([P, TPB, NC, HD1])
                dst = m.att[:, :, bass.ds(h * HD1, HD1)].rearrange("p (j i) d -> p i j d", i=TPB)
                nc.vector.tensor_tensor(dst, turned[:, :, :, 0:HD1], rb, ALU.mult).then_inc(att_ready, 1)

            nc.vector.memset(nparts[:, :, :], 0.0).then_inc(nparts_zeroed, 1)
            dve.wait_ge(nparts_zeroed, 1)

            def maxima(g, more):
                split_maxima(g)
                if more:
                    reduce_rows(g + 1, 0, 2)
                save_turned(g)
                if more:
                    reduce_rows(g + 1, 2, LEAD // 2)

            reduce_rows(0, 0, HALVES)
            maxima(0, True)
            with dve.Fori(0, ROUNDS) as r:
                for b in range(NB):
                    h = r * NB + b
                    reduce_rows(h + 1, LEAD // 2, HALVES)
                    maxima(h + 1, True)
                    sums(h)
            for h in range(ROUNDS * NB, H1):
                if h + 1 < H1:
                    reduce_rows(h + 1, LEAD // 2, HALVES)
                    maxima(h + 1, h + 2 < H1)
                sums(h)

        @block.scalar
        def _(act):
            start_counts(act, exp_ready)

            def head(h):
                for k in range(UNITS):
                    t, c = k // NC, k % NC
                    if c == 0:
                        act.wait_ge(av_done, START + h * NT + t - 1)
                    act.wait_ge(st_ready, START + h * UNITS + k + 1)
                    nc.scalar.activation(pb[:, t % 2, c, :], m.psum[:, E_B + k % 2, :], ACT.Exp, scale=SCALE).then_inc(exp_ready, 1)

            with act.Fori(0, ROUNDS) as r:
                for b in range(NB):
                    head(r * NB + b)
            for h in range(ROUNDS * NB, H1):
                head(h)

        @block.gpsimd
        def _(pool):
            start_counts(pool, vx_ready)
            nc.gpsimd.memset(vx[:, :, :, :], 0.0).then_inc(vx_zeroed, 1)
            pool.wait_ge(vx_zeroed, 1)
            nc.gpsimd.memset(vx[:, :, :, HD1:HD1 + 1], 1.0).then_inc(vx_zeroed, 1)
            pool.wait_ge(vx_zeroed, 2)

            def values(h, b):
                nc.gpsimd.tensor_copy(vx[:, b, :, 0:HD1], m.v1[:, :, bass.ds(h * HD1, HD1)]).then_inc(vx_ready, 1)

            for b in range(NB):
                values(b, b)
            with pool.Fori(0, ROUNDS) as r:
                for b in range(NB):
                    pool.wait_ge(av_done, START + (r * NB + b + 1) * NT)
                    values(r * NB + b + NB, b)
            pool.wait_ge(av_done, START + (H1 - NB) * NT)
            values(H1 - 1, 0)


def output1_block(nc, m, a):
    with ExitStack() as ctx:
        def sem(name):
            return ctx.enter_context(nc.semaphore(name))

        attT = ctx.enter_context(nc.sbuf_tensor("attT", [P, N], F32))
        attT_ready, attT_saved, biased = sem("attT_ready"), sem("attT_saved"), sem("biased")
        o_ready, x_added = sem("o1_ready"), sem("o1_added")
        block = ctx.enter_context(nc.Block())

        @block.gpsimd
        def _(pool):
            bo = m.bo[:, :].rearrange("p (o d) -> p o d", o=1).broadcast_to([P, NT, D])
            x = m.x[:, :].rearrange("p (t d) -> p t d", d=D)
            nc.gpsimd.tensor_tensor(x, x, bo, ALU.add).then_inc(biased, 1)

        @block.tensor
        def _(pe):
            for c in range(NC):
                for i in range(TPB):
                    mm = nc.tensor.transpose(m.psum[:, c, i * P:(i + 1) * P], m.att[:, c * TPB + i, :], m.ident[:, :])
                mm.then_inc(attT_ready, 1)
            for c in range(NC):
                pe.wait_ge(attT_saved, c + 1)
                for i in range(TPB):
                    t = c * TPB + i
                    mm = nc.tensor.matmul(m.psum[:, 4 + c, i * P:(i + 1) * P], attT[:, t * P:(t + 1) * P], m.woT[:, :],
                                          start=True, stop=True)
                mm.then_inc(o_ready, 1)

        @block.scalar
        def _(act):
            for c in range(NC):
                act.wait_ge(attT_ready, c + 1)
                nc.scalar.activation(attT[:, c * BANK:(c + 1) * BANK], m.psum[:, c, :], ACT.Copy).then_inc(attT_saved, 1)

        @block.vector
        def _(dve):
            dve.wait_ge(biased, 1)
            for c in range(NC):
                dve.wait_ge(o_ready, c + 1)
                xc = m.x[:, c * BANK:(c + 1) * BANK]
                nc.vector.tensor_tensor(xc, xc, m.psum[:, 4 + c, :], ALU.add).then_inc(x_added, 1)


def experts_block(nc, m, a):
    K = NETS * HT
    with ExitStack() as ctx:
        def sb(name, shape, dt=F32):
            return ctx.enter_context(nc.sbuf_tensor(name, shape, dt))

        def sem(name):
            return ctx.enter_context(nc.semaphore(name))

        w1 = sb("w1", [P, NETS, HID])
        w2 = sb("w2", [P, NETS, HT, D])
        w2s = sb("w2s", [P, NETS, HT, D])
        b1 = sb("b1", [P, NETS, HT])
        b2 = sb("b2", [P, NETS, D])
        b2s = sb("b2s", [P, D])
        hT = sb("hT", [P, K, BANK])
        mean = sb("mean", [P, 1])
        lg = sb("lg", [1, NE])
        pw = sb("pw", [1, NE])
        psum_1 = sb("psum_1", [1, 1])
        nlg = sb("nlg", [1, 1])
        top = sb("top", [1, 8])
        chosen = sb("chosen", [1, 8], U32)
        cf = sb("cf", [1, NETS])
        cfb = sb("cfb", [P, NETS])
        al = sb("al", [1, 2])

        main_loaded, expert_loaded = sem("main_loaded"), sem("expert_loaded")
        step, logits_ready, exp_done, cf_ready, coef_ready, cfb_saved = (sem("step"), sem("logits_ready"), sem("exp2_ready"),
                                                                         sem("cf_ready"), sem("coefs_ready"), sem("cfb_saved"))
        chosen_ready, w2s_ready, b2_added = sem("chosen_ready"), sem("w2s_ready"), sem("b2_added")
        b2_step = sem("b2_step")
        h_ready, h_saved, y_ready, y_added = sem("h_ready"), sem("h_saved"), sem("y_ready"), sem("y2_added")
        block = ctx.enter_context(nc.Block())
        START = 2

        @block.sync
        def _(sp):
            def net(i, w1_src, w2_src, b1_src, b2_src, s):
                sp.dma_start(w1[:, i, :], w1_src).then_inc(s, 16)
                sp.dma_start(w2[:, i, :, :], w2_src.rearrange("(k p) d -> p k d", p=P)).then_inc(s, 16)
                sp.dma_start(b1[:, i, :], b1_src.rearrange("(k p) -> p k", p=P), allow_slow_non_contiguous=True).then_inc(s, 16)
                sp.dma_start(b2[:, i, :], b2_src.broadcast_to([P, D])).then_inc(s, 16)

            net(0, a["L1_ffn_W1m"], a["L1_ffn_W2m"], a["L1_ffn_b1m"], a["L1_ffn_b2m"].rearrange("(o d) -> o d", o=1), main_loaded)
            sp.wait_ge(chosen_ready, 1)
            for i in range(2):
                e = sp.value_load(chosen[0:1, i:i + 1], min_val=0, max_val=NE - 1)
                net(1 + i, a["L1_ffn_W1e"][bass.ds(e, 1)].rearrange("o d h -> (o d) h"),
                    a["L1_ffn_W2e"][bass.ds(e, 1)].rearrange("o h d -> (o h) d"),
                    a["L1_ffn_b1e"][bass.ds(e, 1)].rearrange("o h -> (o h)"), a["L1_ffn_b2e"][bass.ds(e, 1), :], expert_loaded)

        @block.vector
        def _(dve):
            n = [0]

            def chain(ins):
                n[0] += 1
                ins.then_inc(step, 1)
                dve.wait_ge(step, n[0])

            dve.sem_inc(y_added, START)
            chain(nc.vector.tensor_reduce(mean[:, :], m.xnT[:, :], AX_X, ALU.add))
            nc.vector.tensor_scalar(mean[:, :], mean[:, :], 1.0 / N, None, ALU.mult).then_inc(cf_ready, 1)
            dve.wait_ge(logits_ready, 1)
            chain(nc.vector.tensor_tensor(lg[:, :], m.psum[0:1, 6, 0:NE], m.bg[:, :], ALU.add))
            chain(nc.vector.tensor_reduce(nlg[:, :], lg[:, :], AX_X, ALU.max, negate=True))
            nc.vector.tensor_scalar(al[:, 0:1], m.alpha[:, :], 0.1, 1.0, ALU.max, ALU.min).then_inc(cf_ready, 1)
            dve.wait_ge(exp_done, 1)
            chain(nc.vector.reciprocal(psum_1[:, :], psum_1[:, :]))
            chain(nc.vector.tensor_scalar(pw[:, :], pw[:, :], psum_1[:, 0:1], None, ALU.mult))
            chain(nc.vector.max(top[:, :], pw[:, :]))
            nc.vector.max_index(chosen[:, :], top[:, :], pw[:, :]).then_inc(chosen_ready, 1)
            chain(nc.vector.tensor_tensor(nlg[:, :], top[:, 0:1], top[:, 1:2], ALU.add))
            chain(nc.vector.reciprocal(nlg[:, :], nlg[:, :]))
            chain(nc.vector.tensor_scalar(al[:, 1:2], al[:, 0:1], -1.0, 1.0, ALU.mult, ALU.add))
            chain(nc.vector.tensor_copy(cf[:, 0:1], al[:, 0:1]))
            nc.vector.tensor_scalar(cf[:, 1:3], top[:, 0:2], nlg[:, 0:1], al[:, 1:2], ALU.mult, ALU.mult).then_inc(cf_ready, 1)
            dve.wait_ge(coef_ready, 1)
            nc.vector.tensor_copy(cfb[:, :], m.psum[:, 7, 0:NETS]).then_inc(cfb_saved, 1)
            dve.wait_ge(cfb_saved, 1)
            for i in range(NETS):
                dve.wait_ge(*((expert_loaded, 128) if i else (main_loaded, 64)))
                nc.vector.tensor_scalar(w2s[:, i, :, :], w2[:, i, :, :], cfb[:, i:i + 1], None, ALU.mult).then_inc(w2s_ready, 1)
            nc.vector.tensor_scalar(b2s[:, :], b2[:, 0, :], cfb[:, 0:1], None, ALU.mult).then_inc(b2_step, 1)
            for i in range(1, NETS):
                dve.wait_ge(b2_step, i)
                nc.vector.scalar_tensor_tensor(b2s[:, :], b2[:, i, :], cfb[:, i:i + 1], b2s[:, :], ALU.mult, ALU.add).then_inc(b2_step, 1)
            dve.wait_ge(b2_added, 1)
            with dve.Fori(0, NC) as c:
                dve.wait_ge(y_ready, START + c + 1)
                xc = m.x[:, bass.ds(c * BANK, BANK)]
                nc.vector.tensor_tensor(xc, xc, m.psum[:, 4, :], ALU.add).then_inc(y_added, 1)

        @block.gpsimd
        def _(pool):
            pool.wait_ge(b2_step, NETS)
            x = m.x[:, :].rearrange("p (t d) -> p t d", d=D)
            nc.gpsimd.tensor_tensor(x, x, b2s[:, :].rearrange("p (o d) -> p o d", o=1).broadcast_to([P, NT, D]),
                                    ALU.add).then_inc(b2_added, 1)

        @block.scalar
        def _(act):
            act.sem_inc(h_saved, START)
            act.wait_ge(step, 3)
            nc.scalar.activation(pw[:, :], lg[:, :], ACT.Exp, bias=nlg[:, 0:1], accum_out=psum_1[:, :]).then_inc(exp_done, 1)
            act.wait_ge(main_loaded, 64)
            act.wait_ge(expert_loaded, 128)
            b1f = b1[:, :, :].rearrange("p i k -> p (i k)")
            with act.Fori(0, NC) as c:
                for k in range(K):
                    act.wait_ge(h_ready, START + c * K + k + 1)
                    nc.scalar.activation(hT[:, k, :], m.psum[:, k % 4, :], ACT.Gelu_apprx_tanh, bias=b1f[:, k:k + 1]).then_inc(h_saved, 1)

        @block.tensor
        def _(pe):
            pe.sem_inc(h_ready, START)
            pe.sem_inc(y_ready, START)
            pe.wait_ge(cf_ready, 1)
            nc.tensor.matmul(m.psum[0:1, 6, 0:NE], mean[:, :], m.wg[:, :], start=True, stop=True).then_inc(logits_ready, 1)
            pe.wait_ge(cf_ready, 3)
            nc.tensor.matmul(m.psum[:, 7, 0:NETS], m.ones[0:1, :], cf[:, :], start=True, stop=True).then_inc(coef_ready, 1)
            pe.wait_ge(main_loaded, 64)
            pe.wait_ge(expert_loaded, 128)
            pe.wait_ge(w2s_ready, NETS)
            with pe.Fori(0, NC) as c:
                for k in range(K):
                    i, q = k // HT, k % HT
                    pe.wait_ge(h_saved, START + c * K + max(k - 3, 0))
                    nc.tensor.matmul(m.psum[:, k % 4, :], w1[:, i, q * P:(q + 1) * P], m.xnT[:, bass.ds(c * BANK, BANK)],
                                     start=True, stop=True).then_inc(h_ready, 1)
                pe.wait_ge(y_added, START + c)
                for j in range(TPB):
                    for k in range(K):
                        if j == 0:
                            pe.wait_ge(h_saved, START + c * K + k + 1)
                        mm = nc.tensor.matmul(m.psum[:, 4, j * P:(j + 1) * P], hT[:, k, j * P:(j + 1) * P],
                                              w2s[:, k // HT, k % HT, :], start=(k == 0), stop=(k == K - 1))
                mm.then_inc(y_ready, 1)


def store_block(nc, m, out):
    with ExitStack() as ctx:
        stored = ctx.enter_context(nc.semaphore("stored"))
        block = ctx.enter_context(nc.Block())

        @block.sync
        def _(sp):
            sp.dma_start(out[0].rearrange("(t p) d -> p t d", p=P),
                         m.x[:, :].rearrange("p (t d) -> p t d", d=D)).then_inc(stored, 16)
            sp.wait_ge(stored, 16)


def build(nc, a, out):
    with ExitStack() as ctx:
        def sb(name, shape, dt=F32):
            return ctx.enter_context(nc.sbuf_tensor(name, shape, dt))

        m = Memory()
        m.x = sb("x", [P, NT * D])
        m.xn = sb("xn", [P, NT * D])
        m.xnT = sb("xnT", [P, N])
        m.stats = sb("stats", [P, NT * 6])
        m.moments = sb("moments", [P, NT * 2])
        m.std = sb("std", [P, NT])
        m.rstd = sb("rstd", [P, NT])
        m.ident = sb("ident", [P, P])
        m.identb = sb("identb", [P, P], BF16)
        m.ones = sb("ones", [P, P])
        m.mask = sb("mask", [P, 2 * WL])
        m.ws1 = sb("ws1", [P, UH])
        m.bs1 = sb("bs1", [UH, 1])
        m.ws2 = sb("ws2", [UH, 1])
        m.bs2 = sb("bs2", [P, 1])
        m.psum = ctx.enter_context(nc.psum_tensor("psum", [P, 8, BANK], F32))
        setup_block(nc, m, a)
        ln_block(nc, m, "ln0")
        attn0_block(nc, m, a)

        def row(ap):
            return ap.rearrange("(o d) -> o d", o=1)

        def column(ap):
            return ap.rearrange("(p o) -> p o", o=1)

        with ExitStack() as layer:
            def lb(name, shape, dt=F32):
                return layer.enter_context(nc.sbuf_tensor(name, shape, dt))

            m.qpT, m.rwT, m.akT = lb("qpT", [P, P]), lb("rwT", [P, RD]), lb("akT", [P, NKEY])
            m.av, m.rel = lb("av", [P, NKEY // P * D]), lb("rel", [P, NKEY])
            m.uw1T, m.ub1, m.uw2T, m.ub2 = lb("uw1T", [P, UH]), lb("ub1", [UH, 1]), lb("uw2T", [UH, 1]), lb("ub2", [P, 1])
            m.gw, m.gb = lb("gw", [P, 1]), lb("gb", [P, 1])
            ln_block(nc, m, "ln1", [
                (m.qpT[:, :], a["L0_ffn_q_proj_w"]), (m.rwT[:, :], a["L0_ffn_router_w"]), (m.akT[:, :], a["L0_ffn_aux_keys"]),
                (m.av[:, :].rearrange("p (k d) -> p k d", d=D), a["L0_ffn_aux_values"].rearrange("(k p) d -> p k d", p=P)),
                (m.rel[:, :], row(a["L0_ffn_reliability_mask"]).broadcast_to([P, NKEY])),
                (m.uw1T[:, :], a["L0_ffn_unc_w1"]), (m.ub1[:, :], column(a["L0_ffn_unc_b1"])), (m.uw2T[:, :], a["L0_ffn_unc_w2"]),
                (m.ub2[:, :], row(a["L0_ffn_unc_b2"]).broadcast_to([P, 1])), (m.gw[:, :], row(a["L0_ffn_gate_w1"]).broadcast_to([P, 1])),
                (m.gb[:, :], row(a["L0_ffn_gate_bias"]).broadcast_to([P, 1]))])
            memory_block(nc, m, a)
        with ExitStack() as layer:
            def lb(name, shape, dt=F32):
                return layer.enter_context(nc.sbuf_tensor(name, shape, dt))

            m.v1, m.att = lb("v1", [P, NT, D]), lb("att", [P, NT, D])
            m.woT, m.bo = lb("woT", [P, P]), lb("bo", [P, D])
            m.q_parts = nc.dram_tensor("q_parts", [PARTS, P, N], BF16, kind="Internal").ap()
            m.k_parts = nc.dram_tensor("k_parts", [PARTS, P, N], BF16, kind="Internal").ap()
            m.ones_rows = nc.inline_tensor(np.ones((PARTS, N), mybir.dt.np(BF16)), "ones_rows").ap()
            freq = (1.0 / np.float32(10000.0) ** (np.arange(0, HD1, 2, dtype=np.float32) / HD1)).astype(np.float32)
            angle = np.arange(N, dtype=np.float32)[None, :] * np.repeat(freq, 2)[:, None]
            sign = np.where(np.arange(HD1) % 2, 1.0, -1.0).astype(np.float32)[:, None]
            cos_t = nc.inline_tensor(np.tile(np.cos(angle), (H1, 1)).astype(np.float32), "cos_table").ap()
            sin_t = nc.inline_tensor(np.tile(np.sin(angle) * sign, (H1, 1)).astype(np.float32), "sin_table").ap()
            with ExitStack() as early:
                def eb(name, shape, dt=F32):
                    return early.enter_context(nc.sbuf_tensor(name, shape, dt))

                m.wqT, m.wkT, m.wvT = eb("wqT", [P, P]), eb("wkT", [P, P]), eb("wvT", [P, P])
                m.bq, m.bk, m.bqs, m.bks, m.bv = eb("bq", [P, 1]), eb("bk", [P, 1]), eb("bqs", [P, 1]), eb("bks", [P, 1]), eb("bv", [P, D])
                m.cos, m.sin = eb("cos", [P, N]), eb("sin", [P, N])
                loads = [(m.wqT[:, :], a["L1_attn_Wq"]), (m.wkT[:, :], a["L1_attn_Wk"]), (m.wvT[:, :], a["L1_attn_Wv"]),
                         (m.woT[:, :], a["L1_attn_Wo"]), (m.bq[:, :], column(a["L1_attn_bq"])), (m.bk[:, :], column(a["L1_attn_bk"])),
                         (m.bv[:, :], row(a["L1_attn_bv"]).broadcast_to([P, D])), (m.bo[:, :], row(a["L1_attn_bo"]).broadcast_to([P, D]))]
                for dst, src in ((m.bqs, a["L1_attn_bq"]), (m.bks, a["L1_attn_bk"])):
                    for k in range(2):
                        loads.append((dst[k:P:2, :], src.rearrange("(f two) -> two f", two=2)[1 - k].rearrange("(p o) -> p o", o=1)))
                loads += [(m.cos[:, :], cos_t), (m.sin[:, :], sin_t)]
                ln_block(nc, m, "ln2", loads)
                project1_block(nc, m, a)
            attn1_block(nc, m, a)
            output1_block(nc, m, a)
        with ExitStack() as layer:
            def lb(name, shape, dt=F32):
                return layer.enter_context(nc.sbuf_tensor(name, shape, dt))

            m.wg, m.bg, m.alpha = lb("wg", [P, NE]), lb("bg", [1, NE]), lb("alpha", [1, 1])
            ln_block(nc, m, "ln3", [(m.wg[:, :], a["L1_ffn_w_gate"]), (m.bg[:, :], row(a["L1_ffn_b_gate"])),
                                    (m.alpha[:, :], row(a["L1_ffn_alpha"]))])
            experts_block(nc, m, a)
        store_block(nc, m, out)


_INS = ['L0_attn_x', 'L0_attn_wq', 'L0_attn_wk', 'L0_attn_wv', 'L0_attn_wo', 'L0_attn_ws1', 'L0_attn_bs1', 'L0_attn_ws2', 'L0_attn_bs2',
        'L0_ffn_q_proj_w', 'L0_ffn_router_w', 'L0_ffn_aux_keys', 'L0_ffn_aux_values', 'L0_ffn_reliability_mask', 'L0_ffn_unc_w1',
        'L0_ffn_unc_b1', 'L0_ffn_unc_w2', 'L0_ffn_unc_b2', 'L0_ffn_gate_w1', 'L0_ffn_gate_bias', 'L1_attn_Wq', 'L1_attn_bq', 'L1_attn_Wk',
        'L1_attn_bk', 'L1_attn_Wv', 'L1_attn_bv', 'L1_attn_Wo', 'L1_attn_bo', 'L1_ffn_alpha', 'L1_ffn_w_gate', 'L1_ffn_b_gate', 'L1_ffn_W1m',
        'L1_ffn_b1m', 'L1_ffn_W2m', 'L1_ffn_b2m', 'L1_ffn_W1e', 'L1_ffn_b1e', 'L1_ffn_W2e', 'L1_ffn_b2e']
_TURNED = ['L0_ffn_q_proj_w', 'L0_ffn_router_w', 'L0_ffn_aux_keys', 'L0_ffn_unc_w1', 'L0_ffn_unc_w2',
           'L1_attn_Wq', 'L1_attn_Wk', 'L1_attn_Wv', 'L1_attn_Wo']


def kernel(**inputs):
    import numpy as _np
    import concourse.bacc as _bacc
    from concourse import mybir as _mybir
    from concourse.bass_utils import run_bass_kernel_spmd as _run

    nc = _bacc.Bacc("TRN2", target_bir_lowering=False, num_devices=1)
    arrays, args = {}, {}
    for name in _INS:
        x = inputs[name]
        if name in _TURNED:
            x = _np.asarray(x).T
        x = _np.ascontiguousarray(x)
        if x.ndim == 0:
            x = x.reshape(1)
        arrays[f"in_{name}"] = x
        args[name] = nc.dram_tensor(f"in_{name}", x.shape, _mybir.dt.from_np(x.dtype), kind="ExternalInput").ap()
    out = nc.dram_tensor("out_0", (1, N, D), F32, kind="ExternalOutput").ap()
    build(nc, args, out)
    r = _run(nc, [arrays], core_ids=[0])
    return r.results[0]["out_0"]
```

```python
from contextlib import ExitStack

import numpy as np
import concourse.bass as bass
from concourse import mybir

F32 = mybir.dt.float32
BF16 = mybir.dt.bfloat16
U32 = mybir.dt.uint32
ACT = mybir.ActivationFunctionType
ALU = mybir.AluOpType
AX_X = mybir.AxisListType.X

P = 128
N = 2048
D = 128
NT = N // P
BANK = 512
NC = N // BANK
TPB = BANK // P
EPS = 1e-5

H0, HD0, G0 = 16, 64, 32
PAIRS = H0 // 2
WL = P + G0
F32_LOW = -3.4028234663852886e38
MASKED = -1e30

RD, NKEY, UH = 48, 512, 32

H1, HD1 = 16, 8
PARTS = 3
QROWS = PARTS * PARTS * HD1
MROW = QROWS
KROWS = QROWS + PARTS
VCOLS = 32

HID, NE = 512, 8
HT = HID // P
NETS = 3


class Memory:
    pass


def ln_block(nc, m, tag, loads=()):
    with ExitStack() as ctx:
        variance_steps = ctx.enter_context(nc.semaphore(f"{tag}_variance_steps"))
        std_ready = ctx.enter_context(nc.semaphore(f"{tag}_std_ready"))
        rstd_ready = ctx.enter_context(nc.semaphore(f"{tag}_rstd_ready"))
        xn_ready = ctx.enter_context(nc.semaphore(f"{tag}_xn_ready"))
        xn_pool_ready = ctx.enter_context(nc.semaphore(f"{tag}_xn_pool_ready"))
        turned = ctx.enter_context(nc.semaphore(f"{tag}_turned"))
        loaded = ctx.enter_context(nc.semaphore(f"{tag}_loaded")) if loads else None
        block = ctx.enter_context(nc.Block())
        POOL_TILE = TPB - 1
        mv = m.moments[:, :].rearrange("p (t c) -> p t c", c=2)

        @block.sync
        def _(sp):
            for dst, src in loads:
                sp.dma_start(dst, src, allow_slow_non_contiguous=True).then_inc(loaded, 16)
            if loads:
                sp.wait_ge(loaded, 16 * len(loads))

        @block.vector
        def _(dve):
            for t in range(NT):
                nc.vector.bn_stats(m.stats[:, t * 6:t * 6 + 6], m.x[:, t * D:(t + 1) * D]).then_inc(variance_steps, 1)
            dve.wait_ge(variance_steps, NT)
            for t in range(NT):
                nc.vector.bn_aggr(m.moments[:, t * 2:t * 2 + 2], m.stats[:, t * 6:t * 6 + 6]).then_inc(variance_steps, 1)
            dve.wait_ge(variance_steps, 2 * NT)
            nc.vector.tensor_scalar(m.rstd[:, :], mv[:, :, 1], EPS, None, ALU.add).then_inc(variance_steps, 1)
            dve.wait_ge(std_ready, 1)
            nc.vector.reciprocal(m.rstd[:, :], m.std[:, :]).then_inc(rstd_ready, 1)
            dve.wait_ge(rstd_ready, 1)
            for t in range(NT):
                if t % TPB != POOL_TILE:
                    nc.vector.tensor_scalar(m.xn[:, t * D:(t + 1) * D], m.x[:, t * D:(t + 1) * D],
                                            mv[:, t, 0:1], m.rstd[:, t:t + 1], ALU.subtract, ALU.mult).then_inc(xn_ready, 1)

        @block.gpsimd
        def _(pool):
            pool.wait_ge(rstd_ready, 1)
            for t in range(POOL_TILE, NT, TPB):
                nc.gpsimd.tensor_scalar(m.xn[:, t * D:(t + 1) * D], m.x[:, t * D:(t + 1) * D],
                                        mv[:, t, 0:1], m.rstd[:, t:t + 1], ALU.subtract, ALU.mult).then_inc(xn_pool_ready, 1)

        @block.scalar
        def _(act):
            act.wait_ge(variance_steps, 2 * NT + 1)
            nc.scalar.activation(m.std[:, :], m.rstd[:, :], ACT.Sqrt).then_inc(std_ready, 1)
            for c in range(NC):
                act.wait_ge(turned, c + 1)
                nc.scalar.activation(m.xnT[:, c * BANK:(c + 1) * BANK], m.psum[:, c, :], ACT.Copy)

        @block.tensor
        def _(pe):
            for c in range(NC):
                pe.wait_ge(xn_ready, (TPB - 1) * (c + 1))
                pe.wait_ge(xn_pool_ready, c + 1)
                for i in range(TPB):
                    t = TPB * c + i
                    mm = nc.tensor.transpose(m.psum[:, c, i * P:(i + 1) * P], m.xn[:, t * D:(t + 1) * D], m.ident[:, :])
                mm.then_inc(turned, 1)


def setup_block(nc, m, a):
    with ExitStack() as ctx:
        zeroed = ctx.enter_context(nc.semaphore("zeroed"))
        patterned = ctx.enter_context(nc.semaphore("patterned"))
        loaded = ctx.enter_context(nc.semaphore("loaded"))
        block = ctx.enter_context(nc.Block())

        @block.sync
        def _(sp):
            sp.dma_start(m.x[:, :].rearrange("p (t d) -> p t d", d=D),
                         a["L0_attn_x"][0].rearrange("(t p) d -> p t d", p=P)).then_inc(loaded, 16)
            sp.dma_start(m.ws1[:, :], a["L0_attn_ws1"]).then_inc(loaded, 16)
            sp.dma_start(m.bs1[:, :], a["L0_attn_bs1"].rearrange("(p o) -> p o", o=1)).then_inc(loaded, 16)
            sp.dma_start(m.ws2[:, :], a["L0_attn_ws2"]).then_inc(loaded, 16)
            sp.dma_start(m.bs2[:, :], a["L0_attn_bs2"].rearrange("(o c) -> o c", o=1).broadcast_to([P, 1])).then_inc(loaded, 16)
            sp.wait_ge(loaded, 5 * 16)

        @block.gpsimd
        def _(pool):
            nc.gpsimd.memset(m.ident[:, :], 0.0).then_inc(zeroed, 1)
            nc.gpsimd.memset(m.identb[:, :], 0.0).then_inc(zeroed, 1)
            nc.gpsimd.memset(m.mask[:, :], 0.0).then_inc(zeroed, 1)
            nc.gpsimd.memset(m.ones[:, :], 1.0).then_inc(zeroed, 1)
            pool.wait_ge(zeroed, 4)
            nc.gpsimd.affine_select(out=m.ident[:, :], in_=m.ident[:, :], compare_op=ALU.not_equal, fill=1.0,
                                    base=0, pattern=[[-1, P]], channel_multiplier=1).then_inc(patterned, 1)
            nc.gpsimd.affine_select(out=m.identb[:, :], in_=m.identb[:, :], compare_op=ALU.not_equal, fill=1.0,
                                    base=0, pattern=[[-1, P]], channel_multiplier=1).then_inc(patterned, 1)
            for j in range(2):
                w = m.mask[:, j * WL:j * WL + P]
                nc.gpsimd.affine_select(out=w, in_=w, compare_op=ALU.is_ge, fill=MASKED,
                                        base=0, pattern=[[-1, P]], channel_multiplier=1).then_inc(patterned, 1)


def attn0_block(nc, m, a, loads):
    SCALE = HD0 ** -0.5
    with ExitStack() as ctx:
        def sb(name, shape, dt=F32):
            return ctx.enter_context(nc.sbuf_tensor(name, shape, dt))

        def sem(name):
            return ctx.enter_context(nc.semaphore(name))

        w_cur = sb("w_cur", [P, 2, 3, P])
        wo_cur = sb("wo_cur", [P, 2, D])
        qz = sb("qz", [P, 2, 2, N])
        kx = sb("kx", [P, 2, NT, WL])
        v = sb("v0", [P, 2, NT, P])
        gv = sb("gv", [2 * G0, 2, P])
        gtok = sb("gtok", [P, 2 * G0])
        sm = sb("sm", [P, 4, 2 * WL])
        pr = sb("pr", [P, 4, 2 * WL])
        nmax = sb("nmax", [P, 4, 4])
        total = sb("total", [P, 4, 4])
        rtotal = sb("rtotal", [P, 4, 4])
        pt = sb("pt", [P, 2, 3 * P])
        oT = sb("oT", [P, 4, P])
        ws2r = sb("ws2r", [UH, P])
        gate_h = sb("gate_h", [UH, 1])
        gate_s = sb("gate_s", [P, 1])
        gate_m = sb("gate_m", [P, 1], U32)

        w_loaded = (sem("w_even_loaded"), sem("w_odd_loaded"))
        wo_loaded = (sem("wo_even_loaded"), sem("wo_odd_loaded"))
        zeroed = sem("zeroed0")
        ws2_spread = sem("ws2_spread")
        token_copied = sem("token_copied")
        score_hidden = sem("score_hidden")
        score_gelu = sem("score_gelu")
        score_ready = sem("score_ready")
        score_saved = sem("score_saved")
        low_ready = sem("low_ready")
        gtok_ready = sem("gtok_ready")
        q_ready, q_saved = sem("q_ready"), sem("q_saved")
        k_ready, k_saved = sem("k_ready"), sem("k_saved")
        v_ready, v_saved = sem("v_ready"), sem("v_saved")
        g_ready, g_saved = sem("g_ready"), sem("g_saved")
        scores_ready, masked = sem("scores_ready"), sem("masked")
        max_ready, exp_ready = sem("max_ready"), sem("exp_ready")
        rtotal_ready, probs_ready = sem("rtotal_ready"), sem("probs_ready")
        pt_ready, pt_saved = sem("pt_ready"), sem("pt_saved")
        o_ready, o_saved = sem("o_ready"), sem("o_saved")
        wo_done, y_added = sem("wo_done"), sem("y_added")
        later_loaded = sem("later_loaded")
        block = ctx.enter_context(nc.Block())

        ROUND = 2 * NT
        LAG = 4
        LAST = PAIRS // 2 - 1

        S_B, T_B, O_B, Y_B, J_B = 0, 2, 4, 6, 7
        gk_ps = m.psum[:, J_B, 0:G0]
        gv_ps = m.psum[0:2 * G0, J_B, P:2 * P]

        def job(i, more):
            k = i % NT - LAG
            if i < 0 or k < 0 or i >= ROUND or (i >= NT and not more):
                return None
            return i // NT + 1, k // 3, "qkv"[k % 3]

        @block.sync
        def _(sp):
            def load_w(pair, b):
                for i, w in enumerate((a["L0_attn_wq"], a["L0_attn_wk"], a["L0_attn_wv"])):
                    sp.dma_start(w_cur[:, b, i, :], w[:, bass.ds(pair * P, P)]).then_inc(w_loaded[b], 16)

            def load_wo(pair, b):
                sp.dma_start(wo_cur[:, b, :], a["L0_attn_wo"][bass.ds(pair * P, P), :]).then_inc(wo_loaded[b], 16)

            for b in range(2):
                load_w(b, b)
                load_wo(b, b)
            for dst, src in loads:
                sp.dma_start(dst, src, allow_slow_non_contiguous=True).then_inc(later_loaded, 16)
            with sp.Fori(0, LAST) as r:
                for b in range(2):
                    sp.wait_ge(v_ready, r * 2 * NC + (b + 1) * NC)
                    load_w(r * 2 + (2 + b), b)
                for b in range(2):
                    sp.wait_ge(wo_done, r * ROUND + (b + 1) * NT)
                    load_wo(r * 2 + (2 + b), b)
            sp.wait_ge(later_loaded, 16 * len(loads))

        @block.tensor
        def _(pe):
            nc.tensor.matmul(m.psum[0:UH, J_B, 0:1], m.ws1[:, :], m.xnT[:, 0:1], start=True, stop=True).then_inc(score_hidden, 1)
            pe.wait_ge(score_gelu, 1)
            pe.wait_ge(ws2_spread, 1)
            nc.tensor.matmul(m.psum[:, Y_B, 0:1], ws2r[:, :], gate_h[:, :], start=True, stop=True).then_inc(score_ready, 1)
            pe.wait_ge(gtok_ready, 1)

            def project_globals(b):
                nc.tensor.matmul(gk_ps, w_cur[:, b, 1, :], gtok[:, 0:G0], start=True, stop=True)
                nc.tensor.matmul(gv_ps, gtok[:, :], w_cur[:, b, 2, :], start=True, stop=True).then_inc(g_ready, 1)

            def project(b, c, what, bank):
                if what == "v":
                    for i in range(TPB):
                        t = TPB * c + i
                        mm = nc.tensor.matmul(m.psum[:, bank, i * P:(i + 1) * P], m.xnT[:, t * P:(t + 1) * P],
                                              w_cur[:, b, 2, :], start=True, stop=True)
                    mm.then_inc(v_ready, 1)
                elif what == "q":
                    nc.tensor.matmul(m.psum[:, bank, :], w_cur[:, b, 0, :], m.xnT[:, c * BANK:(c + 1) * BANK],
                                     start=True, stop=True).then_inc(q_ready, 1)
                else:
                    nc.tensor.matmul(m.psum[:, bank, :], w_cur[:, b, 1, :], m.xnT[:, c * BANK:(c + 1) * BANK],
                                     start=True, stop=True).then_inc(k_ready, 1)

            def step(r, i, more=True):
                if i < ROUND or more:
                    b, s = i // NT % 2, i % NT
                    if s == 0:
                        pe.wait_ge(q_saved, r * 2 * NC + (i // NT + 1) * NC)
                        pe.wait_ge(k_saved, r * 2 * NC + (i // NT + 1) * NC)
                        pe.wait_ge(g_saved, r * 2 + i // NT + 1)
                    if i >= 2:
                        pe.wait_ge(masked, r * ROUND + i - 1)
                    for j in range(2):
                        mm = nc.tensor.matmul(m.psum[:, S_B + i % 2, j * WL:(j + 1) * WL],
                                              qz[:, b, j, s * P:(s + 1) * P], kx[:, b, s, :], start=True, stop=True)
                    mm.then_inc(scores_ready, 1)
                if job(i, more) and job(i, more)[1:] == (0, "q"):
                    q = job(i, more)[0]
                    pe.wait_ge(w_loaded[q % 2], (r + q // 2) * 48 + 48)
                    pe.wait_ge(v_saved, r * 2 * NC + q * NC)
                    project_globals(q % 2)
                w = i - 2
                if 0 <= w < ROUND or (w >= ROUND and more):
                    pe.wait_ge(probs_ready, r * ROUND + w + 1)
                    if w >= 2:
                        pe.wait_ge(pt_saved, r * ROUND + w - 1)
                    for j in range(2):
                        nc.tensor.transpose(m.psum[:, T_B + w % 2, j * P:(j + 1) * P], pr[:, w % 4, j * P:(j + 1) * P],
                                            m.ident[:, :])
                    nc.tensor.transpose(m.psum[0:2 * G0, T_B + w % 2, 2 * P:3 * P], pr[:, w % 4, 2 * P:2 * WL],
                                        m.ident[:, :]).then_inc(pt_ready, 1)
                w = i - 3
                if 0 <= w < ROUND or (w >= ROUND and more):
                    b, s = w // NT % 2, w % NT
                    if s == 0:
                        pe.wait_ge(v_saved, r * 2 * NC + (w // NT + 1) * NC)
                    pe.wait_ge(pt_saved, r * ROUND + w + 1)
                    if w >= 2:
                        pe.wait_ge(o_saved, r * ROUND + w - 1)
                    ob = m.psum[:, O_B + w % 2, 0:P]
                    nc.tensor.matmul(ob, gv[:, b, :], pt[0:2 * G0, w % 2, 2 * P:3 * P], start=True, stop=False)
                    for j in range(2):
                        mm = nc.tensor.matmul(ob[j * HD0:(j + 1) * HD0, :], v[:, b, s, j * HD0:(j + 1) * HD0],
                                              pt[:, w % 2, j * P:(j + 1) * P], start=False, stop=True)
                    mm.then_inc(o_ready, 1)
                w = i - LAG
                if 0 <= w < ROUND:
                    b = w // NT
                    if w % NT == 0:
                        pe.wait_ge(wo_loaded[b], r * 16 + 16)
                    pe.wait_ge(o_saved, r * ROUND + w + 1)
                    if w % TPB == 0:
                        pe.wait_ge(y_added, r * 2 * NC + w // TPB + 1)
                    nc.tensor.matmul(m.psum[:, Y_B, (w % TPB) * P:(w % TPB + 1) * P],
                                     oT[:, w % 4, :], wo_cur[:, b, :], start=True, stop=True).then_inc(wo_done, 1)
                if job(i, more):
                    q, c, what = job(i, more)
                    if what == "q" and c == 0:
                        pe.wait_ge(g_saved, r * 2 + q + 1)
                    elif what == "q":
                        pe.wait_ge(v_saved, r * 2 * NC + q * NC + c)
                    elif what == "k":
                        pe.wait_ge(q_saved, r * 2 * NC + q * NC + c + 1)
                    else:
                        pe.wait_ge(k_saved, r * 2 * NC + q * NC + c + 1)
                    project(q % 2, c, what, J_B)

            pe.wait_ge(w_loaded[0], 48)
            project_globals(0)
            for c in range(NC):
                if c == 0:
                    pe.wait_ge(g_saved, 1)
                else:
                    pe.wait_ge(q_saved, c)
                project(0, c, "q", J_B)
                if c >= 1:
                    pe.wait_ge(k_saved, c)
                project(0, c, "k", Y_B)
                if c >= 1:
                    pe.wait_ge(v_saved, c)
                project(0, c, "v", O_B + 1)
            for i in range(LAG):
                step(0, i)
            with pe.Fori(0, LAST) as r:
                for i in range(LAG, ROUND + LAG):
                    step(r, i)
            for i in range(LAG, ROUND + LAG):
                step(LAST, i, more=False)

        @block.vector
        def _(dve):
            dve.sem_inc(y_added, 1)
            nc.vector.tensor_scalar(ws2r[:, :], m.ones[0:UH, :], m.ws2[:, 0:1], None, ALU.mult).then_inc(ws2_spread, 1)
            nc.vector.tensor_copy(gtok[:, 0:G0], m.xnT[:, 0:G0]).then_inc(token_copied, 1)
            nc.vector.tensor_copy(gtok[:, G0:2 * G0], m.xnT[:, 0:G0]).then_inc(token_copied, 1)
            dve.wait_ge(score_ready, 1)
            nc.vector.tensor_scalar(gate_s[:, :], m.psum[:, Y_B, 0:1], m.bs2[:, 0:1], None, ALU.add).then_inc(score_saved, 1)
            dve.wait_ge(score_saved, 1)
            nc.vector.tensor_scalar(gate_m[:, :], gate_s[:, :], F32_LOW, None, ALU.is_lt).then_inc(low_ready, 1)
            dve.wait_ge(low_ready, 1)
            dve.wait_ge(token_copied, 2)
            for j in range(2):
                nc.vector.copy_predicated(gtok[:, j * G0:j * G0 + 1], gate_m[:, :], m.xnT[:, G0:G0 + 1])\
                    .then_inc(*((gtok_ready, 1) if j else (token_copied, 1)))

            def save_globals(r, q):
                b = q % 2
                dve.wait_ge(g_ready, r * 2 + q + 1)
                nc.vector.tensor_copy(kx[:, b, :, P:WL], gk_ps.rearrange("p (o g) -> p o g", o=1).broadcast_to([P, NT, G0]))
                for j in range(2):
                    mm = nc.vector.tensor_copy(gv[j * G0:(j + 1) * G0, b, j * HD0:(j + 1) * HD0],
                                               gv_ps[j * G0:(j + 1) * G0, j * HD0:(j + 1) * HD0])
                mm.then_inc(g_saved, 1)

            def save_keys(r, q, c, bank):
                dve.wait_ge(k_ready, r * 2 * NC + q * NC + c + 1)
                nc.vector.tensor_copy(kx[:, q % 2, TPB * c:TPB * (c + 1), 0:P],
                                      m.psum[:, bank, :].rearrange("p (t k) -> p t k", t=TPB)).then_inc(k_saved, 1)

            def save_values(r, q, c, bank):
                dve.wait_ge(v_ready, r * 2 * NC + q * NC + c + 1)
                nc.vector.tensor_copy(v[:, q % 2, TPB * c:TPB * (c + 1), :],
                                      m.psum[:, bank, :].rearrange("p (t k) -> p t k", t=TPB)).then_inc(v_saved, 1)

            def step(r, i, more=True):
                if job(i - 1, more):
                    q, c, what = job(i - 1, more)
                    if what == "k":
                        save_keys(r, q, c, J_B)
                    elif what == "v":
                        save_values(r, q, c, J_B)
                if i < ROUND or more:
                    dve.wait_ge(scores_ready, r * ROUND + i + 1)
                    nc.vector.tensor_tensor(sm[:, i % 4, :], m.psum[:, S_B + i % 2, 0:2 * WL], m.mask[:, :],
                                            ALU.add).then_inc(masked, 1)
                    dve.wait_ge(masked, r * ROUND + i + 1)
                    smw = sm[:, i % 4, :].rearrange("p (j c) -> p j c", j=2)
                    nc.vector.tensor_reduce(nmax[:, i % 4, 0:2], smw[:, :, 0:P], AX_X, ALU.max, negate=True)
                    nc.vector.tensor_reduce(nmax[:, i % 4, 2:4], smw[:, :, P:WL], AX_X, ALU.max,
                                            negate=True).then_inc(max_ready, 1)
                if job(i, more) and job(i, more)[1:] == (0, "q"):
                    save_globals(r, job(i, more)[0])
                w = i - 1
                if 0 <= w < ROUND or (w >= ROUND and more):
                    dve.wait_ge(exp_ready, r * ROUND + w + 1)
                    nc.vector.reciprocal(rtotal[:, w % 4, :], total[:, w % 4, :]).then_inc(rtotal_ready, 1)
                w = i - 2
                if 0 <= w < ROUND or (w >= ROUND and more):
                    dve.wait_ge(pt_ready, r * ROUND + w + 1)
                    if w >= 2:
                        dve.wait_ge(o_ready, r * ROUND + w - 1)
                    nc.vector.tensor_copy(pt[:, w % 2, 0:2 * P], m.psum[:, T_B + w % 2, 0:2 * P])
                    nc.vector.tensor_copy(pt[0:2 * G0, w % 2, 2 * P:3 * P],
                                          m.psum[0:2 * G0, T_B + w % 2, 2 * P:3 * P]).then_inc(pt_saved, 1)
                if i % TPB == TPB - 1 and i > LAG:
                    g = i // TPB - 1
                    dve.wait_ge(wo_done, r * ROUND + TPB * (g + 1))
                    dve.wait_ge(y_added, r * 2 * NC + g + 1)
                    xg = m.x[:, g % NC * BANK:(g % NC + 1) * BANK]
                    nc.vector.tensor_tensor(xg, xg, m.psum[:, Y_B, :], ALU.add).then_inc(y_added, 1)

            dve.wait_ge(zeroed, 5)
            save_globals(0, 0)
            for c in range(NC):
                save_keys(0, 0, c, Y_B)
                save_values(0, 0, c, O_B + 1)
            for i in range(LAG):
                step(0, i)
            with dve.Fori(0, LAST) as r:
                for i in range(LAG, ROUND + LAG):
                    step(r, i)
            for i in range(LAG, ROUND + LAG):
                step(LAST, i, more=False)

        @block.scalar
        def _(act):
            act.wait_ge(score_hidden, 1)
            nc.scalar.activation(gate_h[:, :], m.psum[0:UH, J_B, 0:1], ACT.Gelu, bias=m.bs1[:, 0:1]).then_inc(score_gelu, 1)

            def save_queries(r, q, c):
                act.wait_ge(q_ready, r * 2 * NC + q * NC + c + 1)
                for j in range(2):
                    h = slice(j * HD0, (j + 1) * HD0)
                    mm = nc.scalar.activation(qz[h, q % 2, j, c * BANK:(c + 1) * BANK], m.psum[h, J_B, :],
                                              ACT.Copy, scale=SCALE)
                mm.then_inc(q_saved, 1)

            def step(r, i, more=True):
                if job(i - 1, more) and job(i - 1, more)[2] == "q":
                    save_queries(r, job(i - 1, more)[0], job(i - 1, more)[1])
                if i < ROUND or more:
                    act.wait_ge(max_ready, r * ROUND + i + 1)
                    if i >= 4:
                        act.wait_ge(pt_ready, r * ROUND + i - 3)
                    for j in range(2):
                        nc.scalar.activation(pr[:, i % 4, j * P:(j + 1) * P], sm[:, i % 4, j * WL:j * WL + P], ACT.Exp,
                                             bias=nmax[:, i % 4, j:j + 1], accum_out=total[:, i % 4, j:j + 1])
                        mm = nc.scalar.activation(pr[:, i % 4, 2 * P + j * G0:2 * P + (j + 1) * G0],
                                                  sm[:, i % 4, j * WL + P:(j + 1) * WL], ACT.Exp,
                                                  bias=nmax[:, i % 4, 2 + j:3 + j], accum_out=total[:, i % 4, 2 + j:3 + j])
                    mm.then_inc(exp_ready, 1)
                w = i - 3
                if 0 <= w < ROUND or (w >= ROUND and more):
                    act.wait_ge(o_ready, r * ROUND + w + 1)
                    nc.scalar.activation(oT[:, w % 4, :], m.psum[:, O_B + w % 2, 0:P], ACT.Copy).then_inc(o_saved, 1)

            act.wait_ge(zeroed, 5)
            for c in range(NC):
                save_queries(0, 0, c)
            for i in range(LAG):
                step(0, i)
            with act.Fori(0, LAST) as r:
                for i in range(LAG, ROUND + LAG):
                    step(r, i)
            for i in range(LAG, ROUND + LAG):
                step(LAST, i, more=False)

        @block.gpsimd
        def _(pool):
            for b in range(2):
                nc.gpsimd.memset(qz[HD0:P, b, 0, :], 0.0).then_inc(zeroed, 1)
                nc.gpsimd.memset(qz[0:HD0, b, 1, :], 0.0).then_inc(zeroed, 1)
            nc.gpsimd.memset(gv[:, :, :], 0.0).then_inc(zeroed, 1)
            with pool.Fori(0, PAIRS) as p:
                for w in range(NT):
                    pool.wait_ge(rtotal_ready, p * NT + w + 1)
                    for cols, r in ((slice(0, 2 * P), slice(0, 2)), (slice(2 * P, 2 * WL), slice(2, 4))):
                        prw = pr[:, w % 4, cols].rearrange("p (j c) -> p j c", j=2)
                        rb = rtotal[:, w % 4, r].rearrange("p (j o) -> p j o", o=1).broadcast_to(list(prw.shape))
                        mm = nc.gpsimd.tensor_tensor(prw, prw, rb, ALU.mult)
                    mm.then_inc(probs_ready, 1)


def memory_block(nc, m, a):
    REPLACED = -3e38
    REL_ROW = P // 2
    with ExitStack() as ctx:
        def sb(name, shape, dt=F32):
            return ctx.enter_context(nc.sbuf_tensor(name, shape, dt))

        def sem(name):
            return ctx.enter_context(nc.semaphore(name))

        qyT = sb("qyT", [P, N])
        rqT = sb("rqT", [P, N])
        rkT = sb("rkT", [P, NKEY])
        h1T = sb("h1T", [UH, N])
        logvar = sb("logvar", [P, NT])
        logvar_sum = sb("logvar_sum", [P, 1])
        learned = sb("learned", [P, NT])
        gate = sb("gate", [P, NT])
        norm = sb("norm", [P, 1])
        sc = sb("sc", [P, 4, NKEY])
        sr = sb("sr", [P, 2, NKEY])
        ex = sb("ex", [P, 2, NKEY])
        wt = sb("wt", [P, 2, NKEY])
        wT = sb("wT", [P, 2, NKEY])
        best = sb("best", [P, NT, 8])
        nbest = sb("nbest", [P, NT])
        wsum = sb("wsum", [P, NT])
        coef = sb("coef", [P, NT])

        zeroed, one_row, rel_loaded = sem("zeroed1"), sem("one_row"), sem("rel_loaded")
        qy_ready, qy_saved = sem("qy_ready"), sem("qy_saved")
        rq_ready, rq_saved = sem("rq_ready"), sem("rq_saved")
        h1_ready, h1_saved = sem("h1_ready"), sem("h1_saved")
        learned_ready, logvar_ready, total_ready = sem("learned_ready"), sem("logvar_ready"), sem("total_ready")
        sigmoid_ready, gate_step, gate_ready = sem("sigmoid_ready"), sem("gate_step"), sem("gate_ready")
        stats_ready, var_ready, x_added = sem("m_stats_ready"), sem("m_var_ready"), sem("x_added")
        sc_ready, sc_saved = sem("sc_ready"), sem("sc_saved")
        best_ready, nbest_ready, ex_ready, replaced = sem("best_ready"), sem("nbest_ready"), sem("ex_ready"), sem("replaced")
        wt_ready, wT_ready, wT_saved = sem("wt_ready"), sem("wT_ready"), sem("wT_saved")
        agg_ready, wsum_ready, coef_ready, y_added = sem("agg_ready"), sem("wsum_ready"), sem("coef_ready"), sem("m_y_added")
        block = ctx.enter_context(nc.Block())
        mv = m.moments[:, :].rearrange("p (t c) -> p t c", c=2)

        @block.tensor
        def _(pe):
            for c in range(NC):
                nc.tensor.matmul(m.psum[:, c, :], m.qpT[:, :], m.xnT[:, c * BANK:(c + 1) * BANK],
                                 start=True, stop=True).then_inc(qy_ready, 1)
            for c in range(NC):
                nc.tensor.matmul(m.psum[0:UH, 4 + c, :], m.uw1T[:, :], m.xnT[:, c * BANK:(c + 1) * BANK],
                                 start=True, stop=True).then_inc(h1_ready, 1)
            for c in range(NC):
                pe.wait_ge(qy_saved, c + 1)
                nc.tensor.matmul(m.psum[0:RD, c, :], m.rwT[:, :], qyT[:, c * BANK:(c + 1) * BANK],
                                 start=True, stop=True).then_inc(rq_ready, 1)
            pe.wait_ge(h1_saved, NC)
            nc.tensor.matmul(m.psum[0:RD, 4, :], m.rwT[:, :], m.akT[:, :],
                             start=True, stop=True).then_inc(rq_ready, 1)
            pe.wait_ge(rq_saved, NC + 1)
            pe.wait_ge(one_row, 1)
            pe.wait_ge(rel_loaded, 16)
            for s in range(NT + 3):
                if s < NT:
                    if s >= 2:
                        pe.wait_ge(sc_saved, s - 1)
                    nc.tensor.matmul(m.psum[:, s % 2, :], rqT[:, s * P:(s + 1) * P], rkT[:, :],
                                     start=True, stop=True).then_inc(sc_ready, 1)
                if s == 1:
                    for t in range(NT):
                        mm = nc.tensor.matmul(m.psum[:, 5, t:t + 1], h1T[:, t * P:(t + 1) * P], m.uw2T[:, :],
                                              start=True, stop=True)
                    mm.then_inc(learned_ready, 1)
                    pe.wait_ge(logvar_ready, 1)
                    nc.tensor.matmul(m.psum[:, 6, 0:1], m.ones[:, :], logvar_sum[:, :], start=True, stop=True).then_inc(total_ready, 1)
                t = s - 2
                if 0 <= t < NT:
                    pe.wait_ge(wt_ready, t + 1)
                    if t >= 2:
                        pe.wait_ge(wT_saved, t - 1)
                    for i in range(NKEY // P):
                        mm = nc.tensor.transpose(m.psum[:, 2 + t % 2, i * P:(i + 1) * P], wt[:, t % 2, i * P:(i + 1) * P],
                                                 m.ident[:, :])
                    mm.then_inc(wT_ready, 1)
                t = s - 3
                if 0 <= t < NT:
                    pe.wait_ge(wT_saved, t + 1)
                    if t == 0:
                        pe.wait_ge(gate_step, 1)
                    if t >= 2:
                        pe.wait_ge(y_added, t - 1)
                    for i in range(NKEY // P):
                        mm = nc.tensor.matmul(m.psum[:, 6 + t % 2, 0:D], wT[:, t % 2, i * P:(i + 1) * P],
                                              m.av[:, i * D:(i + 1) * D], start=(i == 0), stop=(i == NKEY // P - 1))
                    mm.then_inc(agg_ready, 1)

        @block.sync
        def _(sp):
            sp.wait_ge(zeroed, 2)
            sp.dma_start(rkT[REL_ROW:REL_ROW + 1, :], a["L0_ffn_reliability_mask"].rearrange("(o n) -> o n", o=1)).then_inc(rel_loaded, 16)

        @block.gpsimd
        def _(pool):
            nc.gpsimd.memset(rqT[:, :], 0.0).then_inc(zeroed, 1)
            nc.gpsimd.memset(rkT[:, :], 0.0).then_inc(zeroed, 1)
            pool.wait_ge(zeroed, 2)
            nc.gpsimd.memset(rqT[REL_ROW:REL_ROW + 1, :], 1.0).then_inc(one_row, 1)
            pool.wait_ge(one_row, 1)
            nc.gpsimd.tensor_tensor(m.x[:, :], m.x[:, :], m.xn[:, :], ALU.add).then_inc(x_added, 1)

        @block.vector
        def _(dve):
            for t in range(NT):
                nc.vector.bn_stats(m.stats[:, t * 6:t * 6 + 6], m.xn[:, t * D:(t + 1) * D]).then_inc(stats_ready, 1)
            dve.wait_ge(stats_ready, NT)
            for t in range(NT):
                nc.vector.bn_aggr(m.moments[:, t * 2:t * 2 + 2], m.stats[:, t * 6:t * 6 + 6]).then_inc(var_ready, 1)
            dve.wait_ge(zeroed, 2)
            for c in range(NC + 1):
                dve.wait_ge(rq_ready, c + 1)
                if c < NC:
                    nc.vector.tensor_copy(rqT[0:RD, c * BANK:(c + 1) * BANK], m.psum[0:RD, c, :]).then_inc(rq_saved, 1)
                else:
                    nc.vector.tensor_scalar(rkT[0:RD, :], m.psum[0:RD, c, :], RD ** -0.5, None, ALU.mult).then_inc(rq_saved, 1)

            def gates():
                dve.wait_ge(total_ready, 1)
                nc.vector.tensor_scalar(norm[:, :], m.psum[:, 6, 0:1], 1.0 / N, 1e-6, ALU.mult, ALU.add).then_inc(gate_step, 1)
                dve.wait_ge(gate_step, 1)
                nc.vector.reciprocal(norm[:, :], norm[:, :]).then_inc(gate_step, 1)
                dve.wait_ge(gate_step, 2)
                nc.vector.tensor_scalar(logvar[:, :], logvar[:, :], norm[:, 0:1], 0.5, ALU.mult, ALU.mult).then_inc(gate_step, 1)
                dve.wait_ge(sigmoid_ready, 1)
                dve.wait_ge(gate_step, 3)
                nc.vector.scalar_tensor_tensor(gate[:, :], learned[:, :], 2.5, logvar[:, :], ALU.mult, ALU.add).then_inc(gate_step, 1)
                dve.wait_ge(gate_step, 4)
                nc.vector.tensor_scalar(gate[:, :], gate[:, :], 0.0, 5.0, ALU.max, ALU.min).then_inc(gate_step, 1)

            for s in range(NT + 4):
                if s < NT:
                    dve.wait_ge(sc_saved, s + 1)
                    nc.vector.max(best[:, s, :], sc[:, s % 4, :]).then_inc(best_ready, 1)
                t = s - 3
                if 0 <= t < NT:
                    dve.wait_ge(wt_ready, t + 1)
                    nc.vector.reciprocal(coef[:, t:t + 1], wsum[:, t:t + 1]).then_inc(wsum_ready, 1)
                t = s - 1
                if 0 <= t < NT:
                    dve.wait_ge(replaced, t + 1)
                    dve.wait_ge(ex_ready, t + 1)
                    if t >= 2:
                        dve.wait_ge(wT_ready, t - 1)
                    nc.vector.scalar_tensor_tensor(wt[:, t % 2, :], sr[:, t % 2, :], REPLACED, ex[:, t % 2, :], ALU.is_equal,
                                                   ALU.mult, accum_out=wsum[:, t:t + 1]).then_inc(wt_ready, 1)
                if s < NT:
                    dve.wait_ge(best_ready, s + 1)
                    nc.vector.tensor_scalar(nbest[:, s:s + 1], best[:, s, 0:1], -1.0, None, ALU.mult).then_inc(nbest_ready, 1)
                    if s >= 2:
                        dve.wait_ge(wt_ready, s - 1)
                    nc.vector.match_replace(sr[:, s % 2, :], best[:, s, :], sc[:, s % 4, :], REPLACED).then_inc(replaced, 1)
                t = s - 3
                if 0 <= t < NT:
                    if t == 0:
                        dve.wait_ge(gate_ready, 1)
                    dve.wait_ge(wsum_ready, t + 1)
                    nc.vector.tensor_scalar(coef[:, t:t + 1], coef[:, t:t + 1], gate[:, t:t + 1], None, ALU.mult).then_inc(coef_ready, 1)
                t = s - 4
                if 0 <= t < NT:
                    dve.wait_ge(coef_ready, t + 1)
                    dve.wait_ge(agg_ready, t + 1)
                    dve.wait_ge(x_added, 1)
                    xt = m.x[:, t * D:(t + 1) * D]
                    nc.vector.scalar_tensor_tensor(xt, m.psum[:, 6 + t % 2, 0:D], coef[:, t:t + 1], xt,
                                                   ALU.mult, ALU.add).then_inc(y_added, 1)
                if s == 1:
                    gates()

        @block.scalar
        def _(act):
            for c in range(NC):
                act.wait_ge(qy_ready, c + 1)
                nc.scalar.activation(qyT[:, c * BANK:(c + 1) * BANK], m.psum[:, c, :], ACT.Copy).then_inc(qy_saved, 1)
            for c in range(NC):
                act.wait_ge(h1_ready, c + 1)
                nc.scalar.activation(h1T[:, c * BANK:(c + 1) * BANK], m.psum[0:UH, 4 + c, :], ACT.Gelu,
                                     bias=m.ub1[:, 0:1]).then_inc(h1_saved, 1)
            act.wait_ge(var_ready, NT)
            nc.scalar.activation(logvar[:, :], mv[:, :, 1], ACT.Ln, bias=m.ones[:, 0:1], accum_out=logvar_sum[:, :])\
                .then_inc(logvar_ready, 1)

            def save_scores(t):
                act.wait_ge(sc_ready, t + 1)
                if t >= 4:
                    act.wait_ge(replaced, t - 3)
                nc.scalar.activation(sc[:, t % 4, :], m.psum[:, t % 2, :], ACT.Copy).then_inc(sc_saved, 1)

            save_scores(0)
            save_scores(1)
            act.wait_ge(learned_ready, 1)
            nc.scalar.activation(learned[:, :], m.psum[:, 5, 0:NT], ACT.Sigmoid, bias=m.ub2[:, 0:1]).then_inc(sigmoid_ready, 1)
            for s in range(NT + 1):
                if s < NT:
                    act.wait_ge(nbest_ready, s + 1)
                    if s >= 2:
                        act.wait_ge(wt_ready, s - 1)
                    nc.scalar.activation(ex[:, s % 2, :], sc[:, s % 4, :], ACT.Exp, bias=nbest[:, s:s + 1]).then_inc(ex_ready, 1)
                if s == 1:
                    act.wait_ge(gate_step, 5)
                    nc.scalar.activation(gate[:, :], gate[:, :], ACT.Sigmoid, scale=m.gw[:, 0:1], bias=m.gb[:, 0:1])\
                        .then_inc(gate_ready, 1)
                t = s - 1
                if 0 <= t < NT:
                    act.wait_ge(wT_ready, t + 1)
                    if t >= 2:
                        act.wait_ge(agg_ready, t - 1)
                    nc.scalar.activation(wT[:, t % 2, :], m.psum[:, 2 + t % 2, :], ACT.Copy).then_inc(wT_saved, 1)
                if s + 2 < NT:
                    save_scores(s + 2)


def project1_block(nc, m, a):
    with ExitStack() as ctx:
        def sb(name, shape, dt=F32):
            return ctx.enter_context(nc.sbuf_tensor(name, shape, dt))

        def sem(name):
            return ctx.enter_context(nc.semaphore(name))

        wsw = sb("wsw", [P, 2, P])
        direct = sb("direct", [P, 2, BANK])
        partner = sb("partner", [P, 2, BANK])
        rot = sb("rot", [P, 2, BANK])
        rest = sb("rest", [P, 2, BANK])
        parts = sb("parts", [P, 2, PARTS, N], BF16)

        swapped = sem("swapped")
        qk_ready, partner_ready = sem("qk_ready"), sem("partner_ready")
        rot_ready, part1, rest_ready, part2, part3 = sem("rot_ready"), sem("part1"), sem("rest_ready"), sem("part2"), sem("part3")
        v_ready, v_saved = sem("v1_ready"), sem("v1_saved")
        stored = sem("parts_stored")
        block = ctx.enter_context(nc.Block())
        weights, biases, biases_sw = (m.wqT, m.wkT), (m.bq, m.bk), (m.bqs, m.bks)

        JOBS = 2 * NC

        @block.tensor
        def _(pe):
            pe.wait_ge(swapped, 4)
            for u in range(JOBS):
                i, c = u // NC, u % NC
                if u >= 3:
                    pe.wait_ge(partner_ready, u - 2)
                rhs = m.xnT[:, c * BANK:(c + 1) * BANK]
                nc.tensor.matmul(m.psum[:, 2 * (u % 3), :], weights[i][:, :], rhs, start=True, stop=True)
                nc.tensor.matmul(m.psum[:, 2 * (u % 3) + 1, :], wsw[:, i, :], rhs, start=True, stop=True).then_inc(qk_ready, 1)
            for c in range(NC):
                if c >= 2:
                    pe.wait_ge(v_saved, c - 1)
                for i in range(TPB):
                    t = c * TPB + i
                    mm = nc.tensor.matmul(m.psum[:, 6 + c % 2, i * P:(i + 1) * P], m.xnT[:, t * P:(t + 1) * P], m.wvT[:, :],
                                          start=True, stop=True)
                mm.then_inc(v_ready, 1)

        @block.vector
        def _(dve):
            for i in range(2):
                src = weights[i][:, :].rearrange("p (f two) -> p f two", two=2)
                dst = wsw[:, i, :].rearrange("p (f two) -> p f two", two=2)
                for k in range(2):
                    nc.vector.tensor_copy(dst[:, :, k], src[:, :, 1 - k]).then_inc(swapped, 1)
            for s in range(JOBS + 1):
                if s < JOBS:
                    u, i, c = s, s // NC, s % NC
                    dve.wait_ge(qk_ready, u + 1)
                    if u >= 2:
                        dve.wait_ge(rot_ready, u - 1)
                    cols = slice(c * BANK, (c + 1) * BANK)
                    nc.vector.scalar_tensor_tensor(direct[:, u % 2, :], m.psum[:, 2 * (u % 3), :], biases[i][:, 0:1],
                                                   m.cos[:, cols], ALU.add, ALU.mult)
                    nc.vector.scalar_tensor_tensor(partner[:, u % 2, :], m.psum[:, 2 * (u % 3) + 1, :], biases_sw[i][:, 0:1],
                                                   m.sin[:, cols], ALU.add, ALU.mult).then_inc(partner_ready, 1)
                u = s - 1
                if u >= 0:
                    i, c = u // NC, u % NC
                    dve.wait_ge(rot_ready, u + 1)
                    dve.wait_ge(part1, u + 1)
                    if u >= 2:
                        dve.wait_ge(part3, u - 1)
                    nc.vector.tensor_tensor(rest[:, u % 2, :], rot[:, u % 2, :], parts[:, i, 0, c * BANK:(c + 1) * BANK],
                                            ALU.subtract).then_inc(rest_ready, 1)
                if s < JOBS:
                    dve.wait_ge(partner_ready, s + 1)
                    if s >= 2:
                        dve.wait_ge(rest_ready, s - 1)
                    nc.vector.tensor_tensor(rot[:, s % 2, :], direct[:, s % 2, :], partner[:, s % 2, :], ALU.add).then_inc(rot_ready, 1)
            bv = m.bv[:, :].rearrange("p (o d) -> p o d", o=1).broadcast_to([P, TPB, D])
            for c in range(NC):
                dve.wait_ge(v_ready, c + 1)
                nc.vector.tensor_tensor(m.v1[:, c * TPB:(c + 1) * TPB, :],
                                        m.psum[:, 6 + c % 2, :].rearrange("p (t d) -> p t d", d=D), bv, ALU.add).then_inc(v_saved, 1)

        @block.gpsimd
        def _(pool):
            for u in range(JOBS):
                i, c = u // NC, u % NC
                pool.wait_ge(part2, u + 1)
                cols = slice(c * BANK, (c + 1) * BANK)
                nc.gpsimd.tensor_tensor(parts[:, i, 2, cols], rest[:, u % 2, :], parts[:, i, 1, cols], ALU.subtract).then_inc(part3, 1)

        @block.scalar
        def _(act):
            for s in range(JOBS + 1):
                if s < JOBS:
                    i, c = s // NC, s % NC
                    act.wait_ge(rot_ready, s + 1)
                    nc.scalar.activation(parts[:, i, 0, c * BANK:(c + 1) * BANK], rot[:, s % 2, :], ACT.Copy).then_inc(part1, 1)
                u = s - 1
                if u >= 0:
                    i, c = u // NC, u % NC
                    act.wait_ge(rest_ready, u + 1)
                    nc.scalar.activation(parts[:, i, 1, c * BANK:(c + 1) * BANK], rest[:, u % 2, :], ACT.Copy).then_inc(part2, 1)

        @block.sync
        def _(sp):
            for u in range(JOBS):
                i, c = u // NC, u % NC
                cols = slice(c * BANK, (c + 1) * BANK)
                sp.wait_ge(part3, u + 1)
                sp.dma_start((m.q_parts, m.k_parts)[i].rearrange("s r n -> r s n")[:, :, cols], parts[:, i, :, cols]).then_inc(stored, 16)
            sp.wait_ge(stored, 16 * JOBS)


def attn1_block(nc, m, a):
    SCALE = HD1 ** -0.5
    HALF = 2 * BANK
    NB = 3
    with ExitStack() as ctx:
        def sb(name, shape, dt=F32):
            return ctx.enter_context(nc.sbuf_tensor(name, shape, dt))

        def sem(name):
            return ctx.enter_context(nc.semaphore(name))

        qf = sb("qf", [KROWS, NB, N], BF16)
        kf = sb("kf", [KROWS, NB, N], BF16)
        vx = sb("vx", [P, NB, NT, VCOLS])
        pb = sb("pb", [P, 2, NC, BANK])
        rowmax = sb("rowmax", [P, NT, 2])
        nmax = sb("nmax1", [P, NT])
        nrest = sb("nrest", [P, NT])
        nparts = sb("nparts", [P, P // NT, NT], BF16)
        nT = sb("nT", [PARTS * NT, P], BF16)
        acc = sb("acc", [P, BANK])
        rsum = sb("rsum", [P, NT])

        loaded = [sem(f"qk_loaded{b}") for b in range(NB)]
        ones_loaded = sem("ones_loaded")
        nparts_zeroed = sem("nparts_zeroed")
        vx_zeroed, vx_ready = sem("vx_zeroed"), sem("vx_ready")
        rows_ready, rows_reduced = sem("rows_ready"), sem("rows_reduced")
        nmax_ready, npart1, nrest1, npart2, npart3 = sem("nmax_ready"), sem("npart1"), sem("nrest1"), sem("npart2"), sem("npart3")
        nT_ready, nT_saved, max_rows_loaded = sem("nT_ready"), sem("nT_saved"), sem("max_rows_loaded")
        st_ready, exp_ready, av_done = sem("st_ready"), sem("exp1_ready"), sem("av_done")
        acc_saved, accT_ready, rsum_ready, att_ready = sem("acc_saved"), sem("accT_ready"), sem("rsum_ready"), sem("att_ready")
        block = ctx.enter_context(nc.Block())

        START = 2

        def start_counts(eng, *sems):
            for s in sems:
                eng.sem_inc(s, START)

        M_B, E_B, A_B, T_B = 0, 4, 6, 7
        UNITS = NT * NC
        HALVES = 2 * NT
        ROUNDS = H1 // NB - 1
        LEAD = 12
        LOAD = 16 * 2 * PARTS

        def exp_bank(k, last):
            return (M_B + k % 4, 4) if last else (E_B + k % 2, 2)

        @block.sync
        def _(sp):
            def load(h, b):
                for j in range(PARTS):
                    rows = slice(j * PARTS * HD1, (j + 1) * PARTS * HD1)
                    k = m.k_parts[j, bass.ds(h * HD1, HD1), :].rearrange("(o d) n -> o d n", o=1)
                    sp.dma_start(qf[rows, b, :], m.q_parts[:, bass.ds(h * HD1, HD1), :]).then_inc(loaded[b], 16)
                    sp.dma_start(kf[rows, b, :], k.broadcast_to([PARTS, HD1, N])).then_inc(loaded[b], 16)

            def max_rows(g, b):
                sp.wait_ge(nT_saved, START + g + 1)
                sp.dma_start(qf[QROWS:KROWS, b, :], nT[:, :]).then_inc(max_rows_loaded, 16)

            for b in range(NB):
                load(b, b)
                if b == 0:
                    sp.dma_start(kf[QROWS:KROWS, :, :], m.ones_rows.rearrange("r (o n) -> r o n", o=1)
                                 .broadcast_to([PARTS, NB, N])).then_inc(ones_loaded, 16)
            max_rows(0, 0)
            with sp.Fori(0, ROUNDS) as r:
                for b in range(NB):
                    max_rows(r * NB + b + 1, (b + 1) % NB)
                    sp.wait_ge(av_done, START + (r * NB + b + 1) * NT)
                    load(r * NB + b + NB, b)
            for h in range(H1 - 1 - NB, H1 - 1):
                max_rows(h + 1, (h + 1) % NB)
                if h == H1 - 1 - NB:
                    sp.wait_ge(av_done, START + (h + 1) * NT)
                    load(h + NB, h % NB)

        @block.tensor
        def _(pe):
            start_counts(pe, rows_ready, nT_ready, st_ready, av_done, accT_ready)

            def rows(g, b, n):
                t, c, u = n // NC, n % NC, n // 2
                if n % 2 == 0:
                    pe.wait_ge(rows_reduced, START + g * HALVES + u - 1)
                mm = nc.tensor.matmul(m.psum[:, M_B + (u % 2) * 2 + n % 2, :], qf[0:QROWS, b, t * P:(t + 1) * P],
                                      kf[0:QROWS, b, c * BANK:(c + 1) * BANK], start=True, stop=True)
                if n % 2:
                    mm.then_inc(rows_ready, 1)

            def turn_max(g):
                pe.wait_ge(npart3, START + g + 1)
                pe.wait_ge(att_ready, START + g - 1)
                nc.tensor.transpose(m.psum[:, T_B, 0:P // 2].bitcast(BF16),
                                    nparts[:, :, :].rearrange("p a t -> p (a t)"), m.identb[:, :]).then_inc(nT_ready, 1)

            def turn_sums(h, last):
                pe.wait_ge(acc_saved, START + h + 1)
                pe.wait_ge(nT_saved, START + h + (1 if last else 2))
                for i in range(NC):
                    mm = nc.tensor.transpose(m.psum[:, T_B, i * P:(i + 1) * P], acc[:, i * P:(i + 1) * P], m.ident[:, :])
                mm.then_inc(accT_ready, 1)

            def weigh(h, b, t):
                pe.wait_ge(exp_ready, START + h * UNITS + (t + 1) * NC)
                if t == 0:
                    pe.wait_ge(acc_saved, START + h)
                    pe.wait_ge(vx_ready, START + h + 1)
                for c in range(NC):
                    mm = nc.tensor.matmul(m.psum[c * VCOLS:(c + 1) * VCOLS, A_B, :], vx[:, b, t, :], pb[:, t % 2, c, :],
                                          start=(t == 0), stop=(t == NT - 1))
                mm.then_inc(av_done, 1)

            def head(r, b):
                h = r * NB + b
                left = H1 - 1 - h if isinstance(h, int) else NB
                pe.wait_ge(max_rows_loaded, h * 16 + 16)
                n = LEAD
                for t in range(NT + 1):
                    if n == UNITS and left >= 2:
                        b2 = b + 2
                        pe.wait_ge(loaded[b2 % NB], r * LOAD + (1 + b2 // NB) * LOAD)
                    for c, beside in enumerate((1, 2, 1, 0)):
                        if t == NT:
                            break
                        k = t * NC + c
                        bank, banks = exp_bank(k, left == 0)
                        pe.wait_ge(exp_ready, START + h * UNITS + k + 1 - banks)
                        nc.tensor.matmul(m.psum[:, bank, :], kf[:, b, t * P:(t + 1) * P],
                                         qf[:, b, c * BANK:(c + 1) * BANK], start=True, stop=True).then_inc(st_ready, 1)
                        for _ in range(beside):
                            if n < UNITS and left >= 1:
                                rows(h + 1, (b + 1) % NB, n)
                            elif n >= UNITS and left >= 2:
                                rows(h + 2, (b + 2) % NB, n - UNITS)
                            n += 1
                    if t >= 1:
                        weigh(h, b, t - 1)
                    if t == NT - 3 and left >= 1:
                        turn_max(h + 1)
                turn_sums(h, left == 0)

            pe.wait_ge(ones_loaded, 16)
            pe.wait_ge(loaded[0], LOAD)
            for n in range(UNITS):
                rows(0, 0, n)
            pe.wait_ge(loaded[1], LOAD)
            for n in range(LEAD):
                if n == 4:
                    turn_max(0)
                rows(1, 1, n)
            with pe.Fori(0, ROUNDS) as r:
                for b in range(NB):
                    head(r, b)
            for h in range(ROUNDS * NB, H1):
                head(h // NB, h % NB)

        @block.vector
        def _(dve):
            start_counts(dve, rows_reduced, nmax_ready, npart1, nrest1, npart2, npart3, nT_saved, acc_saved, rsum_ready, att_ready)

            def reduce_rows(g, first, end):
                for u in range(first, end):
                    dve.wait_ge(rows_ready, START + g * HALVES + u + 1)
                    nc.vector.tensor_reduce(rowmax[:, u // 2, u % 2:u % 2 + 1],
                                            m.psum[:, M_B + (u % 2) * 2:M_B + (u % 2) * 2 + 2, :].rearrange("p b c -> p (b c)"),
                                            AX_X, ALU.max).then_inc(rows_reduced, 1)

            def split_maxima(g):
                dve.wait_ge(rows_reduced, START + (g + 1) * HALVES)
                nc.vector.tensor_reduce(nmax[:, :], rowmax[:, :, :], AX_X, ALU.max, negate=True).then_inc(nmax_ready, 1)
                dve.wait_ge(nmax_ready, START + g + 1)
                nc.vector.tensor_copy(nparts[:, 0, :], nmax[:, :]).then_inc(npart1, 1)
                dve.wait_ge(npart1, START + g + 1)
                nc.vector.tensor_tensor(nrest[:, :], nmax[:, :], nparts[:, 0, :], ALU.subtract).then_inc(nrest1, 1)
                dve.wait_ge(nrest1, START + g + 1)
                nc.vector.tensor_copy(nparts[:, 1, :], nrest[:, :]).then_inc(npart2, 1)
                dve.wait_ge(npart2, START + g + 1)
                nc.vector.tensor_tensor(nparts[:, 2, :], nrest[:, :], nparts[:, 1, :], ALU.subtract).then_inc(npart3, 1)

            def save_turned(g):
                if not (isinstance(g, int) and g == 0):
                    dve.wait_ge(max_rows_loaded, g * 16)
                dve.wait_ge(nT_ready, START + g + 1)
                nc.vector.tensor_copy(nT[:, :], m.psum[0:PARTS * NT, T_B, 0:P // 2].bitcast(BF16)).then_inc(nT_saved, 1)

            def sums(h):
                dve.wait_ge(av_done, START + (h + 1) * NT)
                dve.wait_ge(accT_ready, START + h)
                nc.vector.tensor_copy(acc[:, :], m.psum[:, A_B, :]).then_inc(acc_saved, 1)
                dve.wait_ge(accT_ready, START + h + 1)
                turned = m.psum[:, T_B, :].rearrange("p (i j c) -> p i j c", i=TPB, j=NC)
                nc.vector.reciprocal(rsum[:, :].rearrange("p (i j) -> p i j", i=TPB), turned[:, :, :, HD1]).then_inc(rsum_ready, 1)
                dve.wait_ge(rsum_ready, START + h + 1)
                rb = rsum[:, :].rearrange("p (i j o) -> p i j o", i=TPB, o=1).broadcast_to([P, TPB, NC, HD1])
                dst = m.att[:, :, bass.ds(h * HD1, HD1)].rearrange("p (j i) d -> p i j d", i=TPB)
                nc.vector.tensor_tensor(dst, turned[:, :, :, 0:HD1], rb, ALU.mult).then_inc(att_ready, 1)

            nc.vector.memset(nparts[:, :, :], 0.0).then_inc(nparts_zeroed, 1)
            dve.wait_ge(nparts_zeroed, 1)

            def maxima(g, more):
                split_maxima(g)
                if more:
                    reduce_rows(g + 1, 0, 1)
                save_turned(g)
                if more:
                    reduce_rows(g + 1, 1, LEAD // 2)

            reduce_rows(0, 0, HALVES)
            maxima(0, True)
            with dve.Fori(0, ROUNDS) as r:
                for b in range(NB):
                    h = r * NB + b
                    reduce_rows(h + 1, LEAD // 2, HALVES)
                    maxima(h + 1, True)
                    sums(h)
            for h in range(ROUNDS * NB, H1):
                if h + 1 < H1:
                    reduce_rows(h + 1, LEAD // 2, HALVES)
                    maxima(h + 1, h + 2 < H1)
                sums(h)

        @block.scalar
        def _(act):
            start_counts(act, exp_ready)

            def head(h, last=False):
                for k in range(UNITS):
                    t, c = k // NC, k % NC
                    if c == 0:
                        act.wait_ge(av_done, START + h * NT + t - 1)
                    act.wait_ge(st_ready, START + h * UNITS + k + 1)
                    nc.scalar.activation(pb[:, t % 2, c, :], m.psum[:, exp_bank(k, last)[0], :], ACT.Exp, scale=SCALE).then_inc(exp_ready, 1)

            with act.Fori(0, ROUNDS) as r:
                for b in range(NB):
                    head(r * NB + b)
            for h in range(ROUNDS * NB, H1):
                head(h, h == H1 - 1)

        @block.gpsimd
        def _(pool):
            start_counts(pool, vx_ready)
            nc.gpsimd.memset(vx[:, :, :, :], 0.0).then_inc(vx_zeroed, 1)
            pool.wait_ge(vx_zeroed, 1)
            nc.gpsimd.memset(vx[:, :, :, HD1:HD1 + 1], 1.0).then_inc(vx_zeroed, 1)
            pool.wait_ge(vx_zeroed, 2)

            def values(h, b):
                nc.gpsimd.tensor_copy(vx[:, b, :, 0:HD1], m.v1[:, :, bass.ds(h * HD1, HD1)]).then_inc(vx_ready, 1)

            for b in range(NB):
                values(b, b)
            with pool.Fori(0, ROUNDS) as r:
                for b in range(NB):
                    pool.wait_ge(av_done, START + (r * NB + b + 1) * NT)
                    values(r * NB + b + NB, b)
            pool.wait_ge(av_done, START + (H1 - NB) * NT)
            values(H1 - 1, 0)


def output1_block(nc, m, a):
    with ExitStack() as ctx:
        def sem(name):
            return ctx.enter_context(nc.semaphore(name))

        attT = ctx.enter_context(nc.sbuf_tensor("attT", [P, N], F32))
        attT_ready, attT_saved, biased = sem("attT_ready"), sem("attT_saved"), sem("biased")
        o_ready, x_added = sem("o1_ready"), sem("o1_added")
        block = ctx.enter_context(nc.Block())

        @block.gpsimd
        def _(pool):
            bo = m.bo[:, :].rearrange("p (o d) -> p o d", o=1).broadcast_to([P, NT, D])
            x = m.x[:, :].rearrange("p (t d) -> p t d", d=D)
            nc.gpsimd.tensor_tensor(x, x, bo, ALU.add).then_inc(biased, 1)

        @block.tensor
        def _(pe):
            for c in range(NC):
                for i in range(TPB):
                    mm = nc.tensor.transpose(m.psum[:, c, i * P:(i + 1) * P], m.att[:, c * TPB + i, :], m.ident[:, :])
                mm.then_inc(attT_ready, 1)
            for c in range(NC):
                pe.wait_ge(attT_saved, c + 1)
                for i in range(TPB):
                    t = c * TPB + i
                    mm = nc.tensor.matmul(m.psum[:, 4 + c, i * P:(i + 1) * P], attT[:, t * P:(t + 1) * P], m.woT[:, :],
                                          start=True, stop=True)
                mm.then_inc(o_ready, 1)

        @block.scalar
        def _(act):
            for c in range(NC):
                act.wait_ge(attT_ready, c + 1)
                nc.scalar.activation(attT[:, c * BANK:(c + 1) * BANK], m.psum[:, c, :], ACT.Copy).then_inc(attT_saved, 1)

        @block.vector
        def _(dve):
            dve.wait_ge(biased, 1)
            for c in range(NC):
                dve.wait_ge(o_ready, c + 1)
                xc = m.x[:, c * BANK:(c + 1) * BANK]
                nc.vector.tensor_tensor(xc, xc, m.psum[:, 4 + c, :], ALU.add).then_inc(x_added, 1)


def network(m, i, w1, w2, b1, b2):
    return [(m.w1[:, i, :], w1), (m.w2[:, i, :, :], w2.rearrange("(k p) d -> p k d", p=P)),
            (m.b1[:, i, :], b1.rearrange("(k p) -> p k", p=P)), (m.b2[:, i, :], b2.broadcast_to([P, D]))]


def experts_block(nc, m, a):
    K = NETS * HT
    with ExitStack() as ctx:
        def sb(name, shape, dt=F32):
            return ctx.enter_context(nc.sbuf_tensor(name, shape, dt))

        def sem(name):
            return ctx.enter_context(nc.semaphore(name))

        w1, w2, b1, b2 = m.w1, m.w2, m.b1, m.b2
        w2s = sb("w2s", [P, NETS, HT, D])
        b2s = sb("b2s", [P, D])
        hT = sb("hT", [P, K, BANK])
        mean = sb("mean", [P, 1])
        lg = sb("lg", [1, NE])
        pw = sb("pw", [1, NE])
        psum_1 = sb("psum_1", [1, 1])
        nlg = sb("nlg", [1, 1])
        top = sb("top", [1, 8])
        chosen = sb("chosen", [1, 8], U32)
        cf = sb("cf", [1, NETS])
        cfb = sb("cfb", [P, NETS])
        al = sb("al", [1, 2])

        expert_loaded = (sem("expert0_loaded"), sem("expert1_loaded"))
        step, logits_ready, exp_done, cf_ready, coef_ready, cfb_saved = (sem("step"), sem("logits_ready"), sem("exp2_ready"),
                                                                         sem("cf_ready"), sem("coefs_ready"), sem("cfb_saved"))
        chosen_ready, w2s_ready, b2_added = sem("chosen_ready"), sem("w2s_ready"), sem("b2_added")
        b2_step = sem("b2_step")
        h_ready, h_saved, y_ready, y_added = sem("h_ready"), sem("h_saved"), sem("y_ready"), sem("y2_added")
        y_main_ready, y_main_added = sem("y_main_ready"), sem("y_main_added")
        block = ctx.enter_context(nc.Block())
        START = 2

        @block.sync
        def _(sp):
            sp.wait_ge(chosen_ready, 1)
            for i in range(2):
                e = sp.value_load(chosen[0:1, i:i + 1], min_val=0, max_val=NE - 1)
                one = bass.ds(e, 1)
                for dst, src in network(m, 1 + i, a["L1_ffn_W1e"][one].rearrange("o d h -> (o d) h"),
                                        a["L1_ffn_W2e"][one].rearrange("o h d -> (o h) d"),
                                        a["L1_ffn_b1e"][one].rearrange("o h -> (o h)"), a["L1_ffn_b2e"][one, :]):
                    sp.dma_start(dst, src, allow_slow_non_contiguous=True).then_inc(expert_loaded[i], 16)

        @block.vector
        def _(dve):
            n = [0]

            def chain(ins):
                n[0] += 1
                ins.then_inc(step, 1)
                dve.wait_ge(step, n[0])

            dve.sem_inc(y_added, START)
            chain(nc.vector.tensor_reduce(mean[:, :], m.xnT[:, :], AX_X, ALU.add))
            nc.vector.tensor_scalar(mean[:, :], mean[:, :], 1.0 / N, None, ALU.mult).then_inc(cf_ready, 1)
            dve.wait_ge(logits_ready, 1)
            chain(nc.vector.tensor_tensor(lg[:, :], m.psum[0:1, 6, 0:NE], m.bg[:, :], ALU.add))
            chain(nc.vector.tensor_reduce(nlg[:, :], lg[:, :], AX_X, ALU.max, negate=True))
            nc.vector.tensor_scalar(al[:, 0:1], m.alpha[:, :], 0.1, 1.0, ALU.max, ALU.min).then_inc(cf_ready, 1)
            dve.wait_ge(exp_done, 1)
            chain(nc.vector.reciprocal(psum_1[:, :], psum_1[:, :]))
            chain(nc.vector.tensor_scalar(pw[:, :], pw[:, :], psum_1[:, 0:1], None, ALU.mult))
            chain(nc.vector.max(top[:, :], pw[:, :]))
            nc.vector.max_index(chosen[:, :], top[:, :], pw[:, :]).then_inc(chosen_ready, 1)
            chain(nc.vector.tensor_tensor(nlg[:, :], top[:, 0:1], top[:, 1:2], ALU.add))
            chain(nc.vector.reciprocal(nlg[:, :], nlg[:, :]))
            chain(nc.vector.tensor_scalar(al[:, 1:2], al[:, 0:1], -1.0, 1.0, ALU.mult, ALU.add))
            chain(nc.vector.tensor_copy(cf[:, 0:1], al[:, 0:1]))
            nc.vector.tensor_scalar(cf[:, 1:3], top[:, 0:2], nlg[:, 0:1], al[:, 1:2], ALU.mult, ALU.mult).then_inc(cf_ready, 1)
            dve.wait_ge(coef_ready, 1)
            nc.vector.tensor_copy(cfb[:, :], m.psum[:, 7, 0:NETS]).then_inc(cfb_saved, 1)
            dve.wait_ge(cfb_saved, 1)
            for i in range(NETS):
                if i >= 1:
                    dve.wait_ge(expert_loaded[i - 1], 64)
                nc.vector.tensor_scalar(w2s[:, i, :, :], w2[:, i, :, :], cfb[:, i:i + 1], None, ALU.mult).then_inc(w2s_ready, 1)
            nc.vector.tensor_scalar(b2s[:, :], b2[:, 0, :], cfb[:, 0:1], None, ALU.mult).then_inc(b2_step, 1)
            for i in range(1, NETS):
                dve.wait_ge(b2_step, i)
                nc.vector.scalar_tensor_tensor(b2s[:, :], b2[:, i, :], cfb[:, i:i + 1], b2s[:, :], ALU.mult, ALU.add).then_inc(b2_step, 1)
            dve.wait_ge(b2_added, 1)
            dve.wait_ge(y_main_ready, 1)
            nc.vector.tensor_tensor(m.x[:, 0:BANK], m.x[:, 0:BANK], m.psum[:, 5, :], ALU.add).then_inc(y_main_added, 1)
            dve.wait_ge(y_main_added, 1)
            with dve.Fori(0, NC) as c:
                dve.wait_ge(y_ready, START + c + 1)
                xc = m.x[:, bass.ds(c * BANK, BANK)]
                nc.vector.tensor_tensor(xc, xc, m.psum[:, 4, :], ALU.add).then_inc(y_added, 1)

        @block.gpsimd
        def _(pool):
            pool.wait_ge(b2_step, NETS)
            x = m.x[:, :].rearrange("p (t d) -> p t d", d=D)
            nc.gpsimd.tensor_tensor(x, x, b2s[:, :].rearrange("p (o d) -> p o d", o=1).broadcast_to([P, NT, D]),
                                    ALU.add).then_inc(b2_added, 1)

        @block.scalar
        def _(act):
            act.sem_inc(h_saved, START)
            act.wait_ge(step, 3)
            nc.scalar.activation(pw[:, :], lg[:, :], ACT.Exp, bias=nlg[:, 0:1], accum_out=psum_1[:, :]).then_inc(exp_done, 1)
            b1f = b1[:, :, :].rearrange("p i k -> p (i k)")

            def chunk(c, first):
                for k in range(K):
                    if first and k >= HT and k % HT == 0:
                        act.wait_ge(expert_loaded[k // HT - 1], 64)
                    act.wait_ge(h_ready, START + c * K + k + 1)
                    nc.scalar.activation(hT[:, k, :], m.psum[:, k % 4, :], ACT.Gelu_apprx_tanh, bias=b1f[:, k:k + 1]).then_inc(h_saved, 1)

            chunk(0, True)
            with act.Fori(0, NC - 1) as c:
                chunk(c + 1, False)

        @block.tensor
        def _(pe):
            pe.sem_inc(h_ready, START)
            pe.sem_inc(y_ready, START)

            def hidden(c, i):
                for k in range(i * HT, (i + 1) * HT):
                    pe.wait_ge(h_saved, START + c * K + max(k - 3, 0))
                    nc.tensor.matmul(m.psum[:, k % 4, :], w1[:, i, k % HT * P:(k % HT + 1) * P], m.xnT[:, bass.ds(c * BANK, BANK)],
                                     start=True, stop=True).then_inc(h_ready, 1)

            def outputs(c, first, end, bank, ready):
                for j in range(TPB):
                    for k in range(first, end):
                        if j == 0:
                            pe.wait_ge(h_saved, START + c * K + k + 1)
                        mm = nc.tensor.matmul(m.psum[:, bank, j * P:(j + 1) * P], hT[:, k, j * P:(j + 1) * P],
                                              w2s[:, k // HT, k % HT, :], start=(k == first), stop=(k == end - 1))
                mm.then_inc(ready, 1)

            pe.wait_ge(cf_ready, 1)
            nc.tensor.matmul(m.psum[0:1, 6, 0:NE], mean[:, :], m.wg[:, :], start=True, stop=True).then_inc(logits_ready, 1)
            hidden(0, 0)
            pe.wait_ge(cf_ready, 3)
            nc.tensor.matmul(m.psum[:, 7, 0:NETS], m.ones[0:1, :], cf[:, :], start=True, stop=True).then_inc(coef_ready, 1)
            pe.wait_ge(w2s_ready, 1)
            outputs(0, 0, HT, 5, y_main_ready)
            for i in range(1, NETS):
                pe.wait_ge(expert_loaded[i - 1], 64)
                hidden(0, i)
            pe.wait_ge(w2s_ready, NETS)
            outputs(0, HT, K, 4, y_ready)
            with pe.Fori(0, NC - 1) as r:
                for i in range(NETS):
                    hidden(r + 1, i)
                pe.wait_ge(y_added, START + r + 1)
                outputs(r + 1, 0, K, 4, y_ready)


def store_block(nc, m, out):
    with ExitStack() as ctx:
        stored = ctx.enter_context(nc.semaphore("stored"))
        block = ctx.enter_context(nc.Block())

        @block.sync
        def _(sp):
            sp.dma_start(out[0].rearrange("(t p) d -> p t d", p=P),
                         m.x[:, :].rearrange("p (t d) -> p t d", d=D)).then_inc(stored, 16)
            sp.wait_ge(stored, 16)


def build(nc, a, out):
    with ExitStack() as ctx:
        def sb(name, shape, dt=F32):
            return ctx.enter_context(nc.sbuf_tensor(name, shape, dt))

        m = Memory()
        m.x = sb("x", [P, NT * D])
        m.xn = sb("xn", [P, NT * D])
        m.xnT = sb("xnT", [P, N])
        m.stats = sb("stats", [P, NT * 6])
        m.moments = sb("moments", [P, NT * 2])
        m.std = sb("std", [P, NT])
        m.rstd = sb("rstd", [P, NT])
        m.ident = sb("ident", [P, P])
        m.identb = sb("identb", [P, P], BF16)
        m.ones = sb("ones", [P, P])
        m.mask = sb("mask", [P, 2 * WL])
        m.ws1 = sb("ws1", [P, UH])
        m.bs1 = sb("bs1", [UH, 1])
        m.ws2 = sb("ws2", [UH, 1])
        m.bs2 = sb("bs2", [P, 1])
        m.psum = ctx.enter_context(nc.psum_tensor("psum", [P, 8, BANK], F32))
        setup_block(nc, m, a)
        ln_block(nc, m, "ln0")

        def row(ap):
            return ap.rearrange("(o d) -> o d", o=1)

        def column(ap):
            return ap.rearrange("(p o) -> p o", o=1)

        m.qpT, m.rwT, m.akT = sb("qpT", [P, P]), sb("rwT", [P, RD]), sb("akT", [P, NKEY])
        m.av = sb("av", [P, NKEY // P * D])
        m.uw1T, m.ub1, m.uw2T, m.ub2 = sb("uw1T", [P, UH]), sb("ub1", [UH, 1]), sb("uw2T", [UH, 1]), sb("ub2", [P, 1])
        m.gw, m.gb = sb("gw", [P, 1]), sb("gb", [P, 1])
        m.woT, m.bo = sb("woT", [P, P]), sb("bo", [P, D])
        m.wqT, m.wkT, m.wvT = sb("wqT", [P, P]), sb("wkT", [P, P]), sb("wvT", [P, P])
        m.bq, m.bk, m.bqs, m.bks, m.bv = sb("bq", [P, 1]), sb("bk", [P, 1]), sb("bqs", [P, 1]), sb("bks", [P, 1]), sb("bv", [P, D])
        m.cos, m.sin = sb("cos", [P, N]), sb("sin", [P, N])
        freq = (1.0 / np.float32(10000.0) ** (np.arange(0, HD1, 2, dtype=np.float32) / HD1)).astype(np.float32)
        angle = np.arange(N, dtype=np.float32)[None, :] * np.repeat(freq, 2)[:, None]
        sign = np.where(np.arange(HD1) % 2, 1.0, -1.0).astype(np.float32)[:, None]
        cos_t = nc.inline_tensor(np.tile(np.cos(angle), (H1, 1)).astype(np.float32), "cos_table").ap()
        sin_t = nc.inline_tensor(np.tile(np.sin(angle) * sign, (H1, 1)).astype(np.float32), "sin_table").ap()
        loads = [(m.qpT[:, :], a["L0_ffn_q_proj_w"]), (m.rwT[:, :], a["L0_ffn_router_w"]), (m.akT[:, :], a["L0_ffn_aux_keys"]),
                 (m.av[:, :].rearrange("p (k d) -> p k d", d=D), a["L0_ffn_aux_values"].rearrange("(k p) d -> p k d", p=P)),
                 (m.uw1T[:, :], a["L0_ffn_unc_w1"]), (m.ub1[:, :], column(a["L0_ffn_unc_b1"])), (m.uw2T[:, :], a["L0_ffn_unc_w2"]),
                 (m.ub2[:, :], row(a["L0_ffn_unc_b2"]).broadcast_to([P, 1])), (m.gw[:, :], row(a["L0_ffn_gate_w1"]).broadcast_to([P, 1])),
                 (m.gb[:, :], row(a["L0_ffn_gate_bias"]).broadcast_to([P, 1])),
                 (m.wqT[:, :], a["L1_attn_Wq"]), (m.wkT[:, :], a["L1_attn_Wk"]), (m.wvT[:, :], a["L1_attn_Wv"]),
                 (m.woT[:, :], a["L1_attn_Wo"]), (m.bq[:, :], column(a["L1_attn_bq"])), (m.bk[:, :], column(a["L1_attn_bk"])),
                 (m.bv[:, :], row(a["L1_attn_bv"]).broadcast_to([P, D])), (m.bo[:, :], row(a["L1_attn_bo"]).broadcast_to([P, D]))]
        for dst, src in ((m.bqs, a["L1_attn_bq"]), (m.bks, a["L1_attn_bk"])):
            for k in range(2):
                loads.append((dst[k:P:2, :], src.rearrange("(f two) -> two f", two=2)[1 - k].rearrange("(p o) -> p o", o=1)))
        loads += [(m.cos[:, :], cos_t), (m.sin[:, :], sin_t)]
        attn0_block(nc, m, a, loads)
        ln_block(nc, m, "ln1")
        memory_block(nc, m, a)
        with ExitStack() as layer:
            def lb(name, shape, dt=F32):
                return layer.enter_context(nc.sbuf_tensor(name, shape, dt))

            m.v1, m.att = lb("v1", [P, NT, D]), lb("att", [P, NT, D])
            m.q_parts = nc.dram_tensor("q_parts", [PARTS, P, N], BF16, kind="Internal").ap()
            m.k_parts = nc.dram_tensor("k_parts", [PARTS, P, N], BF16, kind="Internal").ap()
            m.ones_rows = nc.inline_tensor(np.ones((PARTS, N), mybir.dt.np(BF16)), "ones_rows").ap()
            ln_block(nc, m, "ln2")
            project1_block(nc, m, a)
            attn1_block(nc, m, a)
            output1_block(nc, m, a)
        with ExitStack() as layer:
            def lb(name, shape, dt=F32):
                return layer.enter_context(nc.sbuf_tensor(name, shape, dt))

            m.wg, m.bg, m.alpha = lb("wg", [P, NE]), lb("bg", [1, NE]), lb("alpha", [1, 1])
            m.w1 = lb("w1", [P, NETS, HID])
            m.w2 = lb("w2", [P, NETS, HT, D])
            m.b1, m.b2 = lb("b1", [P, NETS, HT]), lb("b2", [P, NETS, D])
            main = network(m, 0, a["L1_ffn_W1m"], a["L1_ffn_W2m"], a["L1_ffn_b1m"], row(a["L1_ffn_b2m"]))
            ln_block(nc, m, "ln3", main + [(m.wg[:, :], a["L1_ffn_w_gate"]), (m.bg[:, :], row(a["L1_ffn_b_gate"])),
                                    (m.alpha[:, :], row(a["L1_ffn_alpha"]))])
            experts_block(nc, m, a)
        store_block(nc, m, out)


_INS = ['L0_attn_x', 'L0_attn_wq', 'L0_attn_wk', 'L0_attn_wv', 'L0_attn_wo', 'L0_attn_ws1', 'L0_attn_bs1', 'L0_attn_ws2', 'L0_attn_bs2',
        'L0_ffn_q_proj_w', 'L0_ffn_router_w', 'L0_ffn_aux_keys', 'L0_ffn_aux_values', 'L0_ffn_reliability_mask', 'L0_ffn_unc_w1',
        'L0_ffn_unc_b1', 'L0_ffn_unc_w2', 'L0_ffn_unc_b2', 'L0_ffn_gate_w1', 'L0_ffn_gate_bias', 'L1_attn_Wq', 'L1_attn_bq', 'L1_attn_Wk',
        'L1_attn_bk', 'L1_attn_Wv', 'L1_attn_bv', 'L1_attn_Wo', 'L1_attn_bo', 'L1_ffn_alpha', 'L1_ffn_w_gate', 'L1_ffn_b_gate', 'L1_ffn_W1m',
        'L1_ffn_b1m', 'L1_ffn_W2m', 'L1_ffn_b2m', 'L1_ffn_W1e', 'L1_ffn_b1e', 'L1_ffn_W2e', 'L1_ffn_b2e']
_TURNED = ['L0_ffn_q_proj_w', 'L0_ffn_router_w', 'L0_ffn_aux_keys', 'L0_ffn_unc_w1', 'L0_ffn_unc_w2',
           'L1_attn_Wq', 'L1_attn_Wk', 'L1_attn_Wv', 'L1_attn_Wo']


def kernel(**inputs):
    import numpy as _np
    import concourse.bacc as _bacc
    from concourse import mybir as _mybir
    from concourse.bass_utils import run_bass_kernel_spmd as _run

    nc = _bacc.Bacc("TRN2", target_bir_lowering=False, num_devices=1)
    arrays, args = {}, {}
    for name in _INS:
        x = inputs[name]
        if name in _TURNED:
            x = _np.asarray(x).T
        x = _np.ascontiguousarray(x)
        if x.ndim == 0:
            x = x.reshape(1)
        arrays[f"in_{name}"] = x
        args[name] = nc.dram_tensor(f"in_{name}", x.shape, _mybir.dt.from_np(x.dtype), kind="ExternalInput").ap()
    out = nc.dram_tensor("out_0", (1, N, D), F32, kind="ExternalOutput").ap()
    build(nc, args, out)
    r = _run(nc, [arrays], core_ids=[0])
    return r.results[0]["out_0"]
```
